# Optimizing a Trainium2 kernel written in Bass

```python
import numpy as np
import jax
import jax.numpy as jnp

def _softmax(x, axis=-1):
    return jax.nn.softmax(x, axis=axis)

def _gelu(x):
    return jax.nn.gelu(x, approximate=True)

def _silu(x):
    return jax.nn.silu(x)

def _sigmoid(x):
    return jax.nn.sigmoid(x)

def _layernorm(x, axis=-1, eps=1e-05):
    m = jnp.mean(x, axis=axis, keepdims=True)
    v = jnp.var(x, axis=axis, keepdims=True)
    return (x - m) / jnp.sqrt(v + eps)

def _scatter_add(tgt, idx, src, axis=0):
    return tgt.at[idx].add(src)

def _segment_sum(src, seg, n):
    return jax.ops.segment_sum(src, seg, n)
kernel_name = 'mk_sandwich_d2_jaxref_r8_62d920'

def setup_inputs(seed: int=0):
    np.random.seed(seed)
    _w = jnp.asarray

    def _L0_attn_setup():
        import math
        import jax, jax.numpy as jnp
        import numpy as np
        IN_F, OUT_F, HID = (512, 512, 512)
        WINDOW, STRIPES = (6, 3)

        def make_sparse_mask(n_in=IN_F, n_out=OUT_F, window=WINDOW, stripes=STRIPES):
            m = np.zeros((n_in, n_out), dtype=np.float32)
            stride = int(math.sqrt(n_in))
            for k in range(stripes):
                ps = stride * k
                for i in range(0, n_in, window):
                    m[ps + i:ps + i + window, i:i + window] = 1.0
            mb = m.astype(bool)
            return jnp.asarray((mb | mb.T).astype(np.float32))
        key = jax.random.key(seed)
        k1, k2, k3, k4 = jax.random.split(key, 4)
        scale = 1.0 / math.sqrt(IN_F)
        x = jax.random.normal(k1, (8, 96, IN_F), dtype=jnp.float32)
        w1 = jax.random.normal(k2, (HID, IN_F), dtype=jnp.float32) * scale
        w2 = jax.random.normal(k3, (OUT_F, HID), dtype=jnp.float32) * scale
        b2 = jax.random.normal(k4, (OUT_F,), dtype=jnp.float32) * scale
        return {'x': x, 'w1': w1, 'w2': w2, 'b2': b2, 'sparse_mask': make_sparse_mask()}
    _L0_attn_in = _L0_attn_setup()

    def _L0_ffn_setup():
        import jax, jax.numpy as jnp
        import numpy as np
        H = 512
        I = 1376
        R = 32
        NLEV = 16
        Q_ZERO = 7.5
        Q_STEP = 0.005
        LR_SCALE = 0.02

        def _qlinear(x, q, scale, A, Bm):
            w = (q.astype(jnp.float32) - Q_ZERO) * (scale * Q_STEP)[:, None]
            y = jnp.einsum('bsh,oh->bso', x, w)
            return y + LR_SCALE * (x @ A @ Bm)
        key = jax.random.key(seed)
        ks = jax.random.split(key, 13)
        B, S = (2, 256)
        inp = {'x': jax.random.normal(ks[0], (B, S, H), jnp.float32), 'gate_q': jax.random.randint(ks[1], (I, H), 0, NLEV, jnp.int32), 'gate_scale': jax.random.uniform(ks[2], (I,), jnp.float32), 'gate_A': jax.random.normal(ks[3], (H, R), jnp.float32), 'gate_B': jax.random.normal(ks[4], (R, I), jnp.float32), 'up_q': jax.random.randint(ks[5], (I, H), 0, NLEV, jnp.int32), 'up_scale': jax.random.uniform(ks[6], (I,), jnp.float32), 'up_A': jax.random.normal(ks[7], (H, R), jnp.float32), 'up_B': jax.random.normal(ks[8], (R, I), jnp.float32), 'down_q': jax.random.randint(ks[9], (H, I), 0, NLEV, jnp.int32), 'down_scale': jax.random.uniform(ks[10], (H,), jnp.float32), 'down_A': jax.random.normal(ks[11], (I, R), jnp.float32), 'down_B': jax.random.normal(ks[12], (R, H), jnp.float32)}
        return inp
    _L0_ffn_in = _L0_ffn_setup()

    def _L1_attn_setup():
        import jax, jax.numpy as jnp
        import numpy as np
        import math
        HIDDEN = 512
        N_HEADS = 32
        N_KV_HEADS = 8
        HEAD_DIM = HIDDEN // N_HEADS
        GROUPS = N_HEADS // N_KV_HEADS
        ROPE_THETA = 10000.0
        TOKEN_BUDGET = 128
        INIT_BUDGET = 128
        RECENT_BUDGET = 128
        CHUNK = 16
        B, S = (1, 256)

        def _rotate_half(x):
            x1, x2 = jnp.split(x, 2, axis=-1)
            return jnp.concatenate([-x2, x1], axis=-1)

        def _rope(seq_len, dtype):
            inv_freq = 1.0 / ROPE_THETA ** (jnp.arange(0, HEAD_DIM, 2, dtype=jnp.float32) / HEAD_DIM)
            freqs = jnp.arange(seq_len, dtype=jnp.float32)[:, None] * inv_freq[None, :]
            emb = jnp.concatenate([freqs, freqs], axis=-1)
            return (jnp.cos(emb).astype(dtype), jnp.sin(emb).astype(dtype))
        key = jax.random.key(seed)
        ks = jax.random.split(key, 5)
        sc = 0.02
        return {'hidden_states': jax.random.normal(ks[0], (B, S, HIDDEN), dtype=jnp.float32), 'wq': jax.random.normal(ks[1], (N_HEADS * HEAD_DIM, HIDDEN), dtype=jnp.float32) * sc, 'wk': jax.random.normal(ks[2], (N_KV_HEADS * HEAD_DIM, HIDDEN), dtype=jnp.float32) * sc, 'wv': jax.random.normal(ks[3], (N_KV_HEADS * HEAD_DIM, HIDDEN), dtype=jnp.float32) * sc, 'wo': jax.random.normal(ks[4], (HIDDEN, N_HEADS * HEAD_DIM), dtype=jnp.float32) * sc}
    _L1_attn_in = _L1_attn_setup()

    def _L1_ffn_setup():
        import jax, jax.numpy as jnp
        import numpy as np
        ALPHA = 32
        R = 16
        SCALING = ALPHA / R
        key = jax.random.key(seed)
        k1, k2, k3, k4 = jax.random.split(key, 4)
        B_, S, D = (4, 256, 512)
        H, r, O = (8, R, 512)
        x = jax.random.normal(k1, (B_, S, D), dtype=jnp.float32)
        A = jax.random.normal(k2, (H, r, D), dtype=jnp.float32) * 0.02
        Bm = jax.random.normal(k3, (H, O, r), dtype=jnp.float32) * 0.02
        Wr = jax.random.normal(k4, (H, D), dtype=jnp.float32) * 0.02
        br = jnp.zeros((H,), dtype=jnp.float32)
        return {'x': x, 'A': A, 'B': Bm, 'Wr': Wr, 'br': br}
    _L1_ffn_in = _L1_ffn_setup()
    _d = {'L0_attn_x': _L0_attn_in['x'], 'L0_attn_w1': _L0_attn_in['w1'], 'L0_attn_w2': _L0_attn_in['w2'], 'L0_attn_b2': _L0_attn_in['b2'], 'L0_attn_sparse_mask': _L0_attn_in['sparse_mask'], 'L0_ffn_gate_q': _L0_ffn_in['gate_q'], 'L0_ffn_gate_scale': _L0_ffn_in['gate_scale'], 'L0_ffn_gate_A': _L0_ffn_in['gate_A'], 'L0_ffn_gate_B': _L0_ffn_in['gate_B'], 'L0_ffn_up_q': _L0_ffn_in['up_q'], 'L0_ffn_up_scale': _L0_ffn_in['up_scale'], 'L0_ffn_up_A': _L0_ffn_in['up_A'], 'L0_ffn_up_B': _L0_ffn_in['up_B'], 'L0_ffn_down_q': _L0_ffn_in['down_q'], 'L0_ffn_down_scale': _L0_ffn_in['down_scale'], 'L0_ffn_down_A': _L0_ffn_in['down_A'], 'L0_ffn_down_B': _L0_ffn_in['down_B'], 'L1_attn_wq': _L1_attn_in['wq'], 'L1_attn_wk': _L1_attn_in['wk'], 'L1_attn_wv': _L1_attn_in['wv'], 'L1_attn_wo': _L1_attn_in['wo'], 'L1_ffn_A': _L1_ffn_in['A'], 'L1_ffn_B': _L1_ffn_in['B'], 'L1_ffn_Wr': _L1_ffn_in['Wr'], 'L1_ffn_br': _L1_ffn_in['br']}
    _x0 = _d['L0_attn_x']
    _d['L0_attn_x'] = jax.random.normal(jax.random.fold_in(jax.random.key(seed), 1), (2, 1024, 512), dtype=_x0.dtype)
    del _x0
    return _d

def reference(L0_attn_x, L0_attn_w1, L0_attn_w2, L0_attn_b2, L0_attn_sparse_mask, L0_ffn_gate_q, L0_ffn_gate_scale, L0_ffn_gate_A, L0_ffn_gate_B, L0_ffn_up_q, L0_ffn_up_scale, L0_ffn_up_A, L0_ffn_up_B, L0_ffn_down_q, L0_ffn_down_scale, L0_ffn_down_A, L0_ffn_down_B, L1_attn_wq, L1_attn_wk, L1_attn_wv, L1_attn_wo, L1_ffn_A, L1_ffn_B, L1_ffn_Wr, L1_ffn_br):

    def _L0_attn_ref(x, w1, w2, b2, sparse_mask):
        import math
        import jax, jax.numpy as jnp
        import numpy as np
        IN_F, OUT_F, HID = (512, 512, 512)
        WINDOW, STRIPES = (6, 3)

        def make_sparse_mask(n_in=IN_F, n_out=OUT_F, window=WINDOW, stripes=STRIPES):
            m = np.zeros((n_in, n_out), dtype=np.float32)
            stride = int(math.sqrt(n_in))
            for k in range(stripes):
                ps = stride * k
                for i in range(0, n_in, window):
                    m[ps + i:ps + i + window, i:i + window] = 1.0
            mb = m.astype(bool)
            return jnp.asarray((mb | mb.T).astype(np.float32))
        attn = jnp.einsum('ds,td->st', w1, w2) * sparse_mask
        y = jnp.einsum('bds,st->bdt', x, attn) + b2
        return jax.nn.gelu(y, approximate=False)

    def _L0_ffn_ref(x, gate_q, gate_scale, gate_A, gate_B, up_q, up_scale, up_A, up_B, down_q, down_scale, down_A, down_B):
        import jax, jax.numpy as jnp
        import numpy as np
        H = 512
        I = 1376
        R = 32
        NLEV = 16
        Q_ZERO = 7.5
        Q_STEP = 0.005
        LR_SCALE = 0.02

        def _qlinear(x, q, scale, A, Bm):
            w = (q.astype(jnp.float32) - Q_ZERO) * (scale * Q_STEP)[:, None]
            y = jnp.einsum('bsh,oh->bso', x, w)
            return y + LR_SCALE * (x @ A @ Bm)
        g = _qlinear(x, gate_q, gate_scale, gate_A, gate_B)
        u = _qlinear(x, up_q, up_scale, up_A, up_B)
        h = jax.nn.silu(g) * u
        return _qlinear(h, down_q, down_scale, down_A, down_B)

    def _L1_attn_ref(hidden_states, wq, wk, wv, wo):
        import jax, jax.numpy as jnp
        import numpy as np
        import math
        HIDDEN = 512
        N_HEADS = 32
        N_KV_HEADS = 8
        HEAD_DIM = HIDDEN // N_HEADS
        GROUPS = N_HEADS // N_KV_HEADS
        ROPE_THETA = 10000.0
        TOKEN_BUDGET = 128
        INIT_BUDGET = 128
        RECENT_BUDGET = 128
        CHUNK = 16
        B, S = (1, 256)

        def _rotate_half(x):
            x1, x2 = jnp.split(x, 2, axis=-1)
            return jnp.concatenate([-x2, x1], axis=-1)

        def _rope(seq_len, dtype):
            inv_freq = 1.0 / ROPE_THETA ** (jnp.arange(0, HEAD_DIM, 2, dtype=jnp.float32) / HEAD_DIM)
            freqs = jnp.arange(seq_len, dtype=jnp.float32)[:, None] * inv_freq[None, :]
            emb = jnp.concatenate([freqs, freqs], axis=-1)
            return (jnp.cos(emb).astype(dtype), jnp.sin(emb).astype(dtype))
        b, s, _ = hidden_states.shape
        dtype = hidden_states.dtype
        NEG = jnp.finfo(dtype).min
        q = (hidden_states @ wq.T).reshape(b, s, N_HEADS, HEAD_DIM).transpose(0, 2, 1, 3)
        k = (hidden_states @ wk.T).reshape(b, s, N_KV_HEADS, HEAD_DIM).transpose(0, 2, 1, 3)
        v = (hidden_states @ wv.T).reshape(b, s, N_KV_HEADS, HEAD_DIM).transpose(0, 2, 1, 3)
        cos, sin = _rope(s, dtype)
        q = q * cos[None, None] + _rotate_half(q) * sin[None, None]
        k = k * cos[None, None] + _rotate_half(k) * sin[None, None]
        k = jnp.repeat(k, GROUPS, axis=1)
        v = jnp.repeat(v, GROUPS, axis=1)
        scores = jnp.einsum('bhqd,bhkd->bhqk', q, k) / math.sqrt(HEAD_DIM)
        q_pos = jnp.arange(s)[:, None]
        k_pos = jnp.arange(s)[None, :]
        causal = k_pos <= q_pos
        masked = jnp.where(causal[None, None], scores, NEG)
        pad = -s % CHUNK
        padded = jnp.pad(masked, ((0, 0), (0, 0), (0, 0), (0, pad)), constant_values=NEG)
        n_chunks = (s + pad) // CHUNK
        chunk_max = padded.reshape(b, N_HEADS, s, n_chunks, CHUNK).max(axis=-1)
        k_top = min(max(3, TOKEN_BUDGET // CHUNK), n_chunks)
        _, topk_idx = jax.lax.top_k(chunk_max, k_top)
        chunk_mask = jnp.any(topk_idx[..., None] == jnp.arange(n_chunks), axis=-2)
        tok_mask = jnp.repeat(chunk_mask, CHUNK, axis=-1)[..., :s]
        init_mask = k_pos < INIT_BUDGET
        recent_mask = k_pos > q_pos - RECENT_BUDGET
        allowed = causal[None, None] & (tok_mask | init_mask[None, None] | recent_mask[None, None])
        final = jnp.where(allowed, scores, NEG)
        attn = jax.nn.softmax(final, axis=-1)
        out = jnp.einsum('bhqk,bhkd->bhqd', attn, v)
        out = out.transpose(0, 2, 1, 3).reshape(b, s, N_HEADS * HEAD_DIM)
        return out @ wo.T

    def _L1_ffn_ref(x, A, B, Wr, br):
        import jax, jax.numpy as jnp
        import numpy as np
        ALPHA = 32
        R = 16
        SCALING = ALPHA / R
        H = A.shape[0]
        router_logits = jnp.einsum('bsd,hd->bsh', x, Wr) + br
        scores = H * jax.nn.softmax(router_logits, axis=-1)
        low = jnp.einsum('bsd,hrd->bshr', x, A)
        out = jnp.einsum('bshr,hor,bsh->bso', low, B, scores)
        return SCALING * out
    x = L0_attn_x
    x = x + _layernorm(_L0_attn_ref(_layernorm(x, axis=-1), L0_attn_w1, L0_attn_w2, L0_attn_b2, L0_attn_sparse_mask), axis=-1)
    x = x + _layernorm(_L0_ffn_ref(_layernorm(x, axis=-1), L0_ffn_gate_q, L0_ffn_gate_scale, L0_ffn_gate_A, L0_ffn_gate_B, L0_ffn_up_q, L0_ffn_up_scale, L0_ffn_up_A, L0_ffn_up_B, L0_ffn_down_q, L0_ffn_down_scale, L0_ffn_down_A, L0_ffn_down_B), axis=-1)
    x = x + _layernorm(_L1_attn_ref(_layernorm(x, axis=-1), L1_attn_wq, L1_attn_wk, L1_attn_wv, L1_attn_wo), axis=-1)
    x = x + _layernorm(_L1_ffn_ref(_layernorm(x, axis=-1), L1_ffn_A, L1_ffn_B, L1_ffn_Wr, L1_ffn_br), axis=-1)
    return x

_drawn_inputs = setup_inputs


def setup_inputs(seed=0):
    import zlib

    import numpy as np

    out = dict(_drawn_inputs(seed))
    spreads = {'L1_ffn_br': (0.0, 0.1)}
    factors = {}
    for name, (base, spread) in spreads.items():
        noise = np.random.default_rng([zlib.crc32(name.encode()), seed]).standard_normal(out[name].shape)
        drawn = base * np.exp(spread * noise) if base else spread * noise
        out[name] = jnp.asarray(drawn.astype(out[name].dtype))
    for name, factor in factors.items():
        out[name] = (out[name] * factor).astype(out[name].dtype)
    return out
```

```python
from contextlib import ExitStack

import numpy as np

import concourse.bass as bass
from concourse import mybir

F32 = mybir.dt.float32
BF16 = mybir.dt.bfloat16
I32 = mybir.dt.int32
ALU = mybir.AluOpType
ACT = mybir.ActivationFunctionType
AXX = mybir.AxisListType.X
ds = bass.ds

P = 128
BATCH, SEQ, D = 2, 1024, 512
TILES = BATCH * SEQ // P
SEQ_TILES = SEQ // P
DC = D // P
INNER = 1376
IT = (INNER + P - 1) // P
I_LAST = INNER - (IT - 1) * P
RANK = 32
Q_ZERO, Q_STEP, LR_SCALE = 7.5, 0.005, 0.02
HEADS, KV, HD = 32, 8, 16
GQ = HEADS // KV
CHUNK = 16
CPT = P // CHUNK
TOPK = 8
PARTS = 3
ROWS = 6 * HD
LORA_H, LORA_R = 8, 16
EPS = 1e-5
NEG = -float(2.0 ** 100)
TAKEN = 3e38
QK = (HEADS + KV) * HD
QKV = QK + KV * HD
GROUPS = BATCH * KV
ST_TILE = (GQ + 1) * ROWS
ST_W = SEQ_TILES * ST_TILE
MASK_ROWS = 3 * CPT + PARTS
KROWS = ROWS + MASK_ROWS

X_AT = 0
CONST_AT = X_AT + TILES * D
REG = CONST_AT + 1152
SLOT = IT * D
UPQ_AT, DOWNQ_AT, GATEQ_AT, WG_AT = REG, REG + SLOT, REG + 2 * SLOT, REG + 3 * SLOT
WD_AT, HT_AT, WU_AT = UPQ_AT, DOWNQ_AT, GATEQ_AT
ATTN0_AT = WG_AT + DC * INNER
WQKV_AT = ATTN0_AT + DC * D
WORK = WQKV_AT + DC * QKV
V_AT = REG
O_AT = V_AT + GROUPS * SEQ_TILES * 32
CWORK = O_AT + GROUPS * SEQ_TILES * GQ * HD
ARENA = 53100


class Count:

    def __init__(self, sem):
        self.sem, self.total, self.base, self.n = sem, 0, 0, 0

    def enter(self, i, per):
        self.base, self.n, self.per = i * per + self.total, 0, per

    def leave(self, turns):
        assert self.n == self.per, (self.n, self.per)
        self.total += turns * self.per
        self.base, self.n = self.total, 0

    def settle(self):
        self.total, self.base, self.n = self.base + self.n, self.base + self.n, 0

    def mark(self, ins):
        ins.then_inc(self.sem, 1)
        self.n += 1

    def wait(self, eng):
        eng.wait_ge(self.sem, self.base + self.n)

    def wait_apart(self, eng, turnstile):
        self.wait(eng)
        eng.sem_inc(turnstile, 1)


class Mem:

    def __init__(self, nc, ctx):
        self.nc, self.ctx = nc, ctx
        self.arena = ctx.enter_context(nc.sbuf_tensor("arena", [P, ARENA], F32))
        self.banks = [ctx.enter_context(nc.psum_tensor(f"bank{i}", [P, 512], F32)) for i in range(8)]
        self.turnstile, self.last_in = self.sem("turnstile"), self.sem("last_in")
        c = CONST_AT
        self.ident = self.f32(c, P); c += P
        self.causal = self.bf16(c, P); c += P // 2
        self.own_chunk = self.bf16(c, P); c += P // 2
        self.ident_bf = self.bf16(c, P); c += P // 2
        self.ident4 = self.bf16(c, 4 * P); c += 2 * P
        self.chunk_before = self.f32(c, CPT); c += CPT
        self.chunk_own = self.f32(c, CPT); c += CPT
        self.cos = self.f32(c, SEQ_TILES * HD); c += SEQ_TILES * HD
        self.sin = self.f32(c, SEQ_TILES * HD); c += SEQ_TILES * HD
        self.eps = self.f32(c, TILES); c += TILES
        self.half = self.f32(c, TILES); c += TILES
        self.mv_next = self.f32(c, 2 * TILES); c += 2 * TILES
        self.rstd = self.f32(c, TILES); c += TILES
        self.shift = self.f32(c, TILES); c += TILES
        self.scales = self.f32(c, 2 * IT + DC); c += 2 * IT + DC
        self.zero16 = self.f32(c, TILES); c += TILES
        self.ve16 = self.f32(c, TILES); c += TILES
        self.stats = [self.f32(c + 6 * i, 6) for i in range(2)]; c += 12
        self.mv = [self.f32(c + 2 * i, 2) for i in range(2)]; c += 4
        self.ve = [self.f32(c + i, 1) for i in range(2)]; c += 2
        self.rs = [self.f32(c + i, 1) for i in range(2)]; c += 2
        self.ms = [self.f32(c + i, 1) for i in range(2)]; c += 2
        self.stats_x = [self.f32(c + 6 * i, 6) for i in range(2)]; c += 12
        self.mv_x = [self.f32(c + 2 * i, 2) for i in range(2)]; c += 4
        assert c <= REG, c - CONST_AT
        self.key_aug = [self.bf16(ARENA - (2 - i) * SEQ // 2, SEQ) for i in range(2)]

    def f32(self, at, n):
        return self.arena[:, at:at + n]

    def bf16(self, at, n):
        return self.arena[:, at:at + (n + 1) // 2].bitcast(BF16)[:, 0:n]

    def i32(self, at, n):
        return self.arena[:, at:at + n].bitcast(I32)

    def x(self, tile):
        return self.arena[:, ds(tile * D + X_AT, D)]

    def taker(self, at, limit):
        place = [at]

        def take(n, dtype=F32):
            words = n if dtype == F32 else (n + 1) // 2
            view = self.f32(place[0], n) if dtype == F32 else self.bf16(place[0], n)
            place[0] += words
            assert place[0] <= limit, place[0]
            return view
        return take

    def sem(self, name):
        return self.ctx.enter_context(self.nc.semaphore(name))


def rstd_all(pool, m, seq):
    mv = m.mv_next.rearrange("p (t s) -> p t s", s=2)
    seq.mark(pool.tensor_tensor(out=m.rstd, in0=mv[:, :, 1], in1=m.eps, op=ALU.add))
    seq.wait(pool)
    seq.mark(pool.tensor_tensor(out=m.shift, in0=m.rstd, in1=m.half, op=ALU.pow))
    seq.wait(pool)
    seq.mark(pool.tensor_copy(m.rstd, m.shift))
    seq.wait(pool)
    seq.mark(pool.tensor_tensor(out=m.ve16, in0=mv[:, :, 0], in1=m.rstd, op=ALU.mult))
    seq.wait(pool)
    return pool.tensor_tensor(out=m.shift, in0=m.zero16, in1=m.ve16, op=ALU.subtract)


def branch_stats(dve, m, seq, p, y):
    seq.mark(dve.bn_stats(out=m.stats[p], in_=y))
    seq.wait_apart(dve, m.turnstile)
    return dve.bn_aggr(out=m.mv[p], in_=m.stats[p])


def branch_rstd(pool, m, seq, p):
    seq.mark(pool.tensor_tensor(out=m.ve[p], in0=m.mv[p][:, 1:2], in1=m.eps[:, 0:1], op=ALU.add))
    seq.wait(pool)
    return pool.tensor_tensor(out=m.rs[p], in0=m.ve[p], in1=m.half[:, 0:1], op=ALU.pow)


def branch_add(dve, m, seq, p, y, tile, last=False):
    x = m.x(tile)
    seq.mark(dve.scalar_tensor_tensor(out=m.ms[p], in0=m.mv[p][:, 0:1], scalar=-1.0, in1=m.rs[p],
                                      op0=ALU.mult, op1=ALU.mult))
    seq.mark(dve.scalar_tensor_tensor(out=x, in0=y, scalar=m.rs[p], in1=x, op0=ALU.mult, op1=ALU.add))
    seq.wait(dve)
    if last:
        return dve.tensor_scalar(out=x, in0=x, scalar1=m.ms[p], scalar2=None, op0=ALU.add)
    seq.mark(dve.tensor_scalar(out=x, in0=x, scalar1=m.ms[p], scalar2=None, op0=ALU.add))
    seq.wait_apart(dve, m.turnstile)
    seq.mark(dve.bn_stats(out=m.stats_x[p], in_=x))
    seq.wait_apart(dve, m.turnstile)
    seq.mark(dve.bn_aggr(out=m.mv_x[p], in_=m.stats_x[p]))
    seq.wait(dve)
    return dve.tensor_copy(m.mv_next[:, ds(tile * 2, 2)], m.mv_x[p])


BRANCH_ADD_STEPS = 5


def setup_and_sparse(nc, m, s, dram):
    W2, W2T = m.f32(GATEQ_AT, DC * D), m.f32(GATEQ_AT + 2048, DC * D)
    W1, MASK = m.f32(GATEQ_AT + 4096, DC * D), m.f32(GATEQ_AT + 6144, DC * D)
    attn0 = m.f32(ATTN0_AT, DC * D)
    b2, ones = m.f32(WORK, D)[0:1, :], m.f32(WORK + D, P)[0:1, :]
    a = WORK + D + P
    xn = [m.f32(a + i * D, D) for i in range(2)]
    xT = [m.f32(a + (2 + i) * D, D) for i in range(2)]
    y = [m.f32(a + (4 + i) * D, D) for i in range(2)]
    cst = m.f32(a + 6 * D, 6 * P)
    kq = "p (c d) -> p c d"

    weights_in = [s("w2_in"), s("w1_in"), s("mask_in")]
    consts_in, x_in = s("consts_in"), [s(f"x_in{i}") for i in range(4)]
    m.q_in = [s("gate_q_in"), s("up_q_in"), s("down_q_in"), s("lowrank_in"), s("qkv_in")]
    consts_ready, w2_turned, w2T_ready = s("consts_ready"), s("w2_turned"), s("w2T_ready")
    raw_ready, attn0_ready = s("raw_ready"), s("attn0_ready")
    x_stats, rstd_ready = s("x_stats"), s("rstd_ready")
    xn_ready, turned, xT_ready = s("a_xn_ready"), s("a_turned"), s("a_xT_ready")
    y_ready, gelu_ready = s("a_y_ready"), s("a_gelu_ready")
    stats_ready, branch_rstd_ready, added = s("a_stats_ready"), s("a_branch_rstd"), s("a_added")
    dve_seq, pool_seq = Count(s("a_dve_seq")), Count(s("a_pool_seq"))

    with nc.Block() as block:
        @block.sync
        def _(sp):
            sp.dma_start(W2.rearrange(kq, c=DC), dram["w2"].rearrange("(c p) d -> p c d", p=P)).then_inc(weights_in[0], 16)
            sp.dma_start(cst, dram["consts"][:, 0:6 * P]).then_inc(consts_in, 16)
            sp.dma_start(W1.rearrange(kq, c=DC), dram["w1"].rearrange("(c p) d -> p c d", p=P)).then_inc(weights_in[1], 16)
            sp.dma_start(m.f32(X_AT, 4 * D).rearrange(kq, c=4),
                         dram["x"][0:4 * P, :].rearrange("(c p) d -> p c d", p=P)).then_inc(x_in[0], 16)
            sp.dma_start(MASK.rearrange(kq, c=DC), dram["mask"].rearrange("(c p) d -> p c d", p=P)).then_inc(weights_in[2], 16)
            sp.dma_start(b2, dram["b2"].rearrange("(a d) -> a d", a=1)).then_inc(weights_in[2], 16)
            for c in range(1, 4):
                sp.dma_start(m.f32(X_AT + c * 4 * D, 4 * D).rearrange(kq, c=4),
                             dram["x"][c * 4 * P:(c + 1) * 4 * P, :].rearrange("(c p) d -> p c d", p=P)).then_inc(x_in[c], 16)
            full = (IT - 1) * P
            sp.dma_start(m.i32(UPQ_AT, (IT - 1) * D).rearrange(kq, c=IT - 1),
                         dram["up_q"][0:full, :].rearrange("(c p) d -> p c d", p=P)).then_inc(m.q_in[1], 16)
            sp.dma_start(m.i32(UPQ_AT + (IT - 1) * D, D)[0:I_LAST, :], dram["up_q"][full:INNER, :]).then_inc(m.q_in[1], 16)
            sp.dma_start(m.i32(DOWNQ_AT, DC * INNER).rearrange(kq, c=DC),
                         dram["down_q"].rearrange("(c p) i -> p c i", p=P)).then_inc(m.q_in[2], 16)
            sp.wait_ge(attn0_ready, DC)
            sp.dma_start(m.i32(GATEQ_AT, (IT - 1) * D).rearrange(kq, c=IT - 1),
                         dram["gate_q"][0:full, :].rearrange("(c p) d -> p c d", p=P)).then_inc(m.q_in[0], 16)
            sp.dma_start(m.i32(GATEQ_AT + (IT - 1) * D, D)[0:I_LAST, :], dram["gate_q"][full:INNER, :]).then_inc(m.q_in[0], 16)
            load_small_weights(sp, m, dram)

        @block.gpsimd
        def _(pool):
            pool.memset(m.eps, EPS)
            pool.memset(m.half, -0.5)
            pool.memset(m.zero16, 0.0)
            pool.memset(ones, 1.0).then_inc(consts_ready, 1)
            pool.wait_ge(consts_in, 16)
            pool.wait_ge(consts_ready, 1)
            pool.tensor_copy(m.ident, cst[:, 0:P]).then_inc(consts_ready, 1)
            pool.tensor_copy(m.ident_bf, cst[:, 0:P])
            for h in range(4):
                pool.tensor_copy(m.ident4[:, h * P:(h + 1) * P], cst[:, 0:P])
            pool.tensor_copy(m.causal, cst[:, P:2 * P])
            pool.tensor_copy(m.own_chunk, cst[:, 2 * P:3 * P])
            pool.tensor_copy(m.cos, cst[:, 3 * P:4 * P])
            pool.tensor_copy(m.sin, cst[:, 4 * P:5 * P])
            pool.tensor_copy(m.chunk_before, cst[:, 5 * P:5 * P + CPT])
            pool.tensor_copy(m.chunk_own, cst[:, 5 * P + CPT:5 * P + 2 * CPT]).then_inc(consts_ready, 1)
            pool.wait_ge(x_stats, TILES)
            rstd_all(pool, m, pool_seq).then_inc(rstd_ready, 1)
            pool_seq.settle()
            with pool.Fori(0, TILES // 2) as u:
                pool_seq.enter(u, 2)
                for p in range(2):
                    pool.wait_ge(stats_ready, u * 2 + p + 1)
                    branch_rstd(pool, m, pool_seq, p).then_inc(branch_rstd_ready, 1)
            pool_seq.leave(TILES // 2)

        @block.tensor
        def _(pe):
            pe.wait_ge(weights_in[0], 16)
            pe.wait_ge(consts_ready, 2)
            for dc in range(DC):
                for tc in range(DC):
                    last = pe.transpose(m.banks[dc][:, tc * P:(tc + 1) * P], W2[:, tc * D + dc * P:tc * D + (dc + 1) * P], m.ident)
                last.then_inc(w2_turned, 1)
            pe.wait_ge(weights_in[1], 16)
            for sc in range(DC):
                for dc in range(DC):
                    if sc == 0:
                        pe.wait_ge(w2T_ready, dc + 1)
                    last = pe.matmul(m.banks[4 + sc][:, :], W1[:, dc * D + sc * P:dc * D + (sc + 1) * P],
                                     W2T[:, dc * D:(dc + 1) * D], start=dc == 0, stop=dc == DC - 1)
                last.then_inc(raw_ready, 1)

            def turn(k, p):
                pe.wait_ge(xn_ready, k * 1 + 1)
                for dc in range(DC):
                    last = pe.transpose(m.banks[p][:, dc * P:(dc + 1) * P], xn[p][:, dc * P:(dc + 1) * P], m.ident)
                last.then_inc(turned, 1)

            def feed(k, p):
                pe.wait_ge(xT_ready, k + 1)
                pe.wait_ge(gelu_ready, k + 1)
                pe.matmul(m.banks[2 + p][:, :], ones, b2, start=True, stop=False)
                for dc in range(DC):
                    last = pe.matmul(m.banks[2 + p][:, :], xT[p][:, dc * P:(dc + 1) * P], attn0[:, dc * D:(dc + 1) * D],
                                     start=False, stop=dc == DC - 1)
                last.then_inc(y_ready, 1)

            for p in range(2):
                turn(p, p)
            pe.wait_ge(attn0_ready, DC)
            pe.wait_ge(weights_in[2], 32)
            with pe.Fori(0, TILES // 2 - 1) as u:
                for p in range(2):
                    feed(u * 2 + p, p)
                for p in range(2):
                    turn(u * 2 + (2 + p), p)
            for p in range(2):
                feed(TILES - 2 + p, p)

        @block.scalar
        def _(act):
            act.sem_inc(gelu_ready, 2)
            for dc in range(DC):
                act.wait_ge(w2_turned, dc + 1)
                act.activation(W2T[:, dc * D:(dc + 1) * D], m.banks[dc][:, :], ACT.Copy).then_inc(w2T_ready, 1)

            def normed(k, p):
                act.activation(xn[p], m.x(k), ACT.Identity, bias=m.shift[:, ds(k, 1)],
                               scale=m.rstd[:, ds(k, 1)]).then_inc(xn_ready, 1)

            def keep(k, p):
                act.wait_ge(turned, k + 1)
                act.activation(xT[p], m.banks[p][:, :], ACT.Copy).then_inc(xT_ready, 1)

            def gelu(k, p):
                act.wait_ge(y_ready, k + 1)
                act.wait_ge(added, k + 1)
                act.activation(y[p], m.banks[2 + p][:, :], ACT.Gelu).then_inc(gelu_ready, 1)

            act.wait_ge(rstd_ready, 1)
            for p in range(2):
                normed(p, p)
            for p in range(2):
                keep(p, p)
            with act.Fori(0, TILES // 2 - 1) as u:
                for p in range(2):
                    normed(u * 2 + (2 + p), p)
                for p in range(2):
                    gelu(u * 2 + p, p)
                for p in range(2):
                    keep(u * 2 + (2 + p), p)
            for p in range(2):
                gelu(TILES - 2 + p, p)

        @block.vector
        def _(dve):
            dve.sem_inc(added, 2)
            for sc in range(DC):
                if sc == 0:
                    dve.wait_ge(weights_in[2], 32)
                dve.wait_ge(raw_ready, sc + 1)
                dve.tensor_tensor(out=attn0[:, sc * D:(sc + 1) * D], in0=m.banks[4 + sc][:, :],
                                  in1=MASK[:, sc * D:(sc + 1) * D], op=ALU.mult).then_inc(attn0_ready, 1)
            st16 = m.f32(a + 8 * D, 6 * TILES)
            for t in range(TILES):
                if t % 4 == 0:
                    dve.wait_ge(x_in[t // 4], 16)
                dve_seq.mark(dve.bn_stats(out=st16[:, 6 * t:6 * t + 6], in_=m.x(t)))
            for t in range(TILES):
                if t == 0:
                    dve_seq.wait(dve)
                dve.bn_aggr(out=m.mv_next[:, 2 * t:2 * t + 2], in_=st16[:, 6 * t:6 * t + 6]).then_inc(x_stats, 1)
            dve_seq.settle()
            with dve.Fori(0, TILES // 2) as u:
                dve_seq.enter(u, 2 * (1 + BRANCH_ADD_STEPS))
                for p in range(2):
                    dve.wait_ge(gelu_ready, u * 2 + (p + 3))
                    branch_stats(dve, m, dve_seq, p, y[p]).then_inc(stats_ready, 1)
                for p in range(2):
                    dve.wait_ge(branch_rstd_ready, u * 2 + p + 1)
                    branch_add(dve, m, dve_seq, p, y[p], u * 2 + p).then_inc(added, 1)
            dve_seq.leave(TILES // 2)


LOW_AT = WORK + 4864
GB_AT, UB_AT, DB_AT = LOW_AT, LOW_AT + INNER, LOW_AT + 2 * INNER
GA_AT = DB_AT + D
UA_AT, DA_AT = GA_AT + DC * RANK, GA_AT + 2 * DC * RANK
WQ_AT = DA_AT + IT * RANK
GAT_AT = WQ_AT + 6 * D
UAT_AT, DAT_AT = GAT_AT + D, GAT_AT + 2 * D
DEQ_AT = DAT_AT + INNER


def load_small_weights(sp, m, dram):
    kq, full = "p (c d) -> p c d", (IT - 1) * P
    low, qkv = m.q_in[3], m.q_in[4]
    sp.dma_start(m.f32(GB_AT, INNER)[0:RANK, :], dram["gate_B"]).then_inc(low, 16)
    sp.dma_start(m.f32(UB_AT, INNER)[0:RANK, :], dram["up_B"]).then_inc(low, 16)
    sp.dma_start(m.f32(DB_AT, D)[0:RANK, :], dram["down_B"]).then_inc(low, 16)
    sp.dma_start(m.f32(GA_AT, DC * RANK).rearrange(kq, c=DC), dram["gate_A"].rearrange("(c p) r -> p c r", p=P)).then_inc(low, 16)
    sp.dma_start(m.f32(UA_AT, DC * RANK).rearrange(kq, c=DC), dram["up_A"].rearrange("(c p) r -> p c r", p=P)).then_inc(low, 16)
    sp.dma_start(m.f32(DA_AT, (IT - 1) * RANK).rearrange(kq, c=IT - 1),
                 dram["down_A"][0:full, :].rearrange("(c p) r -> p c r", p=P)).then_inc(low, 16)
    sp.dma_start(m.f32(DA_AT + (IT - 1) * RANK, RANK)[0:I_LAST, :], dram["down_A"][full:INNER, :]).then_inc(low, 16)
    for k, name in enumerate(("gate_scale", "up_scale")):
        sp.dma_start(m.scales[:, k * IT:k * IT + IT - 1], dram[name][0:full].rearrange("(c p) -> p c", p=P), allow_slow_non_contiguous=True).then_inc(low, 16)
        sp.dma_start(m.scales[0:I_LAST, k * IT + IT - 1:(k + 1) * IT],
                     dram[name][full:INNER].rearrange("(p c) -> p c", c=1), allow_slow_non_contiguous=True).then_inc(low, 16)
    sp.dma_start(m.scales[:, 2 * IT:2 * IT + DC], dram["down_scale"].rearrange("(c p) -> p c", p=P), allow_slow_non_contiguous=True).then_inc(low, 16)
    sp.dma_start(m.f32(WQ_AT, DC * D).rearrange(kq, c=DC), dram["wq"].rearrange("(c p) d -> p c d", p=P)).then_inc(qkv, 16)
    sp.dma_start(m.f32(WQ_AT + DC * D, D), dram["wk"]).then_inc(qkv, 16)
    sp.dma_start(m.f32(WQ_AT + (DC + 1) * D, D), dram["wv"]).then_inc(qkv, 16)


LOW_LOADS, QKV_LOADS = 12, 3


def weights(nc, m, s, dram):
    deq = [m.f32(DEQ_AT + i * D, D) for i in range(2)]
    down_AT_tile = [m.f32(DEQ_AT + (2 + i) * D, P)[0:RANK, :] for i in range(2)]
    gAT, uAT, dAT = (m.f32(at, n)[0:RANK, :] for at, n in ((GAT_AT, D), (UAT_AT, D), (DAT_AT, INNER)))
    wide = [(GATEQ_AT, gAT, GB_AT, WG_AT, 0), (UPQ_AT, uAT, UB_AT, WU_AT, IT)]
    down_first = 2 * IT
    scales_ready, factors_turned, factors_ready = s("scales_ready"), s("factors_turned"), s("factors_ready")
    deq_ready, down_A_ready, built, placed = s("deq_ready"), s("down_A_ready"), s("w_built"), s("w_placed")
    qkv_turned, qkv_placed = s("qkv_turned"), s("qkv_placed")
    scaled = 2 * IT + DC

    def rows(tile):
        return I_LAST if isinstance(tile, int) and tile == IT - 1 else P

    def each_tile(eng, first, body):
        with eng.Fori(0, (IT - 1) // 2) as u:
            for k in range(2):
                body(u * 2 + k, (first + k) % 2)
        body(IT - 1, (first + IT - 1) % 2)

    with nc.Block() as block:
        @block.tensor
        def _(pe):
            pe.wait_ge(m.q_in[3], 16 * LOW_LOADS)
            for k, (at, n) in enumerate(((GA_AT, DC), (UA_AT, DC))):
                for c in range(n):
                    last = pe.transpose(m.banks[k][0:RANK, c * P:(c + 1) * P], m.f32(at + c * RANK, RANK), m.ident)
                last.then_inc(factors_turned, 1)
            for c in range(IT):
                r = rows(c)
                last = pe.transpose(m.banks[2 + c // 4][0:RANK, c % 4 * P:c % 4 * P + r],
                                    m.f32(DA_AT + c * RANK, RANK)[0:r, :], m.ident[0:r, 0:r])
                if c % 4 == 3 or c == IT - 1:
                    last.then_inc(factors_turned, 1)
            pe.wait_ge(factors_ready, 5)
            for _, AT, b_at, _, first in wide:
                B = m.f32(b_at, INNER)[0:RANK, :]

                def tile(t, p):
                    r = rows(t)
                    bank = m.banks[6 + p]
                    pe.wait_ge(deq_ready, t + first + 1)
                    pe.wait_ge(placed, t + first + 1)
                    for hc in range(DC):
                        pe.matmul(bank[:, hc * P:hc * P + r], deq[p][0:r, hc * P:(hc + 1) * P], m.ident[0:r, 0:r],
                                  start=hc == 0, stop=False, skip_group_check=True)
                    for hc in range(DC):
                        last = pe.matmul(bank[:, hc * P:hc * P + r], AT[:, hc * P:(hc + 1) * P], B[:, ds(t * P, r)],
                                         start=False, stop=hc == DC - 1, skip_group_check=True)
                    last.then_inc(built, 1)
                each_tile(pe, first, tile)

            def down_tile(t, p):
                r = rows(t)
                bank = m.banks[6 + p]
                pe.wait_ge(deq_ready, t + down_first + 1)
                pe.wait_ge(down_A_ready, t + 3)
                pe.wait_ge(placed, t + down_first + 1)
                for oc in range(DC):
                    pe.matmul(bank[0:r, oc * P:(oc + 1) * P], deq[p][:, oc * P:oc * P + r], m.ident,
                              start=oc == 0, stop=False, skip_group_check=True)
                pe.matmul(bank[0:r, :], down_AT_tile[p][:, 0:r], m.f32(DB_AT, D)[0:RANK, :],
                          start=False, stop=True, skip_group_check=True).then_inc(built, 1)
            each_tile(pe, down_first, down_tile)

            pe.wait_ge(m.q_in[4], 16 * QKV_LOADS)
            for c in range(DC + 2):
                if c >= 5:
                    pe.wait_ge(qkv_placed, c - 4)
                for hc in range(DC):
                    last = pe.transpose(m.banks[c % 5][:, hc * P:(hc + 1) * P],
                                        m.f32(WQ_AT + c * D + hc * P, P), m.ident)
                last.then_inc(qkv_turned, 1)

        @block.vector
        def _(dve):
            dve.wait_ge(m.q_in[3], 16 * LOW_LOADS)
            dve.tensor_scalar(out=m.scales[:, 0:IT - 1], in0=m.scales[:, 0:IT - 1], scalar1=Q_STEP, scalar2=None, op0=ALU.mult)
            dve.tensor_scalar(out=m.scales[0:I_LAST, IT - 1:IT], in0=m.scales[0:I_LAST, IT - 1:IT], scalar1=Q_STEP, scalar2=None, op0=ALU.mult)
            dve.tensor_scalar(out=m.scales[:, IT:2 * IT - 1], in0=m.scales[:, IT:2 * IT - 1], scalar1=Q_STEP, scalar2=None, op0=ALU.mult)
            dve.tensor_scalar(out=m.scales[0:I_LAST, 2 * IT - 1:2 * IT], in0=m.scales[0:I_LAST, 2 * IT - 1:2 * IT], scalar1=Q_STEP, scalar2=None, op0=ALU.mult)
            dve.tensor_scalar(out=m.scales[:, 2 * IT:scaled], in0=m.scales[:, 2 * IT:scaled], scalar1=Q_STEP, scalar2=None, op0=ALU.mult).then_inc(scales_ready, 1)
            dve.wait_ge(scales_ready, 1)
            for k, (q_at, _, _, _, first) in enumerate(wide):
                dve.wait_ge(m.q_in[k], 32)

                def tile(t, p):
                    r = rows(t)
                    dve.wait_ge(built, t + first + 1)
                    dve.tensor_scalar(out=deq[p][0:r, :], in0=m.arena[0:r, ds(t * D + q_at, D)].bitcast(I32),
                                      scalar1=-Q_ZERO, scalar2=m.scales[0:r, ds(t + k * IT, 1)],
                                      op0=ALU.add, op1=ALU.mult).then_inc(deq_ready, 1)
                each_tile(dve, first, tile)
            dve.wait_ge(m.q_in[2], 16)
            q = m.i32(DOWNQ_AT, DC * INNER).rearrange("p (c i) -> p c i", c=DC)

            def down_tile(t, p):
                r = rows(t)
                dve.wait_ge(built, t + down_first + 1)
                dve.scalar_tensor_tensor(out=deq[p].rearrange("p (c i) -> p c i", c=DC)[:, :, 0:r], in0=q[:, :, ds(t * P, r)],
                                         scalar=-Q_ZERO, in1=m.scales[:, 2 * IT:scaled].unsqueeze(2).to_broadcast([P, DC, r]),
                                         op0=ALU.add, op1=ALU.mult).then_inc(deq_ready, 1)
            each_tile(dve, down_first, down_tile)

        @block.gpsimd
        def _(pool):
            pool.sem_inc(down_A_ready, 2)
            pool.sem_inc(built, 2)
            pool.wait_ge(factors_ready, 5)

            def tile(t, p):
                r = rows(t)
                pool.wait_ge(built, t + down_first + 1)
                pool.tensor_copy(down_AT_tile[p][:, 0:r], dAT[:, ds(t * P, r)]).then_inc(down_A_ready, 1)
            each_tile(pool, down_first, tile)

        @block.scalar
        def _(act):
            act.sem_inc(placed, 2)
            for k, AT in enumerate((gAT, uAT)):
                act.wait_ge(factors_turned, k + 1)
                act.activation(AT, m.banks[k][0:RANK, :], ACT.Copy, scale=LR_SCALE).then_inc(factors_ready, 1)
            for k in range(3):
                n = min(D, INNER - k * D)
                act.wait_ge(factors_turned, k + 3)
                act.activation(dAT[:, k * D:k * D + n], m.banks[2 + k][0:RANK, 0:n], ACT.Copy, scale=LR_SCALE).then_inc(factors_ready, 1)
            for _, _, _, out_at, first in wide:
                W = m.f32(out_at, DC * INNER).rearrange("p (c i) -> p c i", c=DC)

                def tile(t, p):
                    r = rows(t)
                    act.wait_ge(built, t + first + 3)
                    act.activation(W[:, :, ds(t * P, r)], m.banks[6 + p].rearrange("p (c i) -> p c i", c=DC)[:, :, 0:r],
                                   ACT.Copy).then_inc(placed, 1)
                each_tile(act, first, tile)

            def down_tile(t, p):
                r = rows(t)
                act.wait_ge(built, t + down_first + 3)
                act.activation(m.arena[0:r, ds(t * D + WD_AT, D)], m.banks[6 + p][0:r, :], ACT.Copy).then_inc(placed, 1)
            each_tile(act, down_first, down_tile)

            W = m.f32(WQKV_AT, DC * QKV).rearrange("p (c n) -> p c n", c=DC)
            for c in range(DC + 2):
                act.wait_ge(qkv_turned, c + 1)
                act.activation(W[:, :, c * P:(c + 1) * P], m.banks[c % 5].rearrange("p (c n) -> p c n", c=DC), ACT.Copy).then_inc(qkv_placed, 1)


def gated(nc, m, s, dram):
    G = 4
    Wg, Wu = m.f32(WG_AT, DC * INNER), m.f32(WU_AT, DC * INNER)
    xT = m.f32(WORK, DC * G * P)
    xn = [m.f32(WORK + DC * G * P + i * D, D) for i in range(G)]
    silu = [m.f32(WORK + DC * G * P + (G + i) * D, D) for i in range(2)]
    rstd_ready, xn_ready, turned, xT_ready = s("b_rstd"), s("b_xn"), s("b_turned"), s("b_xT")
    products, silu_ready, h_ready = s("b_products"), s("b_silu"), s("b_h_ready")
    down_ready, stats_ready, branch_rstd_ready, added = s("b_down"), s("b_stats"), s("b_branch_rstd"), s("b_added")
    dve_seq, pool_seq = Count(s("b_dve_seq")), Count(s("b_pool_seq"))
    n_groups = TILES // G

    def rows(i):
        return I_LAST if i == IT - 1 else P

    def h_free(g, i):
        return g * IT + (i + 1 if i >= 2 else 2 - i)

    def over_groups(eng, body):
        with eng.Fori(0, n_groups - 1) as g:
            body(g, False)
        body(n_groups - 1, True)

    with nc.Block() as block:
        @block.tensor
        def _(pe):
            def turn(g, t):
                k = g * G + t
                pe.wait_ge(xn_ready, k + 1)
                pe.wait_ge(xT_ready, k + 1)
                for dc in range(DC):
                    last = pe.transpose(m.banks[4 + t % 2][:, dc * P:(dc + 1) * P], xn[t][:, dc * P:(dc + 1) * P], m.ident)
                last.then_inc(turned, 1)

            def group(g, last_group):
                pe.wait_ge(xT_ready, g * G + (G + 2))
                for i in range(IT):
                    r = rows(i)
                    pe.wait_ge(h_ready, h_free(g, i))
                    for W, bank in ((Wg, m.banks[i % 2]), (Wu, m.banks[2 + i % 2])):
                        for dc in range(DC):
                            last = pe.matmul(bank[0:r, :], W[:, dc * INNER + i * P:dc * INNER + i * P + r],
                                             xT[:, dc * G * P:(dc + 1) * G * P], start=dc == 0, stop=dc == DC - 1)
                    last.then_inc(products, 1)
                if not last_group:
                    for t in range(G):
                        turn(g + 1, t)
                pe.wait_ge(h_ready, g * IT + (IT + 2))
                for t in range(G):
                    pe.wait_ge(added, g * G + (t + 1))
                    for i in range(IT):
                        r = rows(i)
                        last = pe.matmul(m.banks[6 + t % 2][:, :], m.f32(HT_AT + i * D + t * P, P)[0:r, :],
                                         m.f32(WD_AT + i * D, D)[0:r, :], start=i == 0, stop=i == IT - 1)
                    last.then_inc(down_ready, 1)

            for t in range(G):
                turn(0, t)
            over_groups(pe, group)

        @block.scalar
        def _(act):
            def normed(g, t):
                k = g * G + t
                act.activation(xn[t], m.x(k), ACT.Identity, bias=m.shift[:, ds(k, 1)],
                               scale=m.rstd[:, ds(k, 1)]).then_inc(xn_ready, 1)

            def keep(g, t):
                act.wait_ge(turned, g * G + (t + 1))
                act.activation(xT.rearrange("p (c n) -> p c n", c=DC)[:, :, t * P:(t + 1) * P],
                               m.banks[4 + t % 2].rearrange("p (c n) -> p c n", c=DC), ACT.Copy).then_inc(xT_ready, 1)

            def group(g, last_group):
                for i in range(IT):
                    r = rows(i)
                    act.wait_ge(products, g * IT + (i + 1))
                    act.wait_ge(h_ready, h_free(g, i))
                    act.activation(silu[i % 2][0:r, :], m.banks[i % 2][0:r, :], ACT.Silu).then_inc(silu_ready, 1)
                    if i in (1, 3, 5, 7) and not last_group:
                        normed(g + 1, i // 2)
                if not last_group:
                    for t in range(G):
                        keep(g + 1, t)

            act.sem_inc(xT_ready, 2)
            act.wait_ge(rstd_ready, 1)
            for t in range(G):
                normed(0, t)
            for t in range(G):
                keep(0, t)
            over_groups(act, group)

        @block.vector
        def _(dve):
            dve.sem_inc(h_ready, 2)
            dve.sem_inc(added, 2)

            def group(g, _):
                for i in range(IT):
                    r = rows(i)
                    dve.wait_ge(silu_ready, g * IT + (i + 1))
                    dve.tensor_tensor(out=m.f32(HT_AT + i * D, D)[0:r, :], in0=m.banks[2 + i % 2][0:r, :],
                                      in1=silu[i % 2][0:r, :], op=ALU.mult).then_inc(h_ready, 1)
                dve_seq.enter(g, G * (1 + BRANCH_ADD_STEPS))
                for t in range(G):
                    dve.wait_ge(down_ready, g * G + (t + 1))
                    branch_stats(dve, m, dve_seq, t % 2, m.banks[6 + t % 2][:, :]).then_inc(stats_ready, 1)
                    dve.wait_ge(branch_rstd_ready, g * G + (t + 1))
                    branch_add(dve, m, dve_seq, t % 2, m.banks[6 + t % 2][:, :], g * G + t).then_inc(added, 1)
            over_groups(dve, group)

        @block.gpsimd
        def _(pool):
            rstd_all(pool, m, pool_seq).then_inc(rstd_ready, 1)
            pool_seq.settle()

            def group(g, _):
                pool_seq.enter(g, G)
                for t in range(G):
                    pool.wait_ge(stats_ready, g * G + (t + 1))
                    branch_rstd(pool, m, pool_seq, t % 2).then_inc(branch_rstd_ready, 1)
            over_groups(pool, group)


def project(nc, m, s, dram):
    W = m.f32(WQKV_AT, DC * QKV)
    take = m.taker(WORK, ARENA - SEQ)
    xn, xT = [take(D) for _ in range(2)], [take(D) for _ in range(2)]
    raw, spun = [take(QK) for _ in range(2)], [take(QK) for _ in range(2)]
    rotated = [take(QK) for _ in range(2)]
    part = [[take(QK, BF16) for _ in range(PARTS)] for _ in range(2)]
    q_rows, k_rows = [take(HEADS * ROWS, BF16) for _ in range(2)], [take(KV * ROWS, BF16) for _ in range(2)]
    key_rows = take(SEQ)
    v_all = m.f32(V_AT, GROUPS * SEQ_TILES * 32)
    rstd_ready, xn_ready, turned, xT_ready = s("c_rstd"), s("c_xn"), s("c_turned"), s("c_xT")
    products, raw_ready, v_ready, spun_ready = s("c_products"), s("c_raw"), s("c_v"), s("c_spun")
    rotated_ready, high_ready, high_rows_ready = s("c_rotated"), s("c_high"), s("c_high_rows")
    rows_ready, rows_out = s("c_rows_ready"), [s(f"c_rows_out{b}") for b in range(2)]
    v_blank, rows_in = s("c_v_blank"), s("c_rows_in")
    dve_seq, pool_seq = Count(s("c_dve_seq")), Count(s("c_pool_seq"))

    def heads(ap):
        return ap.rearrange("p (h d) -> p h d", d=HD)

    def slots(ap):
        return ap.rearrange("p (h r d) -> p h r d", r=6, d=HD)

    def q_of(ap, n):
        return heads(ap[:, 0:HEADS * HD]).unsqueeze(2).to_broadcast([P, HEADS, n, HD])

    def k_of(ap, n):
        return heads(ap[:, HEADS * HD:QK]).unsqueeze(2).to_broadcast([P, KV, n, HD])

    with nc.Block() as block:
        @block.sync
        def _(sp):
            sp.dma_start(key_rows[ROWS:KROWS, :], dram["key_rows"]).then_inc(rows_in, 16)
            with sp.Fori(0, SEQ_TILES) as i:
                for b in range(2):
                    k = i * 2 + b
                    to = dram["rows"][b * KV:(b + 1) * KV].rearrange("k p (t w) -> p k t w", t=SEQ_TILES)[:, :, ds(i, 1), :].squeeze(2)
                    sp.wait_ge(high_rows_ready, k + 1)
                    sp.wait_ge(rows_ready, k + 1)
                    sp.dma_start(to[:, :, 0:GQ * ROWS], q_rows[b].rearrange("p (k w) -> p k w", k=KV)).then_inc(rows_out[b], 16)
                    sp.dma_start(to[:, :, GQ * ROWS:], k_rows[b].rearrange("p (k w) -> p k w", k=KV)).then_inc(rows_out[b], 16)
            for b in range(2):
                sp.wait_ge(rows_out[b], SEQ_TILES * 32 + 32)

        @block.tensor
        def _(pe):
            def turn(k, b):
                pe.wait_ge(xn_ready, k + 1)
                for dc in range(DC):
                    last = pe.transpose(m.banks[b][:, dc * P:(dc + 1) * P], xn[b][:, dc * P:(dc + 1) * P], m.ident)
                last.then_inc(turned, 1)

            def feed(k, b):
                pe.wait_ge(xT_ready, k + 1)
                pe.wait_ge(v_ready, k + 1)
                for dc in range(DC):
                    pe.matmul(m.banks[2 + b][:, :], xT[b][:, dc * P:(dc + 1) * P], W[:, dc * QKV:dc * QKV + D],
                              start=dc == 0, stop=dc == DC - 1)
                for dc in range(DC):
                    last = pe.matmul(m.banks[4 + b][:, 0:QKV - D], xT[b][:, dc * P:(dc + 1) * P], W[:, dc * QKV + D:(dc + 1) * QKV],
                                     start=dc == 0, stop=dc == DC - 1)
                last.then_inc(products, 1)

            for b in range(2):
                turn(b, b)
            with pe.Fori(0, SEQ_TILES - 1) as i:
                for b in range(2):
                    feed(i * 2 + b, b)
                for b in range(2):
                    turn(i * 2 + (2 + b), b)
            for b in range(2):
                feed(TILES - 2 + b, b)

        @block.scalar
        def _(act):
            def normed(i, b):
                act.activation(xn[b], m.x(i + b * SEQ_TILES), ACT.Identity, bias=m.shift[:, ds(i + b * SEQ_TILES, 1)],
                               scale=m.rstd[:, ds(i + b * SEQ_TILES, 1)]).then_inc(xn_ready, 1)

            def keep(k, b):
                act.wait_ge(turned, k + 1)
                act.activation(xT[b], m.banks[b][:, :], ACT.Copy).then_inc(xT_ready, 1)

            def evacuate(i, b):
                k = i * 2 + b
                act.wait_ge(products, k + 1)
                act.wait_ge(rotated_ready, k + 1)
                act.activation(raw[b][:, 0:D], m.banks[2 + b][:, :], ACT.Copy)
                act.activation(raw[b][:, D:QK], m.banks[4 + b][:, 0:QK - D], ACT.Copy).then_inc(raw_ready, 1)
                v = v_all.rearrange("p (b k t c) -> p b k t c", b=BATCH, k=KV, t=SEQ_TILES)[:, b]
                act.activation(v[:, :, ds(i, 1), 0:HD].squeeze(2), heads(m.banks[4 + b][:, QK - D:QKV - D]), ACT.Copy).then_inc(v_ready, 1)

            def cut(i, b):
                k = i * 2 + b
                act.wait_ge(rotated_ready, k + 3)
                act.activation(part[b][0], rotated[b], ACT.Copy).then_inc(high_ready, 1)
                act.wait_ge(rows_out[b], i * 32 + 32)
                act.wait_ge(high_ready, k + 1)
                act.activation(slots(q_rows[b])[:, :, 0:3, :], q_of(part[b][0], 3), ACT.Copy).then_inc(high_rows_ready, 1)

            act.sem_inc(v_ready, 2)
            act.wait_ge(rstd_ready, 1)
            act.wait_ge(v_blank, 1)
            for b in range(2):
                normed(0, b)
            for b in range(2):
                keep(b, b)
            with act.Fori(0, SEQ_TILES - 1) as i:
                for b in range(2):
                    normed(i + 1, b)
                for b in range(2):
                    evacuate(i, b)
                for b in range(2):
                    keep(i * 2 + (2 + b), b)
                for b in range(2):
                    cut(i, b)
            for b in range(2):
                evacuate(SEQ_TILES - 1, b)
            for b in range(2):
                cut(SEQ_TILES - 1, b)

        @block.gpsimd
        def _(pool):
            v = v_all.rearrange("p (n c) -> p n c", c=32)
            pool.memset(v[:, :, HD + 1:], 0.0)
            pool.memset(v[:, :, HD:HD + 1], 1.0).then_inc(v_blank, 1)
            rstd_all(pool, m, pool_seq).then_inc(rstd_ready, 1)
            pool.sem_inc(rotated_ready, 2)
            for b in range(2):
                pool.sem_inc(rows_out[b], 32)
            pool_seq.settle()
            with pool.Fori(0, SEQ_TILES) as i:
                for b in range(2):
                    sin = m.sin.rearrange("p (t d) -> p t d", d=HD)[:, ds(i, 1), :]
                    pool.wait_ge(rotated_ready, i * 2 + b + 1)
                    pool.wait_ge(raw_ready, i * 2 + b + 1)
                    pool.sem_inc(m.turnstile, 1)
                    h = HD // 2
                    for lo, hi in ((0, h), (h, 0)):
                        last = pool.tensor_tensor(out=heads(spun[b])[:, :, lo:lo + h], in0=heads(raw[b])[:, :, hi:hi + h],
                                                  in1=sin[:, :, lo:lo + h].to_broadcast([P, QK // HD, h]), op=ALU.mult)
                    last.then_inc(spun_ready, 1)

        @block.vector
        def _(dve):
            dve.wait_ge(rows_in, 16)
            for k in range(2):
                dve.tensor_copy(m.key_aug[k][ROWS:KROWS, :], key_rows[ROWS:KROWS, :])
            with dve.Fori(0, SEQ_TILES) as i:
                dve_seq.enter(i, 12)
                cos = m.cos.rearrange("p (t d) -> p t d", d=HD)[:, ds(i, 1), :]
                for b in range(2):
                    k = i * 2 + b
                    dve.wait_ge(raw_ready, k + 1)
                    dve_seq.mark(dve.tensor_tensor(out=heads(rotated[b]), in0=heads(raw[b]),
                                                   in1=cos.to_broadcast([P, QK // HD, HD]), op=ALU.mult))
                    dve_seq.wait(dve)
                    dve.wait_ge(spun_ready, k + 1)
                    dve.tensor_tensor(out=rotated[b], in0=rotated[b], in1=spun[b], op=ALU.add).then_inc(rotated_ready, 1)
                for b in range(2):
                    k = i * 2 + b
                    high, mid, low = part[b]
                    dve.wait_ge(high_ready, k + 1)
                    dve_seq.mark(dve.tensor_tensor(out=rotated[b], in0=rotated[b], in1=high, op=ALU.subtract))
                    dve_seq.wait(dve)
                    dve_seq.mark(dve.tensor_copy(mid, rotated[b]))
                    dve_seq.wait(dve)
                    dve_seq.mark(dve.tensor_tensor(out=low, in0=rotated[b], in1=mid, op=ALU.subtract))
                    dve.wait_ge(rows_out[b], i * 32 + 32)
                    q, kk = slots(q_rows[b]), slots(k_rows[b])
                    dve_seq.mark(dve.tensor_copy(kk[:, :, 0:4:3, :], k_of(high, 2)))
                    dve_seq.mark(dve.tensor_copy(kk[:, :, 5:6, :], k_of(high, 1)))
                    dve.tensor_copy(kk[:, :, 1:5:3, :], k_of(mid, 2))
                    dve.tensor_copy(q[:, :, 3:5, :], q_of(mid, 2))
                    dve_seq.wait(dve)
                    dve.tensor_copy(kk[:, :, 2:3, :], k_of(low, 1))
                    dve.tensor_copy(q[:, :, 5:6, :], q_of(low, 1)).then_inc(rows_ready, 1)
            dve_seq.leave(SEQ_TILES)


def attention(nc, m, s, dram):
    take = m.taker(CWORK, ARENA - SEQ)
    N = GQ * P
    query_aug = [take(2 * N, BF16) for _ in range(4)]
    chunk_diag = [take(N, BF16) for _ in range(4)]
    staged = [take(ST_W, BF16) for _ in range(2)]
    v_staged = [take(SEQ_TILES * 32) for _ in range(2)]
    probs = [take(N) for _ in range(4)]
    W = [take(GQ * 2 * (MASK_ROWS + 1), BF16) for _ in range(SEQ_TILES)]
    cmax = [take(GQ * 64) for _ in range(2)]
    left = [take(GQ * 64) for _ in range(2)]
    top = [take(GQ * TOPK) for _ in range(2)]
    own = [take(GQ * CPT) for _ in range(2)]
    own_dropped = [take(GQ) for _ in range(2)]
    minus = [take(GQ) for _ in range(2)]
    minus_rest = [take(GQ) for _ in range(2)]
    ot = [take(P) for _ in range(2)]
    inv = [take(GQ) for _ in range(2)]
    o_staged = [take(SEQ_TILES * GQ * HD) for _ in range(2)]
    neg_one, one_row = take(GQ), take(GQ)
    key_aug = m.key_aug

    score_bank, back_bank = m.banks[0:3], m.banks[3:5]
    turn_bank, sum_bank, close_bank = m.banks[5], m.banks[6], m.banks[7]
    turn_bf = turn_bank[:, :].bitcast(BF16)

    staged_in, stored = [s(f"d_staged{p}") for p in range(2)], [s(f"d_stored{p}") for p in range(2)]
    top_turned, top_kept = s("d_top_turned"), s("d_top_kept")
    scored, reduced = s("d_scored"), s("d_reduced")
    mask_ready, minus_ready = s("d_mask"), s("d_minus")
    mask_turned, mask_kept = s("d_mask_turned"), s("d_mask_kept")
    masked_scored, probs_ready, summed = s("d_masked_scored"), s("d_probs"), s("d_summed")
    ot_ready, closed_turned, closed = s("d_ot"), s("d_closed_turned"), s("d_closed")
    w_blank, top_ready, own_ready, diag_ready = s("d_w_blank"), s("d_top"), s("d_own"), s("d_diag")
    dve_seq, pool_seq = Count(s("d_dve_seq")), Count(s("d_pool_seq"))

    halves = [1 if (i + 1) * P <= 512 else 2 for i in range(SEQ_TILES)]
    score_at = [GQ * sum(halves[:i]) for i in range(SEQ_TILES + 1)]
    back_at = [i * (i + 1) // 2 for i in range(SEQ_TILES + 1)]
    SC, BK, TT = score_at[-1], back_at[-1], SEQ_TILES + 2
    assert SC % 3 == 0 and BK % 4 == 0
    PAIR = 2 * SEQ_TILES

    class Step:

        def __init__(self, t, k):
            self.g, self.i, self.k, self.p = t * 2 + k // SEQ_TILES, k % SEQ_TILES, k, k // SEQ_TILES % 2
            self.n, self.q = t * PAIR + k, t + k // PAIR
            self.exists = not isinstance(t, int) or 0 <= t * PAIR + k < GROUPS * SEQ_TILES
            self.slot = k % 4
            self.two = self.i >= 4

    def over_steps(eng, body, seq=None, per=0):
        for k in range(3):
            body(0, k)
        if seq:
            seq.settle()
        with eng.Fori(0, GROUPS // 2 - 1) as t:
            if seq:
                seq.enter(t, per)
            for k in range(3, PAIR + 3):
                body(t, k)
        if seq:
            seq.leave(GROUPS // 2 - 1)
        for k in range(3, PAIR + 3):
            body(GROUPS // 2 - 1, k)

    with nc.Block() as block:
        @block.sync
        def _(sp):
            def load(g, p):
                sp.dma_start(staged[p], dram["rows"][ds(g, 1)].squeeze(0)).then_inc(staged_in[p], 16)
                sp.dma_start(v_staged[p], m.arena[:, ds(g * (SEQ_TILES * 32) + V_AT, SEQ_TILES * 32)]).then_inc(staged_in[p], 16)

            def store(g, p):
                sp.wait_ge(closed, g * SEQ_TILES + SEQ_TILES)
                sp.dma_start(m.arena[:, ds(g * (SEQ_TILES * GQ * HD) + O_AT, SEQ_TILES * GQ * HD)], o_staged[p]).then_inc(stored[p], 16)

            load(0, 0)
            load(1, 1)
            load_last_weights(sp, m, dram)
            with sp.Fori(0, GROUPS // 2 - 1) as t:
                for p in range(2):
                    sp.wait_ge(summed, t * 2 * BK + ((p + 1) * BK + 4))
                    load(t * 2 + (2 + p), p)
                    store(t * 2 + p, p)
            for p in range(2):
                store(GROUPS - 2 + p, p)
            for p in range(2):
                sp.wait_ge(stored[p], 16 * (GROUPS // 2 + 1))

        @block.tensor
        def _(pe):
            def turn_q(st):
                pe.wait_ge(top_kept, st.g * TT + (2 + st.i))
                if st.i == 0:
                    pe.wait_ge(staged_in[st.p], st.q * 32 + 32)
                for h in range(GQ):
                    at = st.i * ST_TILE + h * ROWS
                    last = pe.transpose(turn_bf[0:ROWS, h * P:(h + 1) * P], staged[st.p][:, at:at + ROWS], m.ident_bf)
                last.then_inc(top_turned, 1)

            def turn_k(g, p, q, half, first):
                if not first:
                    pe.wait_ge(top_kept, g * TT + half)
                if half == 0:
                    pe.wait_ge(staged_in[p], q * 32 + 32)
                for c in range(4):
                    at = (half * 4 + c) * ST_TILE + GQ * ROWS
                    last = pe.transpose(turn_bf[0:ROWS, c * P:(c + 1) * P], staged[p][:, at:at + ROWS], m.ident_bf)
                last.then_inc(top_turned, 1)

            def turn_mask(st):
                if not (isinstance(st.n, int) and st.n == 0):
                    pe.wait_ge(mask_kept, st.n)
                pe.wait_ge(minus_ready, st.n + 1)
                pe.wait_ge(mask_ready, st.n + 1)
                w = W[st.i].rearrange("p (h f r) -> p h f r", h=GQ, f=2)
                for h in range(GQ):
                    for f in range(1 + st.two):
                        last = pe.transpose(turn_bf[ROWS:KROWS, f * N + h * P:f * N + (h + 1) * P],
                                            w[:, h, f, 0:MASK_ROWS], m.ident_bf)
                last.then_inc(mask_turned, 1)

            def score(st, h, half):
                u = score_at[st.i] + h * halves[st.i] + half
                k0, k1 = half * 512, min((st.i + 1) * P, (half + 1) * 512)
                bank = score_bank[u % 3]
                diagonal = k1 == (st.i + 1) * P
                if h == 0 and half == 0:
                    pe.wait_ge(top_kept, st.g * TT + (3 + st.i))
                pe.wait_ge(reduced, st.g * SC + (u + 1))
                last = pe.matmul(bank[:, 0:k1 - k0], query_aug[st.slot][0:ROWS, h * P:(h + 1) * P], key_aug[st.p][0:ROWS, k0:k1],
                                 start=True, stop=not diagonal)
                if diagonal:
                    last = pe.matmul(bank[:, k1 - k0 - P:k1 - k0], m.ident_bf, m.causal, start=False, stop=True)
                last.then_inc(scored, 1)

            def masked_score(st, j):
                u = back_at[st.i] + j
                bank = back_bank[u % 2]
                if j == 0:
                    pe.wait_ge(mask_kept, st.n + 1)
                pe.wait_ge(probs_ready, st.g * BK + (u + 1))
                f = int(st.two and j >= 4)
                extra = j == st.i or (j == st.i - 1 and st.i >= 2)
                last = pe.matmul(bank[:, :], key_aug[st.p][0:KROWS, j * P:(j + 1) * P], query_aug[st.slot][0:KROWS, f * N:(f + 1) * N],
                                 start=True, stop=not extra)
                if j == st.i:
                    last = pe.matmul(bank[:, :], m.causal, m.ident4, start=False, stop=True)
                elif extra:
                    pe.wait_ge(diag_ready, st.g * (SEQ_TILES - 2) + (st.i - 1))
                    last = pe.matmul(bank[:, :], m.own_chunk, chunk_diag[st.slot], start=False, stop=True)
                last.then_inc(masked_scored, 1)

            def weigh(st, j):
                u = back_at[st.i] + j
                if j == 0:
                    pe.wait_ge(ot_ready, st.n + 1)
                pe.wait_ge(probs_ready, st.g * BK + (u + 3))
                for h in range(GQ):
                    last = pe.matmul(sum_bank[32 * h:32 * h + 32, 0:P], v_staged[st.p][:, j * 32:(j + 1) * 32],
                                     probs[u % 4][:, h * P:(h + 1) * P], start=j == 0, stop=j == st.i, tile_position=(0, 32 * h))
                last.then_inc(summed, 1)

            def close(st):
                pe.wait_ge(ot_ready, st.n + 2)
                pe.wait_ge(closed, st.n) if not (isinstance(st.n, int) and st.n == 0) else None
                pe.transpose(close_bank[:, 0:P], ot[st.k % 2], m.ident).then_inc(closed_turned, 1)

            def body(t, k):
                front, mid, back, end = (Step(t, k - n) for n in range(4))
                after = Step(t, k + 1)
                if after.exists:
                    turn_q(after)
                if end.exists:
                    close(end)
                fronts = [(score, front, h, half) for h in range(GQ) for half in range(halves[front.i])] if front.exists else []
                backs = []
                if back.exists:
                    for j in range(back.i + 1):
                        backs.append((masked_score, back, j))
                        if j >= 1:
                            backs.append((weigh, back, j - 1))
                    backs.append((weigh, back, back.i))
                total = max(len(fronts), len(backs), 1)
                turned = not mid.exists
                for n in range(total):
                    for f in fronts[n * len(fronts) // total:(n + 1) * len(fronts) // total]:
                        f[0](*f[1:])
                    for f in backs[n * len(backs) // total:(n + 1) * len(backs) // total]:
                        f[0](*f[1:])
                    if not turned and n >= total * 2 // 3:
                        turn_mask(mid)
                        turned = True
                if not turned:
                    turn_mask(mid)
                if front.exists and front.i == 6 and Step(t, k + 2).exists:
                    for half in range(2):
                        turn_k(front.g + 1, 1 - front.p, Step(t, k + 2).q, half, False)

            turn_k(0, 0, 0, 0, True)
            turn_k(0, 0, 0, 1, False)
            turn_q(Step(0, 0))
            over_steps(pe, body)

        @block.scalar
        def _(act):
            act.sem_inc(probs_ready, 2)
            act.sem_inc(ot_ready, 1)
            act.sem_inc(closed_turned, 2)

            def keep_k(g, p, half):
                act.wait_ge(top_turned, g * TT + (half + 1))
                act.activation(key_aug[p][0:ROWS, half * 512:(half + 1) * 512], turn_bf[0:ROWS, 0:N], ACT.Copy).then_inc(top_kept, 1)

            def keep_q(st):
                act.wait_ge(top_turned, st.g * TT + (3 + st.i))
                if st.two:
                    act.activation(query_aug[st.slot][0:ROWS, N:2 * N], turn_bf[0:ROWS, 0:N], ACT.Copy)
                act.activation(query_aug[st.slot][0:ROWS, 0:N], turn_bf[0:ROWS, 0:N], ACT.Copy).then_inc(top_kept, 1)

            def keep_mask(st):
                act.wait_ge(mask_turned, st.n + 1)
                n = (1 + st.two) * N
                act.activation(query_aug[st.slot][ROWS:KROWS, 0:n], turn_bf[ROWS:KROWS, 0:n], ACT.Copy).then_inc(mask_kept, 1)

            def exponent(st, j):
                u = back_at[st.i] + j
                act.wait_ge(masked_scored, st.g * BK + (u + 1))
                act.wait_ge(summed, st.g * BK + (u + 1))
                act.activation(probs[u % 4], back_bank[u % 2][:, :], ACT.Exp, scale=float(HD) ** -0.5).then_inc(probs_ready, 1)

            def keep_sums(st):
                act.wait_ge(summed, st.g * BK + (back_at[st.i + 1] + 4))
                act.wait_ge(closed_turned, st.n + 1)
                act.activation(ot[st.k % 2], sum_bank[:, 0:P], ACT.Copy).then_inc(ot_ready, 1)

            def body(t, k):
                front, mid, back, end = (Step(t, k - n) for n in range(4))
                after = Step(t, k + 1)
                if end.exists:
                    keep_sums(end)
                n = back.i + 1 if back.exists else 0
                first = min(n, 1)
                for j in range(first):
                    exponent(back, j)
                if after.exists:
                    keep_q(after)
                cut = max(first, n * 2 // 3 + 1)
                for j in range(first, min(cut, n)):
                    exponent(back, j)
                if mid.exists:
                    keep_mask(mid)
                for j in range(min(cut, n), n):
                    exponent(back, j)
                if front.exists and front.i == 6 and Step(t, k + 2).exists:
                    for half in range(2):
                        keep_k(front.g + 1, 1 - front.p, half)

            for half in range(2):
                keep_k(0, 0, half)
            keep_q(Step(0, 0))
            over_steps(act, body)

        @block.vector
        def _(dve):
            dve.sem_inc(reduced, 3)

            def body(t, k):
                front, end = Step(t, k), Step(t, k - 3)
                p = front.k % 2

                def finish():
                    e = end.k % 2
                    dve.wait_ge(closed_turned, end.n + 3)
                    x = close_bank[:, 0:P].rearrange("p (h c) -> p h c", h=GQ)
                    dve_seq.mark(dve.reciprocal(inv[e].unsqueeze(2), x[:, :, HD:HD + 1]))
                    if end.i == 0:
                        dve.wait_ge(stored[end.p], end.q * 16 + 16)
                    dve_seq.wait(dve)
                    dve.tensor_tensor(out=o_staged[end.p][:, end.i * GQ * HD:(end.i + 1) * GQ * HD].rearrange("p (h d) -> p h d", h=GQ),
                                      in0=x[:, :, 0:HD], in1=inv[e].unsqueeze(2).to_broadcast([P, GQ, HD]),
                                      op=ALU.mult).then_inc(closed, 1)

                if end.exists:
                    finish()
                if not front.exists:
                    return
                i = front.i
                n = (i + 1) * CPT
                cm, lf, tp = cmax[p], left[p], top[p]
                if not (isinstance(front.n, int) and front.n < 2):
                    dve.wait_ge(minus_ready, front.n - 1)
                chunks = lambda x, h: x[:, h * 64:h * 64 + n]

                def reduce(h):
                    for half in range(halves[i]):
                        u = score_at[i] + h * halves[i] + half
                        k0, k1 = half * 512, min((i + 1) * P, (half + 1) * 512)
                        dve.wait_ge(scored, front.g * SC + (u + 1))
                        dve.tensor_reduce(out=cm[:, h * 64 + k0 // CHUNK:h * 64 + k1 // CHUNK],
                                          in_=score_bank[u % 3][:, 0:k1 - k0].rearrange("p (c d) -> p c d", d=CHUNK),
                                          axis=AXX, op=ALU.max).then_inc(reduced, 1)

                def best(h):
                    dve.wait_ge(reduced, front.g * SC + (score_at[i] + (h + 1) * halves[i] + 3))
                    dve.sem_inc(m.turnstile, 1)
                    dve_seq.mark(dve.max(out=tp[:, h * TOPK:(h + 1) * TOPK], in_=chunks(cm, h)))

                def drop(h):
                    dve_seq.mark(dve.match_replace(out=chunks(lf, h), in_to_replace=tp[:, h * TOPK:(h + 1) * TOPK],
                                                   in_values=chunks(cm, h), imm_value=TAKEN))
                for h in range(GQ):
                    reduce(h)
                    if h >= 1:
                        best(h - 1)
                best(GQ - 1)
                dve_seq.wait(dve)
                dve.sem_inc(top_ready, 1)
                if i < 2:
                    dve.sem_inc(mask_ready, 1)
                    return
                for h in range(GQ):
                    drop(h)
                dve_seq.wait(dve)
                w = W[i].rearrange("p (h f r) -> p h f r", h=GQ, f=2)
                lh = lf.rearrange("p (h c) -> p h c", h=GQ)
                near = lh[:, :, (i - 1) * CPT:i * CPT]
                wide = lambda c: c.unsqueeze(1).to_broadcast([P, GQ, CPT])
                own3 = own[p].rearrange("p (h c) -> p h c", h=GQ)
                dve_seq.mark(dve.scalar_tensor_tensor(out=own3, in0=near, scalar=1e38, in1=wide(m.chunk_own),
                                                      op0=ALU.is_lt, op1=ALU.mult))
                f, c = ((i - 1) - 1) // 3, ((i - 1) - 1) % 3 * CPT
                if i >= 3:
                    a = min(i - 2, 3) * CPT
                    dve.tensor_scalar(out=w[:, :, 0, 0:a], in0=lh[:, :, CPT:CPT + a], scalar1=1e38, scalar2=NEG,
                                      op0=ALU.is_lt, op1=ALU.mult)
                if i >= 6:
                    a = (i - 5) * CPT
                    dve.tensor_scalar(out=w[:, :, 1, 0:a], in0=lh[:, :, 4 * CPT:4 * CPT + a], scalar1=1e38, scalar2=NEG,
                                      op0=ALU.is_lt, op1=ALU.mult)
                dve_seq.wait(dve)
                dve.wait_ge(minus_ready, front.n)
                dve.tensor_reduce(out=own_dropped[p].unsqueeze(2), in_=own3, axis=AXX, op=ALU.add).then_inc(own_ready, 1)
                dve.scalar_tensor_tensor(out=w[:, :, f, c:c + CPT], in0=near, scalar=1e38, in1=wide(m.chunk_before),
                                         op0=ALU.is_lt, op1=ALU.mult).then_inc(mask_ready, 1)

            over_steps(dve, body, dve_seq, PAIR * (1 + GQ) + 2 * (SEQ_TILES - 2) * (GQ + 1))

        @block.gpsimd
        def _(pool):
            for i in range(SEQ_TILES):
                pool.memset(W[i], 0.0)
            pool.memset(one_row, 1.0)
            pool.memset(neg_one, -1.0).then_inc(w_blank, 1)
            pool.sem_inc(summed, 4)
            for p in range(2):
                pool.sem_inc(stored[p], 16)
            pool.wait_ge(w_blank, 1)

            def body(t, k):
                st = Step(t, k)
                if not st.exists:
                    return
                p = st.k % 2
                pool.wait_ge(top_ready, st.n + 1)
                w = W[st.i].rearrange("p (h f r) -> p h f r", h=GQ, f=2)
                tp = top[p].rearrange("p (h c) -> p h c", h=GQ)
                c = 3 * CPT
                both = lambda x: x.unsqueeze(2).unsqueeze(3).to_broadcast([P, GQ, 2, 1])
                slot = lambda n: w[:, :, :, c + n:c + n + 1]
                one = lambda n: w[:, :, 0, c + n:c + n + 1]
                mi, re = minus[p].unsqueeze(2), minus_rest[p].unsqueeze(2)
                minus1 = neg_one.unsqueeze(2)
                pool_seq.mark(pool.tensor_tensor(out=mi, in0=tp[:, :, 0:1], in1=minus1, op=ALU.mult))
                pool_seq.mark(pool.tensor_tensor(out=slot(0), in0=both(tp[:, :, 0]), in1=both(neg_one), op=ALU.mult))
                pool_seq.wait(pool)
                pool_seq.mark(pool.tensor_tensor(out=re, in0=mi, in1=one(0), op=ALU.subtract))
                pool_seq.wait(pool)
                pool_seq.mark(pool.tensor_tensor(out=slot(1), in0=both(minus_rest[p]), in1=both(one_row), op=ALU.mult))
                pool_seq.wait(pool)
                pool.tensor_tensor(out=slot(2), in0=both(minus_rest[p]), in1=w[:, :, :, c + 1:c + 2], op=ALU.subtract).then_inc(minus_ready, 1)
                if st.i >= 2:
                    pool.wait_ge(own_ready, st.g * (SEQ_TILES - 2) + (st.i - 1))
                    pool.sem_inc(m.turnstile, 1)
                    for h in range(GQ):
                        last = pool.tensor_scalar(out=chunk_diag[st.slot][:, h * P:(h + 1) * P], in0=m.ident_bf,
                                                  scalar1=own_dropped[p][:, h:h + 1], scalar2=NEG, op0=ALU.mult, op1=ALU.mult)
                    last.then_inc(diag_ready, 1)

            over_steps(pool, body, pool_seq, PAIR * 4)


def load_last_weights(sp, m, dram):
    kq = "p (c d) -> p c d"
    sp.dma_start(m.f32(WO_AT, DC * D).rearrange(kq, c=DC), dram["wo"].rearrange("(c p) d -> p c d", p=P)).then_inc(m.last_in, 16)
    sp.dma_start(m.f32(LA_AT, D), dram["lora_A"].rearrange("h r d -> (h r) d")).then_inc(m.last_in, 16)
    sp.dma_start(m.f32(WR_AT, D)[0:LORA_H, :], dram["Wr"]).then_inc(m.last_in, 16)
    sp.dma_start(m.f32(BR_AT, LORA_H)[0:1, :], dram["br"].rearrange("(a h) -> a h", a=1)).then_inc(m.last_in, 16)
    for oc in range(DC):
        sp.dma_start(m.f32(LB_AT + oc * P, P).rearrange("p (h r) -> p h r", h=LORA_H),
                     dram["lora_B"][:, oc * P:(oc + 1) * P, :].rearrange("h o r -> o h r")).then_inc(m.last_in, 16)


LAST_LOADS = 4 + DC
WO_AT = 37000
LA_AT, WR_AT, LB_AT, BR_AT = WO_AT + DC * D, WO_AT + (DC + 1) * D, WO_AT + (DC + 2) * D, WO_AT + (DC + 3) * D
WOT_AT = BR_AT + 16
LOW_N = LORA_H * LORA_R + LORA_H
LOWW_AT = WOT_AT + DC * D
LBT_AT = LOWW_AT + DC * LOW_N
LWORK = LBT_AT + D


def output(nc, m, s, dram):
    woT = m.f32(WOT_AT, DC * D)
    low_w = m.f32(LOWW_AT, DC * LOW_N).rearrange("p (c n) -> p c n", c=DC)
    take = m.taker(LWORK, ARENA)
    o_tile, oT = [take(D) for _ in range(2)], [take(D) for _ in range(2)]
    o_all = m.f32(O_AT, GROUPS * SEQ_TILES * GQ * HD).rearrange("p (b k t c) -> p b k t c", b=BATCH, k=KV, t=SEQ_TILES)
    w_turned, w_placed = s("e_w_turned"), s("e_w_placed")
    gathered, turned, oT_ready, y_ready = [s(f"e_gathered{b}") for b in range(2)], s("e_turned"), s("e_oT"), s("e_y")
    stats_ready, branch_rstd_ready, added = s("e_stats"), s("e_branch_rstd"), s("e_added")
    dve_seq, pool_seq = Count(s("e_dve_seq")), Count(s("e_pool_seq"))
    n_weights = DC + 3

    with nc.Block() as block:
        @block.sync
        def _(sp):
            with sp.Fori(0, SEQ_TILES) as i:
                for b in range(2):
                    sp.wait_ge(turned, i * 2 + b + 1)
                    sp.dma_start(o_tile[b].rearrange("p (k c) -> p k c", k=KV),
                                 o_all[:, b, :, ds(i, 1), :].squeeze(2)).then_inc(gathered[b], 16)

        @block.tensor
        def _(pe):
            def turn(i, b):
                pe.wait_ge(gathered[b], i * 16 + 16)
                for dc in range(DC):
                    last = pe.transpose(m.banks[b][:, dc * P:(dc + 1) * P], o_tile[b][:, dc * P:(dc + 1) * P], m.ident)
                last.then_inc(turned, 1)

            def feed(k, b):
                pe.wait_ge(oT_ready, k + 1)
                pe.wait_ge(added, k + 1)
                for dc in range(DC):
                    last = pe.matmul(m.banks[2 + b][:, :], oT[b][:, dc * P:(dc + 1) * P], woT[:, dc * D:(dc + 1) * D],
                                     start=dc == 0, stop=dc == DC - 1)
                last.then_inc(y_ready, 1)

            pe.wait_ge(m.last_in, 16 * LAST_LOADS)
            for c in range(n_weights):
                bank = m.banks[4 + c % 4]
                if c >= 4:
                    pe.wait_ge(w_placed, c - 3)
                for dc in range(DC):
                    if c < DC:
                        last = pe.transpose(bank[:, dc * P:(dc + 1) * P], m.f32(WO_AT + c * D + dc * P, P), m.ident)
                    elif c == DC:
                        last = pe.transpose(bank[:, dc * P:(dc + 1) * P], m.f32(LA_AT + dc * P, P), m.ident)
                    elif c == DC + 1:
                        last = pe.transpose(bank[:, dc * LORA_H:(dc + 1) * LORA_H], m.f32(WR_AT + dc * P, P)[0:LORA_H, :],
                                            m.ident[0:LORA_H, 0:LORA_H])
                    else:
                        last = pe.transpose(bank[:, dc * P:(dc + 1) * P], m.f32(LB_AT + dc * P, P), m.ident)
                last.then_inc(w_turned, 1)
            for b in range(2):
                turn(0, b)
            pe.wait_ge(w_placed, DC)
            with pe.Fori(0, SEQ_TILES - 1) as i:
                for b in range(2):
                    feed(i * 2 + b, b)
                for b in range(2):
                    turn(i + 1, b)
            for b in range(2):
                feed(TILES - 2 + b, b)

        @block.scalar
        def _(act):
            act.sem_inc(turned, 2)
            for c in range(n_weights):
                act.wait_ge(w_turned, c + 1)
                bank = m.banks[4 + c % 4]
                if c < DC:
                    out = woT.rearrange("p (c n) -> p c n", c=DC)[:, :, c * P:(c + 1) * P]
                    last = act.activation(out, bank.rearrange("p (c n) -> p c n", c=DC), ACT.Copy)
                elif c == DC:
                    last = act.activation(low_w[:, :, 0:P], bank.rearrange("p (c n) -> p c n", c=DC), ACT.Copy)
                elif c == DC + 1:
                    last = act.activation(low_w[:, :, P:LOW_N], bank[:, 0:DC * LORA_H].rearrange("p (c n) -> p c n", c=DC), ACT.Copy)
                else:
                    last = act.activation(m.f32(LBT_AT, D), bank[:, :], ACT.Copy)
                last.then_inc(w_placed, 1)
            with act.Fori(0, SEQ_TILES) as i:
                for b in range(2):
                    act.wait_ge(turned, i * 2 + b + 3)
                    act.activation(oT[b], m.banks[b][:, :], ACT.Copy).then_inc(oT_ready, 1)

        @block.vector
        def _(dve):
            dve.sem_inc(added, 2)
            with dve.Fori(0, SEQ_TILES) as i:
                dve_seq.enter(i, 2 * (1 + BRANCH_ADD_STEPS))
                for b in range(2):
                    dve.wait_ge(y_ready, i * 2 + b + 1)
                    branch_stats(dve, m, dve_seq, b, m.banks[2 + b][:, :]).then_inc(stats_ready, 1)
                for b in range(2):
                    dve.wait_ge(branch_rstd_ready, i * 2 + b + 1)
                    branch_add(dve, m, dve_seq, b, m.banks[2 + b][:, :], i + b * SEQ_TILES).then_inc(added, 1)
            dve_seq.leave(SEQ_TILES)

        @block.gpsimd
        def _(pool):
            with pool.Fori(0, SEQ_TILES) as i:
                pool_seq.enter(i, 2)
                for b in range(2):
                    pool.wait_ge(stats_ready, i * 2 + b + 1)
                    branch_rstd(pool, m, pool_seq, b).then_inc(branch_rstd_ready, 1)
            pool_seq.leave(SEQ_TILES)


def routed(nc, m, s, dram):
    low_w = m.f32(LOWW_AT, DC * LOW_N)
    take = m.taker(LWORK, ARENA)
    xn, xT = [take(D) for _ in range(2)], [take(D) for _ in range(2)]
    ls, lsT = [take(P) for _ in range(2)], [take(P) for _ in range(2)]
    peak, total, share = [take(1) for _ in range(2)], [take(1) for _ in range(2)], [take(1) for _ in range(2)]
    e, score = [take(LORA_H) for _ in range(2)], [take(LORA_H) for _ in range(2)]
    ones = take(P)[0:1, :]
    rstd_ready, xn_ready, turned, xT_ready = s("f_rstd"), s("f_xn"), s("f_turned"), s("f_xT")
    low_ready, peak_ready, e_ready, ls_ready = s("f_low"), s("f_peak"), s("f_e"), s("f_ls")
    ls_turned, lsT_ready, y_ready = s("f_ls_turned"), s("f_lsT"), s("f_y")
    stats_ready, branch_rstd_ready, added = s("f_stats"), s("f_branch_rstd"), s("f_added")
    stored = s("f_stored")
    dve_seq, pool_seq = Count(s("f_dve_seq")), Count(s("f_pool_seq"))
    LR = LORA_H * LORA_R
    branch_scale = float(LORA_H * 2)

    def over_pairs(eng, body, seq=None, per=0):
        with eng.Fori(0, TILES // 2 - 1) as u:
            if seq:
                seq.enter(u, per)
            body(u, False)
        if seq:
            seq.leave(TILES // 2 - 1)
        body(TILES // 2 - 1, True)

    with nc.Block() as block:
        @block.sync
        def _(sp):
            with sp.Fori(0, TILES) as k:
                sp.wait_ge(added, k + 3)
                sp.dma_start(dram["out"][ds(k * P, P), :], m.x(k)).then_inc(stored, 16)
            sp.wait_ge(stored, 16 * TILES)

        @block.tensor
        def _(pe):
            def turn(k, p):
                pe.wait_ge(xn_ready, k + 1)
                for dc in range(DC):
                    last = pe.transpose(m.banks[p][:, dc * P:(dc + 1) * P], xn[p][:, dc * P:(dc + 1) * P], m.ident)
                last.then_inc(turned, 1)

            def body(u, last_pair):
                for p in range(2):
                    pe.wait_ge(xT_ready, u * 2 + (p + 1))
                    pe.wait_ge(ls_ready, u * 2 + (p + 1))
                    for dc in range(DC):
                        pe.matmul(m.banks[2 + p][:, 0:LOW_N], xT[p][:, dc * P:(dc + 1) * P], low_w[:, dc * LOW_N:(dc + 1) * LOW_N],
                                  start=dc == 0, stop=False)
                    pe.matmul(m.banks[2 + p][:, LR:LOW_N], ones, m.f32(BR_AT, LORA_H)[0:1, :], start=False, stop=True).then_inc(low_ready, 1)
                if not last_pair:
                    for p in range(2):
                        turn(u * 2 + (2 + p), p)
                for p in range(2):
                    pe.wait_ge(ls_ready, u * 2 + (p + 3))
                    pe.transpose(m.banks[4 + p][:, 0:LR], ls[p], m.ident).then_inc(ls_turned, 1)
                for p in range(2):
                    pe.wait_ge(lsT_ready, u * 2 + (p + 1))
                    pe.wait_ge(added, u * 2 + (p + 1))
                    pe.matmul(m.banks[6 + p][:, :], lsT[p], m.f32(LBT_AT, D), start=True, stop=True).then_inc(y_ready, 1)

            for p in range(2):
                turn(p, p)
            over_pairs(pe, body)

        @block.scalar
        def _(act):
            def normed(k, p):
                act.activation(xn[p], m.x(k), ACT.Identity, bias=m.shift[:, ds(k, 1)],
                               scale=m.rstd[:, ds(k, 1)]).then_inc(xn_ready, 1)

            def keep(k, p):
                act.wait_ge(turned, k + 1)
                act.activation(xT[p], m.banks[p][:, :], ACT.Copy).then_inc(xT_ready, 1)

            def body(u, last_pair):
                if not last_pair:
                    for p in range(2):
                        normed(u * 2 + (2 + p), p)
                for p in range(2):
                    act.wait_ge(peak_ready, u * 2 + (p + 1))
                    act.activation(e[p], m.banks[2 + p][:, LR:LOW_N], ACT.Exp, bias=peak[p], accum_out=total[p]).then_inc(e_ready, 1)
                if not last_pair:
                    for p in range(2):
                        keep(u * 2 + (2 + p), p)
                for p in range(2):
                    act.wait_ge(ls_turned, u * 2 + (p + 1))
                    act.activation(lsT[p], m.banks[4 + p][:, 0:LR], ACT.Copy).then_inc(lsT_ready, 1)

            act.wait_ge(rstd_ready, 1)
            for p in range(2):
                normed(p, p)
            for p in range(2):
                keep(p, p)
            over_pairs(act, body)

        @block.vector
        def _(dve):
            dve.sem_inc(added, 2)
            dve.sem_inc(ls_ready, 2)

            def body(u, _):
                for p in range(2):
                    dve.wait_ge(low_ready, u * 2 + (p + 1))
                    dve.tensor_reduce(out=peak[p], in_=m.banks[2 + p][:, LR:LOW_N], axis=AXX, op=ALU.max, negate=True).then_inc(peak_ready, 1)
                for p in range(2):
                    dve.wait_ge(e_ready, u * 2 + (p + 1))
                    dve_seq.mark(dve.reciprocal(share[p], total[p]))
                    dve_seq.wait(dve)
                    dve_seq.mark(dve.tensor_scalar(out=score[p], in0=e[p], scalar1=share[p], scalar2=branch_scale, op0=ALU.mult, op1=ALU.mult))
                    dve_seq.wait(dve)
                    dve.tensor_tensor(out=ls[p].rearrange("p (h r) -> p h r", h=LORA_H), in0=m.banks[2 + p][:, 0:LR].rearrange("p (h r) -> p h r", h=LORA_H),
                                      in1=score[p].unsqueeze(2).to_broadcast([P, LORA_H, LORA_R]), op=ALU.mult).then_inc(ls_ready, 1)
                for p in range(2):
                    dve.wait_ge(y_ready, u * 2 + (p + 1))
                    branch_stats(dve, m, dve_seq, p, m.banks[6 + p][:, :]).then_inc(stats_ready, 1)
                for p in range(2):
                    dve.wait_ge(branch_rstd_ready, u * 2 + (p + 1))
                    branch_add(dve, m, dve_seq, p, m.banks[6 + p][:, :], u * 2 + p, last=True).then_inc(added, 1)
            over_pairs(dve, body, dve_seq, 2 * 5)

        @block.gpsimd
        def _(pool):
            pool.memset(ones, 1.0)
            rstd_all(pool, m, pool_seq).then_inc(rstd_ready, 1)
            pool_seq.settle()

            def body(u, _):
                for p in range(2):
                    pool.wait_ge(stats_ready, u * 2 + (p + 1))
                    branch_rstd(pool, m, pool_seq, p).then_inc(branch_rstd_ready, 1)
            over_pairs(pool, body, pool_seq, 2)




def program(nc, dram, phases=99):
    with ExitStack() as ctx:
        m = Mem(nc, ctx)
        stages = [setup_and_sparse, weights, gated, project, attention, output, routed]
        for stage in stages[:phases]:
            stage(nc, m, m.sem, dram)


def shape_constants():
    c = np.zeros((P, 6 * P), np.float32)
    row, col = np.arange(P)[:, None], np.arange(P)[None, :]
    c[:, 0:P] = row == col
    c[:, P:2 * P] = np.where(col > row, np.float32(NEG), np.float32(0))
    c[:, 2 * P:3 * P] = (row // CHUNK == col // CHUNK) & (col <= row)
    inv = np.float32(1.0) / np.float32(10000.0) ** (np.arange(0, HD, 2, dtype=np.float32) / np.float32(HD))
    freq = np.arange(SEQ, dtype=np.float32)[:, None] * inv[None, :].astype(np.float32)
    emb = np.concatenate([freq, freq], 1).astype(np.float32)
    sin = np.sin(emb).astype(np.float32)
    sin[:, :HD // 2] *= -1
    lay = lambda t: t.reshape(SEQ_TILES, P, HD).transpose(1, 0, 2).reshape(P, SEQ_TILES * HD)
    c[:, 3 * P:4 * P] = lay(np.cos(emb).astype(np.float32))
    c[:, 4 * P:5 * P] = lay(sin)
    ch = np.arange(CPT)[None, :]
    c[:, 5 * P:5 * P + CPT] = np.where(ch < row // CHUNK, np.float32(NEG), np.float32(0))
    c[:, 5 * P + CPT:5 * P + 2 * CPT] = ch == row // CHUNK
    k = np.zeros((MASK_ROWS, SEQ), np.float32)
    for j in range(1, SEQ_TILES - 1):
        for ch in range(CPT):
            k[(j - 1) % 3 * CPT + ch, j * P + ch * CHUNK:j * P + (ch + 1) * CHUNK] = 1
    k[3 * CPT:, :] = 1
    return c, k


_NAMES = {"x": "L0_attn_x", "w1": "L0_attn_w1", "w2": "L0_attn_w2", "b2": "L0_attn_b2", "mask": "L0_attn_sparse_mask",
          "gate_q": "L0_ffn_gate_q", "gate_scale": "L0_ffn_gate_scale", "gate_A": "L0_ffn_gate_A", "gate_B": "L0_ffn_gate_B",
          "up_q": "L0_ffn_up_q", "up_scale": "L0_ffn_up_scale", "up_A": "L0_ffn_up_A", "up_B": "L0_ffn_up_B",
          "down_q": "L0_ffn_down_q", "down_scale": "L0_ffn_down_scale", "down_A": "L0_ffn_down_A", "down_B": "L0_ffn_down_B",
          "wq": "L1_attn_wq", "wk": "L1_attn_wk", "wv": "L1_attn_wv", "wo": "L1_attn_wo",
          "lora_A": "L1_ffn_A", "lora_B": "L1_ffn_B", "Wr": "L1_ffn_Wr", "br": "L1_ffn_br"}


def kernel(**inputs):
    import concourse.bacc as bacc
    from concourse.bass_utils import run_bass_kernel_spmd

    nc = bacc.Bacc("TRN2", target_bir_lowering=False, num_devices=1)
    consts, key_rows = shape_constants()
    arrays = {"consts": consts, "key_rows": key_rows}
    arrays |= {short: np.ascontiguousarray(inputs[name]) for short, name in _NAMES.items()}
    arrays["x"] = arrays["x"].reshape(BATCH * SEQ, D)
    dram = {n: nc.dram_tensor(f"in_{n}", a.shape, mybir.dt.from_np(a.dtype), kind="ExternalInput").ap()
            for n, a in arrays.items()}
    dram["rows"] = nc.dram_tensor("qk_rows", (GROUPS, P, ST_W), BF16).ap()
    dram["out"] = nc.dram_tensor("out", (BATCH * SEQ, D), F32, kind="ExternalOutput").ap()
    program(nc, dram)
    r = run_bass_kernel_spmd(nc, [{f"in_{n}": a for n, a in arrays.items()}], core_ids=[0])
    return r.results[0]["out"].reshape(BATCH, SEQ, D)
```

```python
from contextlib import ExitStack

import numpy as np

import concourse.bass as bass
from concourse import mybir

F32 = mybir.dt.float32
BF16 = mybir.dt.bfloat16
I32 = mybir.dt.int32
ALU = mybir.AluOpType
ACT = mybir.ActivationFunctionType
AXX = mybir.AxisListType.X
ds = bass.ds

P = 128
BATCH, SEQ, D = 2, 1024, 512
TILES = BATCH * SEQ // P
SEQ_TILES = SEQ // P
DC = D // P
INNER = 1376
IT = (INNER + P - 1) // P
I_LAST = INNER - (IT - 1) * P
RANK = 32
Q_ZERO, Q_STEP, LR_SCALE = 7.5, 0.005, 0.02
HEADS, KV, HD = 32, 8, 16
GQ = HEADS // KV
CHUNK = 16
CPT = P // CHUNK
TOPK = 8
PARTS = 3
ROWS = 6 * HD
LORA_H, LORA_R = 8, 16
EPS = 1e-5
NEG = -float(2.0 ** 100)
TAKEN = 3e38
QK = (HEADS + KV) * HD
QKV = QK + KV * HD
GROUPS = BATCH * KV
ST_TILE = (GQ + 1) * ROWS
ST_W = SEQ_TILES * ST_TILE
MASK_ROWS = 3 * CPT + PARTS
KROWS = ROWS + MASK_ROWS

X_AT = 0
CONST_AT = X_AT + TILES * D
REG = CONST_AT + 1152
SLOT = IT * D
UPQ_AT, DOWNQ_AT, GATEQ_AT, WG_AT = REG, REG + SLOT, REG + 2 * SLOT, REG + 3 * SLOT
WD_AT, HT_AT, WU_AT = UPQ_AT, DOWNQ_AT, GATEQ_AT
ATTN0_AT = WG_AT + DC * INNER
WQKV_AT = ATTN0_AT + DC * D
WORK = WQKV_AT + DC * QKV
V_AT = REG
O_AT = V_AT + GROUPS * SEQ_TILES * 32
CWORK = O_AT + GROUPS * SEQ_TILES * GQ * HD
ARENA = 53100


class Count:

    def __init__(self, sem):
        self.sem, self.total, self.base, self.n = sem, 0, 0, 0

    def enter(self, i, per):
        self.base, self.n, self.per = i * per + self.total, 0, per

    def leave(self, turns):
        assert self.n == self.per, (self.n, self.per)
        self.total += turns * self.per
        self.base, self.n = self.total, 0

    def settle(self):
        self.total, self.base, self.n = self.base + self.n, self.base + self.n, 0

    def mark(self, ins):
        ins.then_inc(self.sem, 1)
        self.n += 1

    def wait(self, eng):
        eng.wait_ge(self.sem, self.base + self.n)

    def wait_apart(self, eng, turnstile):
        self.wait(eng)
        eng.sem_inc(turnstile, 1)


class Mem:

    def __init__(self, nc, ctx):
        self.nc, self.ctx = nc, ctx
        self.arena = ctx.enter_context(nc.sbuf_tensor("arena", [P, ARENA], F32))
        self.banks = [ctx.enter_context(nc.psum_tensor(f"bank{i}", [P, 512], F32)) for i in range(8)]
        self.turnstile, self.last_in = self.sem("turnstile"), self.sem("last_in")
        c = CONST_AT
        self.ident = self.f32(c, P); c += P
        self.causal = self.bf16(c, P); c += P // 2
        self.own_chunk = self.bf16(c, P); c += P // 2
        self.ident_bf = self.bf16(c, P); c += P // 2
        self.ident4 = self.bf16(c, 4 * P); c += 2 * P
        self.chunk_before = self.f32(c, CPT); c += CPT
        self.chunk_own = self.f32(c, CPT); c += CPT
        self.cos = self.f32(c, SEQ_TILES * HD); c += SEQ_TILES * HD
        self.sin = self.f32(c, SEQ_TILES * HD); c += SEQ_TILES * HD
        self.eps = self.f32(c, TILES); c += TILES
        self.half = self.f32(c, TILES); c += TILES
        self.mv_next = self.f32(c, 2 * TILES); c += 2 * TILES
        self.rstd = self.f32(c, TILES); c += TILES
        self.shift = self.f32(c, TILES); c += TILES
        self.scales = self.f32(c, 2 * IT + DC); c += 2 * IT + DC
        self.zero16 = self.f32(c, TILES); c += TILES
        self.ve16 = self.f32(c, TILES); c += TILES
        self.stats = [self.f32(c + 6 * i, 6) for i in range(2)]; c += 12
        self.mv = [self.f32(c + 2 * i, 2) for i in range(2)]; c += 4
        self.ve = [self.f32(c + i, 1) for i in range(2)]; c += 2
        self.rs = [self.f32(c + i, 1) for i in range(2)]; c += 2
        self.ms = [self.f32(c + i, 1) for i in range(2)]; c += 2
        self.stats_x = [self.f32(c + 6 * i, 6) for i in range(2)]; c += 12
        self.mv_x = [self.f32(c + 2 * i, 2) for i in range(2)]; c += 4
        assert c <= REG, c - CONST_AT
        self.key_aug = [self.bf16(ARENA - (2 - i) * SEQ // 2, SEQ) for i in range(2)]

    def f32(self, at, n):
        return self.arena[:, at:at + n]

    def bf16(self, at, n):
        return self.arena[:, at:at + (n + 1) // 2].bitcast(BF16)[:, 0:n]

    def i32(self, at, n):
        return self.arena[:, at:at + n].bitcast(I32)

    def x(self, tile):
        return self.arena[:, ds(tile * D + X_AT, D)]

    def taker(self, at, limit):
        place = [at]

        def take(n, dtype=F32):
            words = n if dtype == F32 else (n + 1) // 2
            view = self.f32(place[0], n) if dtype == F32 else self.bf16(place[0], n)
            place[0] += words
            assert place[0] <= limit, place[0]
            return view
        return take

    def sem(self, name):
        return self.ctx.enter_context(self.nc.semaphore(name))


def rstd_all(pool, m, seq):
    mv = m.mv_next.rearrange("p (t s) -> p t s", s=2)
    seq.mark(pool.tensor_tensor(out=m.rstd, in0=mv[:, :, 1], in1=m.eps, op=ALU.add))
    seq.wait(pool)
    seq.mark(pool.tensor_tensor(out=m.shift, in0=m.rstd, in1=m.half, op=ALU.pow))
    seq.wait(pool)
    seq.mark(pool.tensor_copy(m.rstd, m.shift))
    seq.wait(pool)
    seq.mark(pool.tensor_tensor(out=m.ve16, in0=mv[:, :, 0], in1=m.rstd, op=ALU.mult))
    seq.wait(pool)
    return pool.tensor_tensor(out=m.shift, in0=m.zero16, in1=m.ve16, op=ALU.subtract)


def branch_stats(dve, m, seq, p, y):
    seq.mark(dve.bn_stats(out=m.stats[p], in_=y))
    seq.wait_apart(dve, m.turnstile)
    return dve.bn_aggr(out=m.mv[p], in_=m.stats[p])


def branch_rstd(pool, m, seq, p):
    seq.mark(pool.tensor_tensor(out=m.ve[p], in0=m.mv[p][:, 1:2], in1=m.eps[:, 0:1], op=ALU.add))
    seq.wait(pool)
    return pool.tensor_tensor(out=m.rs[p], in0=m.ve[p], in1=m.half[:, 0:1], op=ALU.pow)


def branch_add(dve, m, seq, p, y, tile, last=False):
    x = m.x(tile)
    seq.mark(dve.scalar_tensor_tensor(out=m.ms[p], in0=m.mv[p][:, 0:1], scalar=-1.0, in1=m.rs[p],
                                      op0=ALU.mult, op1=ALU.mult))
    seq.mark(dve.scalar_tensor_tensor(out=x, in0=y, scalar=m.rs[p], in1=x, op0=ALU.mult, op1=ALU.add))
    seq.wait(dve)
    if last:
        return dve.tensor_scalar(out=x, in0=x, scalar1=m.ms[p], scalar2=None, op0=ALU.add)
    seq.mark(dve.tensor_scalar(out=x, in0=x, scalar1=m.ms[p], scalar2=None, op0=ALU.add))
    seq.wait_apart(dve, m.turnstile)
    seq.mark(dve.bn_stats(out=m.stats_x[p], in_=x))
    seq.wait_apart(dve, m.turnstile)
    seq.mark(dve.bn_aggr(out=m.mv_x[p], in_=m.stats_x[p]))
    seq.wait(dve)
    return dve.tensor_copy(m.mv_next[:, ds(tile * 2, 2)], m.mv_x[p])


BRANCH_ADD_STEPS = 5


def setup_and_sparse(nc, m, s, dram):
    W2, W2T = m.f32(GATEQ_AT, DC * D), m.f32(GATEQ_AT + 2048, DC * D)
    W1, MASK = m.f32(GATEQ_AT + 4096, DC * D), m.f32(GATEQ_AT + 6144, DC * D)
    attn0 = m.f32(ATTN0_AT, DC * D)
    b2, ones = m.f32(WORK, D)[0:1, :], m.f32(WORK + D, P)[0:1, :]
    a = WORK + D + P
    xn = [m.f32(a + i * D, D) for i in range(2)]
    xT = [m.f32(a + (2 + i) * D, D) for i in range(2)]
    y = [m.f32(a + (4 + i) * D, D) for i in range(2)]
    cst = m.f32(a + 6 * D, 6 * P)
    kq = "p (c d) -> p c d"

    weights_in = [s("w2_in"), s("w1_in"), s("mask_in")]
    consts_in, x_in = s("consts_in"), [s(f"x_in{i}") for i in range(4)]
    m.q_in = [s("gate_q_in"), s("up_q_in"), s("down_q_in"), s("lowrank_in"), s("qkv_in")]
    consts_ready, w2_turned, w2T_ready = s("consts_ready"), s("w2_turned"), s("w2T_ready")
    raw_ready, attn0_ready = s("raw_ready"), s("attn0_ready")
    x_stats, rstd_ready = s("x_stats"), s("rstd_ready")
    xn_ready, turned, xT_ready = s("a_xn_ready"), s("a_turned"), s("a_xT_ready")
    y_ready, gelu_ready = s("a_y_ready"), s("a_gelu_ready")
    stats_ready, branch_rstd_ready, added = s("a_stats_ready"), s("a_branch_rstd"), s("a_added")
    dve_seq, pool_seq = Count(s("a_dve_seq")), Count(s("a_pool_seq"))

    with nc.Block() as block:
        @block.sync
        def _(sp):
            sp.dma_start(W2.rearrange(kq, c=DC), dram["w2"].rearrange("(c p) d -> p c d", p=P)).then_inc(weights_in[0], 16)
            sp.dma_start(cst, dram["consts"][:, 0:6 * P]).then_inc(consts_in, 16)
            sp.dma_start(W1.rearrange(kq, c=DC), dram["w1"].rearrange("(c p) d -> p c d", p=P)).then_inc(weights_in[1], 16)
            sp.dma_start(m.f32(X_AT, 4 * D).rearrange(kq, c=4),
                         dram["x"][0:4 * P, :].rearrange("(c p) d -> p c d", p=P)).then_inc(x_in[0], 16)
            sp.dma_start(MASK.rearrange(kq, c=DC), dram["mask"].rearrange("(c p) d -> p c d", p=P)).then_inc(weights_in[2], 16)
            sp.dma_start(b2, dram["b2"].rearrange("(a d) -> a d", a=1)).then_inc(weights_in[2], 16)
            for c in range(1, 4):
                sp.dma_start(m.f32(X_AT + c * 4 * D, 4 * D).rearrange(kq, c=4),
                             dram["x"][c * 4 * P:(c + 1) * 4 * P, :].rearrange("(c p) d -> p c d", p=P)).then_inc(x_in[c], 16)
            full = (IT - 1) * P
            sp.dma_start(m.i32(UPQ_AT, (IT - 1) * D).rearrange(kq, c=IT - 1),
                         dram["up_q"][0:full, :].rearrange("(c p) d -> p c d", p=P)).then_inc(m.q_in[1], 16)
            sp.dma_start(m.i32(UPQ_AT + (IT - 1) * D, D)[0:I_LAST, :], dram["up_q"][full:INNER, :]).then_inc(m.q_in[1], 16)
            sp.dma_start(m.i32(DOWNQ_AT, DC * INNER).rearrange(kq, c=DC),
                         dram["down_q"].rearrange("(c p) i -> p c i", p=P)).then_inc(m.q_in[2], 16)
            sp.wait_ge(attn0_ready, DC)
            sp.dma_start(m.i32(GATEQ_AT, (IT - 1) * D).rearrange(kq, c=IT - 1),
                         dram["gate_q"][0:full, :].rearrange("(c p) d -> p c d", p=P)).then_inc(m.q_in[0], 16)
            sp.dma_start(m.i32(GATEQ_AT + (IT - 1) * D, D)[0:I_LAST, :], dram["gate_q"][full:INNER, :]).then_inc(m.q_in[0], 16)
            load_small_weights(sp, m, dram)

        @block.gpsimd
        def _(pool):
            pool.memset(m.eps, EPS)
            pool.memset(m.half, -0.5)
            pool.memset(m.zero16, 0.0)
            pool.memset(ones, 1.0).then_inc(consts_ready, 1)
            pool.wait_ge(consts_in, 16)
            pool.wait_ge(consts_ready, 1)
            pool.tensor_copy(m.ident, cst[:, 0:P]).then_inc(consts_ready, 1)
            pool.tensor_copy(m.ident_bf, cst[:, 0:P])
            for h in range(4):
                pool.tensor_copy(m.ident4[:, h * P:(h + 1) * P], cst[:, 0:P])
            pool.tensor_copy(m.causal, cst[:, P:2 * P])
            pool.tensor_copy(m.own_chunk, cst[:, 2 * P:3 * P])
            pool.tensor_copy(m.cos, cst[:, 3 * P:4 * P])
            pool.tensor_copy(m.sin, cst[:, 4 * P:5 * P])
            pool.tensor_copy(m.chunk_before, cst[:, 5 * P:5 * P + CPT])
            pool.tensor_copy(m.chunk_own, cst[:, 5 * P + CPT:5 * P + 2 * CPT]).then_inc(consts_ready, 1)
            pool.wait_ge(x_stats, TILES)
            rstd_all(pool, m, pool_seq).then_inc(rstd_ready, 1)
            pool_seq.settle()
            with pool.Fori(0, TILES // 2) as u:
                pool_seq.enter(u, 2)
                for p in range(2):
                    pool.wait_ge(stats_ready, u * 2 + p + 1)
                    branch_rstd(pool, m, pool_seq, p).then_inc(branch_rstd_ready, 1)
            pool_seq.leave(TILES // 2)

        @block.tensor
        def _(pe):
            pe.wait_ge(weights_in[0], 16)
            pe.wait_ge(consts_ready, 2)
            for dc in range(DC):
                for tc in range(DC):
                    last = pe.transpose(m.banks[dc][:, tc * P:(tc + 1) * P], W2[:, tc * D + dc * P:tc * D + (dc + 1) * P], m.ident)
                last.then_inc(w2_turned, 1)
            pe.wait_ge(weights_in[1], 16)
            for sc in range(DC):
                for dc in range(DC):
                    if sc == 0:
                        pe.wait_ge(w2T_ready, dc + 1)
                    last = pe.matmul(m.banks[4 + sc][:, :], W1[:, dc * D + sc * P:dc * D + (sc + 1) * P],
                                     W2T[:, dc * D:(dc + 1) * D], start=dc == 0, stop=dc == DC - 1)
                last.then_inc(raw_ready, 1)

            def turn(k, p):
                pe.wait_ge(xn_ready, k * 1 + 1)
                for dc in range(DC):
                    last = pe.transpose(m.banks[p][:, dc * P:(dc + 1) * P], xn[p][:, dc * P:(dc + 1) * P], m.ident)
                last.then_inc(turned, 1)

            def feed(k, p):
                pe.wait_ge(xT_ready, k + 1)
                pe.wait_ge(gelu_ready, k + 1)
                pe.matmul(m.banks[2 + p][:, :], ones, b2, start=True, stop=False)
                for dc in range(DC):
                    last = pe.matmul(m.banks[2 + p][:, :], xT[p][:, dc * P:(dc + 1) * P], attn0[:, dc * D:(dc + 1) * D],
                                     start=False, stop=dc == DC - 1)
                last.then_inc(y_ready, 1)

            for p in range(2):
                turn(p, p)
            pe.wait_ge(attn0_ready, DC)
            pe.wait_ge(weights_in[2], 32)
            with pe.Fori(0, TILES // 2 - 1) as u:
                for p in range(2):
                    feed(u * 2 + p, p)
                for p in range(2):
                    turn(u * 2 + (2 + p), p)
            for p in range(2):
                feed(TILES - 2 + p, p)

        @block.scalar
        def _(act):
            act.sem_inc(gelu_ready, 2)
            for dc in range(DC):
                act.wait_ge(w2_turned, dc + 1)
                act.activation(W2T[:, dc * D:(dc + 1) * D], m.banks[dc][:, :], ACT.Copy).then_inc(w2T_ready, 1)

            def normed(k, p):
                act.activation(xn[p], m.x(k), ACT.Identity, bias=m.shift[:, ds(k, 1)],
                               scale=m.rstd[:, ds(k, 1)]).then_inc(xn_ready, 1)

            def keep(k, p):
                act.wait_ge(turned, k + 1)
                act.activation(xT[p], m.banks[p][:, :], ACT.Copy).then_inc(xT_ready, 1)

            def gelu(k, p):
                act.wait_ge(y_ready, k + 1)
                act.wait_ge(added, k + 1)
                act.activation(y[p], m.banks[2 + p][:, :], ACT.Gelu).then_inc(gelu_ready, 1)

            act.wait_ge(rstd_ready, 1)
            for p in range(2):
                normed(p, p)
            for p in range(2):
                keep(p, p)
            with act.Fori(0, TILES // 2 - 1) as u:
                for p in range(2):
                    normed(u * 2 + (2 + p), p)
                for p in range(2):
                    gelu(u * 2 + p, p)
                for p in range(2):
                    keep(u * 2 + (2 + p), p)
            for p in range(2):
                gelu(TILES - 2 + p, p)

        @block.vector
        def _(dve):
            dve.sem_inc(added, 2)
            for sc in range(DC):
                if sc == 0:
                    dve.wait_ge(weights_in[2], 32)
                dve.wait_ge(raw_ready, sc + 1)
                dve.tensor_tensor(out=attn0[:, sc * D:(sc + 1) * D], in0=m.banks[4 + sc][:, :],
                                  in1=MASK[:, sc * D:(sc + 1) * D], op=ALU.mult).then_inc(attn0_ready, 1)
            st16 = m.f32(a + 8 * D, 6 * TILES)
            for t in range(TILES):
                if t % 4 == 0:
                    dve.wait_ge(x_in[t // 4], 16)
                dve_seq.mark(dve.bn_stats(out=st16[:, 6 * t:6 * t + 6], in_=m.x(t)))
            for t in range(TILES):
                if t == 0:
                    dve_seq.wait(dve)
                dve.bn_aggr(out=m.mv_next[:, 2 * t:2 * t + 2], in_=st16[:, 6 * t:6 * t + 6]).then_inc(x_stats, 1)
            dve_seq.settle()
            with dve.Fori(0, TILES // 2) as u:
                dve_seq.enter(u, 2 * (1 + BRANCH_ADD_STEPS))
                for p in range(2):
                    dve.wait_ge(gelu_ready, u * 2 + (p + 3))
                    branch_stats(dve, m, dve_seq, p, y[p]).then_inc(stats_ready, 1)
                for p in range(2):
                    dve.wait_ge(branch_rstd_ready, u * 2 + p + 1)
                    branch_add(dve, m, dve_seq, p, y[p], u * 2 + p).then_inc(added, 1)
            dve_seq.leave(TILES // 2)


LOW_AT = WORK + 4864
GB_AT, UB_AT, DB_AT = LOW_AT, LOW_AT + INNER, LOW_AT + 2 * INNER
GA_AT = DB_AT + D
UA_AT, DA_AT = GA_AT + DC * RANK, GA_AT + 2 * DC * RANK
WQ_AT = DA_AT + IT * RANK
GAT_AT = WQ_AT + 6 * D
UAT_AT, DAT_AT = GAT_AT + D, GAT_AT + 2 * D
DEQ_AT = DAT_AT + INNER


def load_small_weights(sp, m, dram):
    kq, full = "p (c d) -> p c d", (IT - 1) * P
    low, qkv = m.q_in[3], m.q_in[4]
    sp.dma_start(m.f32(GB_AT, INNER)[0:RANK, :], dram["gate_B"]).then_inc(low, 16)
    sp.dma_start(m.f32(UB_AT, INNER)[0:RANK, :], dram["up_B"]).then_inc(low, 16)
    sp.dma_start(m.f32(DB_AT, D)[0:RANK, :], dram["down_B"]).then_inc(low, 16)
    sp.dma_start(m.f32(GA_AT, DC * RANK).rearrange(kq, c=DC), dram["gate_A"].rearrange("(c p) r -> p c r", p=P)).then_inc(low, 16)
    sp.dma_start(m.f32(UA_AT, DC * RANK).rearrange(kq, c=DC), dram["up_A"].rearrange("(c p) r -> p c r", p=P)).then_inc(low, 16)
    sp.dma_start(m.f32(DA_AT, (IT - 1) * RANK).rearrange(kq, c=IT - 1),
                 dram["down_A"][0:full, :].rearrange("(c p) r -> p c r", p=P)).then_inc(low, 16)
    sp.dma_start(m.f32(DA_AT + (IT - 1) * RANK, RANK)[0:I_LAST, :], dram["down_A"][full:INNER, :]).then_inc(low, 16)
    for k, name in enumerate(("gate_scale", "up_scale")):
        sp.dma_start(m.scales[:, k * IT:k * IT + IT - 1], dram[name][0:full].rearrange("(c p) -> p c", p=P), allow_slow_non_contiguous=True).then_inc(low, 16)
        sp.dma_start(m.scales[0:I_LAST, k * IT + IT - 1:(k + 1) * IT],
                     dram[name][full:INNER].rearrange("(p c) -> p c", c=1), allow_slow_non_contiguous=True).then_inc(low, 16)
    sp.dma_start(m.scales[:, 2 * IT:2 * IT + DC], dram["down_scale"].rearrange("(c p) -> p c", p=P), allow_slow_non_contiguous=True).then_inc(low, 16)
    sp.dma_start(m.f32(WQ_AT, DC * D).rearrange(kq, c=DC), dram["wq"].rearrange("(c p) d -> p c d", p=P)).then_inc(qkv, 16)
    sp.dma_start(m.f32(WQ_AT + DC * D, D), dram["wk"]).then_inc(qkv, 16)
    sp.dma_start(m.f32(WQ_AT + (DC + 1) * D, D), dram["wv"]).then_inc(qkv, 16)


LOW_LOADS, QKV_LOADS = 12, 3


def weights(nc, m, s, dram):
    deq = [m.f32(DEQ_AT + i * D, D) for i in range(2)]
    down_AT_tile = [m.f32(DEQ_AT + (2 + i) * D, P)[0:RANK, :] for i in range(2)]
    gAT, uAT, dAT = (m.f32(at, n)[0:RANK, :] for at, n in ((GAT_AT, D), (UAT_AT, D), (DAT_AT, INNER)))
    wide = [(GATEQ_AT, gAT, GB_AT, WG_AT, 0), (UPQ_AT, uAT, UB_AT, WU_AT, IT)]
    down_first = 2 * IT
    scales_ready, factors_turned, factors_ready = s("scales_ready"), s("factors_turned"), s("factors_ready")
    deq_ready, down_A_ready, built, placed = s("deq_ready"), s("down_A_ready"), s("w_built"), s("w_placed")
    qkv_turned, qkv_placed = s("qkv_turned"), s("qkv_placed")
    scaled = 2 * IT + DC

    def rows(tile):
        return I_LAST if isinstance(tile, int) and tile == IT - 1 else P

    def each_tile(eng, first, body):
        with eng.Fori(0, (IT - 1) // 2) as u:
            for k in range(2):
                body(u * 2 + k, (first + k) % 2)
        body(IT - 1, (first + IT - 1) % 2)

    with nc.Block() as block:
        @block.tensor
        def _(pe):
            pe.wait_ge(m.q_in[3], 16 * LOW_LOADS)
            for k, (at, n) in enumerate(((GA_AT, DC), (UA_AT, DC))):
                for c in range(n):
                    last = pe.transpose(m.banks[k][0:RANK, c * P:(c + 1) * P], m.f32(at + c * RANK, RANK), m.ident)
                last.then_inc(factors_turned, 1)
            for c in range(IT):
                r = rows(c)
                last = pe.transpose(m.banks[2 + c // 4][0:RANK, c % 4 * P:c % 4 * P + r],
                                    m.f32(DA_AT + c * RANK, RANK)[0:r, :], m.ident[0:r, 0:r])
                if c % 4 == 3 or c == IT - 1:
                    last.then_inc(factors_turned, 1)
            pe.wait_ge(factors_ready, 5)
            for _, AT, b_at, _, first in wide:
                B = m.f32(b_at, INNER)[0:RANK, :]

                def tile(t, p):
                    r = rows(t)
                    bank = m.banks[6 + p]
                    pe.wait_ge(deq_ready, t + first + 1)
                    pe.wait_ge(placed, t + first + 1)
                    for hc in range(DC):
                        pe.matmul(bank[:, hc * P:hc * P + r], deq[p][0:r, hc * P:(hc + 1) * P], m.ident[0:r, 0:r],
                                  start=hc == 0, stop=False, skip_group_check=True)
                    for hc in range(DC):
                        last = pe.matmul(bank[:, hc * P:hc * P + r], AT[:, hc * P:(hc + 1) * P], B[:, ds(t * P, r)],
                                         start=False, stop=hc == DC - 1, skip_group_check=True)
                    last.then_inc(built, 1)
                each_tile(pe, first, tile)

            def down_tile(t, p):
                r = rows(t)
                bank = m.banks[6 + p]
                pe.wait_ge(deq_ready, t + down_first + 1)
                pe.wait_ge(down_A_ready, t + 3)
                pe.wait_ge(placed, t + down_first + 1)
                for oc in range(DC):
                    pe.matmul(bank[0:r, oc * P:(oc + 1) * P], deq[p][:, oc * P:oc * P + r], m.ident,
                              start=oc == 0, stop=False, skip_group_check=True)
                pe.matmul(bank[0:r, :], down_AT_tile[p][:, 0:r], m.f32(DB_AT, D)[0:RANK, :],
                          start=False, stop=True, skip_group_check=True).then_inc(built, 1)
            each_tile(pe, down_first, down_tile)

            pe.wait_ge(m.q_in[4], 16 * QKV_LOADS)
            for c in range(DC + 2):
                if c >= 5:
                    pe.wait_ge(qkv_placed, c - 4)
                for hc in range(DC):
                    last = pe.transpose(m.banks[c % 5][:, hc * P:(hc + 1) * P],
                                        m.f32(WQ_AT + c * D + hc * P, P), m.ident)
                last.then_inc(qkv_turned, 1)

        @block.vector
        def _(dve):
            dve.wait_ge(m.q_in[3], 16 * LOW_LOADS)
            dve.tensor_scalar(out=m.scales[:, 0:IT - 1], in0=m.scales[:, 0:IT - 1], scalar1=Q_STEP, scalar2=None, op0=ALU.mult)
            dve.tensor_scalar(out=m.scales[0:I_LAST, IT - 1:IT], in0=m.scales[0:I_LAST, IT - 1:IT], scalar1=Q_STEP, scalar2=None, op0=ALU.mult)
            dve.tensor_scalar(out=m.scales[:, IT:2 * IT - 1], in0=m.scales[:, IT:2 * IT - 1], scalar1=Q_STEP, scalar2=None, op0=ALU.mult)
            dve.tensor_scalar(out=m.scales[0:I_LAST, 2 * IT - 1:2 * IT], in0=m.scales[0:I_LAST, 2 * IT - 1:2 * IT], scalar1=Q_STEP, scalar2=None, op0=ALU.mult)
            dve.tensor_scalar(out=m.scales[:, 2 * IT:scaled], in0=m.scales[:, 2 * IT:scaled], scalar1=Q_STEP, scalar2=None, op0=ALU.mult).then_inc(scales_ready, 1)
            dve.wait_ge(scales_ready, 1)
            for k, (q_at, _, _, _, first) in enumerate(wide):
                dve.wait_ge(m.q_in[k], 32)

                def tile(t, p):
                    r = rows(t)
                    dve.wait_ge(built, t + first + 1)
                    dve.tensor_scalar(out=deq[p][0:r, :], in0=m.arena[0:r, ds(t * D + q_at, D)].bitcast(I32),
                                      scalar1=-Q_ZERO, scalar2=m.scales[0:r, ds(t + k * IT, 1)],
                                      op0=ALU.add, op1=ALU.mult).then_inc(deq_ready, 1)
                each_tile(dve, first, tile)
            dve.wait_ge(m.q_in[2], 16)
            q = m.i32(DOWNQ_AT, DC * INNER).rearrange("p (c i) -> p c i", c=DC)

            def down_tile(t, p):
                r = rows(t)
                dve.wait_ge(built, t + down_first + 1)
                dve.scalar_tensor_tensor(out=deq[p].rearrange("p (c i) -> p c i", c=DC)[:, :, 0:r], in0=q[:, :, ds(t * P, r)],
                                         scalar=-Q_ZERO, in1=m.scales[:, 2 * IT:scaled].unsqueeze(2).to_broadcast([P, DC, r]),
                                         op0=ALU.add, op1=ALU.mult).then_inc(deq_ready, 1)
            each_tile(dve, down_first, down_tile)

        @block.gpsimd
        def _(pool):
            pool.sem_inc(down_A_ready, 2)
            pool.sem_inc(built, 2)
            pool.wait_ge(factors_ready, 5)

            def tile(t, p):
                r = rows(t)
                pool.wait_ge(built, t + down_first + 1)
                pool.tensor_copy(down_AT_tile[p][:, 0:r], dAT[:, ds(t * P, r)]).then_inc(down_A_ready, 1)
            each_tile(pool, down_first, tile)

        @block.scalar
        def _(act):
            act.sem_inc(placed, 2)
            for k, AT in enumerate((gAT, uAT)):
                act.wait_ge(factors_turned, k + 1)
                act.activation(AT, m.banks[k][0:RANK, :], ACT.Copy, scale=LR_SCALE).then_inc(factors_ready, 1)
            for k in range(3):
                n = min(D, INNER - k * D)
                act.wait_ge(factors_turned, k + 3)
                act.activation(dAT[:, k * D:k * D + n], m.banks[2 + k][0:RANK, 0:n], ACT.Copy, scale=LR_SCALE).then_inc(factors_ready, 1)
            for _, _, _, out_at, first in wide:
                W = m.f32(out_at, DC * INNER).rearrange("p (c i) -> p c i", c=DC)

                def tile(t, p):
                    r = rows(t)
                    act.wait_ge(built, t + first + 3)
                    act.activation(W[:, :, ds(t * P, r)], m.banks[6 + p].rearrange("p (c i) -> p c i", c=DC)[:, :, 0:r],
                                   ACT.Copy).then_inc(placed, 1)
                each_tile(act, first, tile)

            def down_tile(t, p):
                r = rows(t)
                act.wait_ge(built, t + down_first + 3)
                act.activation(m.arena[0:r, ds(t * D + WD_AT, D)], m.banks[6 + p][0:r, :], ACT.Copy).then_inc(placed, 1)
            each_tile(act, down_first, down_tile)

            W = m.f32(WQKV_AT, DC * QKV).rearrange("p (c n) -> p c n", c=DC)
            for c in range(DC + 2):
                act.wait_ge(qkv_turned, c + 1)
                act.activation(W[:, :, c * P:(c + 1) * P], m.banks[c % 5].rearrange("p (c n) -> p c n", c=DC), ACT.Copy).then_inc(qkv_placed, 1)


def gated(nc, m, s, dram):
    G = 4
    Wg, Wu = m.f32(WG_AT, DC * INNER), m.f32(WU_AT, DC * INNER)
    xT = m.f32(WORK, DC * G * P)
    xn = [m.f32(WORK + DC * G * P + i * D, D) for i in range(G)]
    silu = [m.f32(WORK + DC * G * P + (G + i) * D, D) for i in range(2)]
    rstd_ready, xn_ready, turned, xT_ready = s("b_rstd"), s("b_xn"), s("b_turned"), s("b_xT")
    products, silu_ready, h_ready = s("b_products"), s("b_silu"), s("b_h_ready")
    down_ready, stats_ready, branch_rstd_ready, added = s("b_down"), s("b_stats"), s("b_branch_rstd"), s("b_added")
    dve_seq, pool_seq = Count(s("b_dve_seq")), Count(s("b_pool_seq"))
    n_groups = TILES // G

    def rows(i):
        return I_LAST if i == IT - 1 else P

    def h_free(g, i):
        return g * IT + (i + 1 if i >= 2 else 2 - i)

    def over_groups(eng, body):
        with eng.Fori(0, n_groups - 1) as g:
            body(g, False)
        body(n_groups - 1, True)

    with nc.Block() as block:
        @block.tensor
        def _(pe):
            def turn(g, t):
                k = g * G + t
                pe.wait_ge(xn_ready, k + 1)
                pe.wait_ge(xT_ready, k + 1)
                for dc in range(DC):
                    last = pe.transpose(m.banks[4 + t % 2][:, dc * P:(dc + 1) * P], xn[t][:, dc * P:(dc + 1) * P], m.ident)
                last.then_inc(turned, 1)

            def group(g, last_group):
                pe.wait_ge(xT_ready, g * G + (G + 2))
                for i in range(IT):
                    r = rows(i)
                    pe.wait_ge(h_ready, h_free(g, i))
                    for W, bank in ((Wg, m.banks[i % 2]), (Wu, m.banks[2 + i % 2])):
                        for dc in range(DC):
                            last = pe.matmul(bank[0:r, :], W[:, dc * INNER + i * P:dc * INNER + i * P + r],
                                             xT[:, dc * G * P:(dc + 1) * G * P], start=dc == 0, stop=dc == DC - 1)
                    last.then_inc(products, 1)
                if not last_group:
                    for t in range(G):
                        turn(g + 1, t)
                pe.wait_ge(h_ready, g * IT + (IT + 2))
                for t in range(G):
                    pe.wait_ge(added, g * G + (t + 1))
                    for i in range(IT):
                        r = rows(i)
                        last = pe.matmul(m.banks[6 + t % 2][:, :], m.f32(HT_AT + i * D + t * P, P)[0:r, :],
                                         m.f32(WD_AT + i * D, D)[0:r, :], start=i == 0, stop=i == IT - 1)
                    last.then_inc(down_ready, 1)

            for t in range(G):
                turn(0, t)
            over_groups(pe, group)

        @block.scalar
        def _(act):
            def normed(g, t):
                k = g * G + t
                act.activation(xn[t], m.x(k), ACT.Identity, bias=m.shift[:, ds(k, 1)],
                               scale=m.rstd[:, ds(k, 1)]).then_inc(xn_ready, 1)

            def keep(g, t):
                act.wait_ge(turned, g * G + (t + 1))
                act.activation(xT.rearrange("p (c n) -> p c n", c=DC)[:, :, t * P:(t + 1) * P],
                               m.banks[4 + t % 2].rearrange("p (c n) -> p c n", c=DC), ACT.Copy).then_inc(xT_ready, 1)

            def group(g, last_group):
                for i in range(IT):
                    r = rows(i)
                    act.wait_ge(products, g * IT + (i + 1))
                    act.wait_ge(h_ready, h_free(g, i))
                    act.activation(silu[i % 2][0:r, :], m.banks[i % 2][0:r, :], ACT.Silu).then_inc(silu_ready, 1)
                    if i in (1, 3, 5, 7) and not last_group:
                        normed(g + 1, i // 2)
                if not last_group:
                    for t in range(G):
                        keep(g + 1, t)

            act.sem_inc(xT_ready, 2)
            act.wait_ge(rstd_ready, 1)
            for t in range(G):
                normed(0, t)
            for t in range(G):
                keep(0, t)
            over_groups(act, group)

        @block.vector
        def _(dve):
            dve.sem_inc(h_ready, 2)
            dve.sem_inc(added, 2)

            def group(g, _):
                for i in range(IT):
                    r = rows(i)
                    dve.wait_ge(silu_ready, g * IT + (i + 1))
                    dve.tensor_tensor(out=m.f32(HT_AT + i * D, D)[0:r, :], in0=m.banks[2 + i % 2][0:r, :],
                                      in1=silu[i % 2][0:r, :], op=ALU.mult).then_inc(h_ready, 1)
                dve_seq.enter(g, G * (1 + BRANCH_ADD_STEPS))
                for t in range(G):
                    dve.wait_ge(down_ready, g * G + (t + 1))
                    branch_stats(dve, m, dve_seq, t % 2, m.banks[6 + t % 2][:, :]).then_inc(stats_ready, 1)
                    dve.wait_ge(branch_rstd_ready, g * G + (t + 1))
                    branch_add(dve, m, dve_seq, t % 2, m.banks[6 + t % 2][:, :], g * G + t).then_inc(added, 1)
            over_groups(dve, group)

        @block.gpsimd
        def _(pool):
            rstd_all(pool, m, pool_seq).then_inc(rstd_ready, 1)
            pool_seq.settle()

            def group(g, _):
                pool_seq.enter(g, G)
                for t in range(G):
                    pool.wait_ge(stats_ready, g * G + (t + 1))
                    branch_rstd(pool, m, pool_seq, t % 2).then_inc(branch_rstd_ready, 1)
            over_groups(pool, group)


def project(nc, m, s, dram):
    W = m.f32(WQKV_AT, DC * QKV)
    take = m.taker(WORK, ARENA - SEQ)
    xn, xT = [take(D) for _ in range(2)], [take(D) for _ in range(2)]
    raw, spun = [take(QK) for _ in range(2)], [take(QK) for _ in range(2)]
    rotated = [take(QK) for _ in range(2)]
    part = [[take(QK, BF16) for _ in range(PARTS)] for _ in range(2)]
    q_rows, k_rows = [take(HEADS * ROWS, BF16) for _ in range(2)], [take(KV * ROWS, BF16) for _ in range(2)]
    key_rows = take(SEQ)
    v_all = m.f32(V_AT, GROUPS * SEQ_TILES * 32)
    rstd_ready, xn_ready, turned, xT_ready = s("c_rstd"), s("c_xn"), s("c_turned"), s("c_xT")
    products, raw_ready, v_ready, spun_ready = s("c_products"), s("c_raw"), s("c_v"), s("c_spun")
    rotated_ready, high_ready, high_rows_ready = s("c_rotated"), s("c_high"), s("c_high_rows")
    rows_ready, rows_out = s("c_rows_ready"), [s(f"c_rows_out{b}") for b in range(2)]
    v_blank, rows_in = s("c_v_blank"), s("c_rows_in")
    dve_seq, pool_seq = Count(s("c_dve_seq")), Count(s("c_pool_seq"))

    def heads(ap):
        return ap.rearrange("p (h d) -> p h d", d=HD)

    def slots(ap):
        return ap.rearrange("p (h r d) -> p h r d", r=6, d=HD)

    def q_of(ap, n):
        return heads(ap[:, 0:HEADS * HD]).unsqueeze(2).to_broadcast([P, HEADS, n, HD])

    def k_of(ap, n):
        return heads(ap[:, HEADS * HD:QK]).unsqueeze(2).to_broadcast([P, KV, n, HD])

    with nc.Block() as block:
        @block.sync
        def _(sp):
            sp.dma_start(key_rows[ROWS:KROWS, :], dram["key_rows"]).then_inc(rows_in, 16)
            with sp.Fori(0, SEQ_TILES) as i:
                for b in range(2):
                    k = i * 2 + b
                    to = dram["rows"][b * KV:(b + 1) * KV].rearrange("k p (t w) -> p k t w", t=SEQ_TILES)[:, :, ds(i, 1), :].squeeze(2)
                    sp.wait_ge(high_rows_ready, k + 1)
                    sp.wait_ge(rows_ready, k + 1)
                    sp.dma_start(to[:, :, 0:GQ * ROWS], q_rows[b].rearrange("p (k w) -> p k w", k=KV)).then_inc(rows_out[b], 16)
                    sp.dma_start(to[:, :, GQ * ROWS:], k_rows[b].rearrange("p (k w) -> p k w", k=KV)).then_inc(rows_out[b], 16)
            for b in range(2):
                sp.wait_ge(rows_out[b], SEQ_TILES * 32 + 32)

        @block.tensor
        def _(pe):
            def turn(k, b):
                pe.wait_ge(xn_ready, k + 1)
                for dc in range(DC):
                    last = pe.transpose(m.banks[b][:, dc * P:(dc + 1) * P], xn[b][:, dc * P:(dc + 1) * P], m.ident)
                last.then_inc(turned, 1)

            def feed(k, b):
                pe.wait_ge(xT_ready, k + 1)
                pe.wait_ge(v_ready, k + 1)
                for dc in range(DC):
                    pe.matmul(m.banks[2 + b][:, :], xT[b][:, dc * P:(dc + 1) * P], W[:, dc * QKV:dc * QKV + D],
                              start=dc == 0, stop=dc == DC - 1)
                for dc in range(DC):
                    last = pe.matmul(m.banks[4 + b][:, 0:QKV - D], xT[b][:, dc * P:(dc + 1) * P], W[:, dc * QKV + D:(dc + 1) * QKV],
                                     start=dc == 0, stop=dc == DC - 1)
                last.then_inc(products, 1)

            for b in range(2):
                turn(b, b)
            with pe.Fori(0, SEQ_TILES - 1) as i:
                for b in range(2):
                    feed(i * 2 + b, b)
                for b in range(2):
                    turn(i * 2 + (2 + b), b)
            for b in range(2):
                feed(TILES - 2 + b, b)

        @block.scalar
        def _(act):
            def normed(i, b):
                act.activation(xn[b], m.x(i + b * SEQ_TILES), ACT.Identity, bias=m.shift[:, ds(i + b * SEQ_TILES, 1)],
                               scale=m.rstd[:, ds(i + b * SEQ_TILES, 1)]).then_inc(xn_ready, 1)

            def keep(k, b):
                act.wait_ge(turned, k + 1)
                act.activation(xT[b], m.banks[b][:, :], ACT.Copy).then_inc(xT_ready, 1)

            def evacuate(i, b):
                k = i * 2 + b
                act.wait_ge(products, k + 1)
                act.wait_ge(rotated_ready, k + 1)
                act.activation(raw[b][:, 0:D], m.banks[2 + b][:, :], ACT.Copy)
                act.activation(raw[b][:, D:QK], m.banks[4 + b][:, 0:QK - D], ACT.Copy).then_inc(raw_ready, 1)
                v = v_all.rearrange("p (b k t c) -> p b k t c", b=BATCH, k=KV, t=SEQ_TILES)[:, b]
                act.activation(v[:, :, ds(i, 1), 0:HD].squeeze(2), heads(m.banks[4 + b][:, QK - D:QKV - D]), ACT.Copy).then_inc(v_ready, 1)

            def cut(i, b):
                k = i * 2 + b
                act.wait_ge(rotated_ready, k + 3)
                act.activation(part[b][0], rotated[b], ACT.Copy).then_inc(high_ready, 1)
                act.wait_ge(rows_out[b], i * 32 + 32)
                act.wait_ge(high_ready, k + 1)
                act.activation(slots(q_rows[b])[:, :, 0:3, :], q_of(part[b][0], 3), ACT.Copy).then_inc(high_rows_ready, 1)

            act.sem_inc(v_ready, 2)
            act.wait_ge(rstd_ready, 1)
            act.wait_ge(v_blank, 1)
            for b in range(2):
                normed(0, b)
            for b in range(2):
                keep(b, b)
            with act.Fori(0, SEQ_TILES - 1) as i:
                for b in range(2):
                    normed(i + 1, b)
                for b in range(2):
                    evacuate(i, b)
                for b in range(2):
                    keep(i * 2 + (2 + b), b)
                for b in range(2):
                    cut(i, b)
            for b in range(2):
                evacuate(SEQ_TILES - 1, b)
            for b in range(2):
                cut(SEQ_TILES - 1, b)

        @block.gpsimd
        def _(pool):
            v = v_all.rearrange("p (n c) -> p n c", c=32)
            pool.memset(v[:, :, HD + 1:], 0.0)
            pool.memset(v[:, :, HD:HD + 1], 1.0).then_inc(v_blank, 1)
            rstd_all(pool, m, pool_seq).then_inc(rstd_ready, 1)
            pool.sem_inc(rotated_ready, 2)
            for b in range(2):
                pool.sem_inc(rows_out[b], 32)
            pool_seq.settle()
            with pool.Fori(0, SEQ_TILES) as i:
                for b in range(2):
                    sin = m.sin.rearrange("p (t d) -> p t d", d=HD)[:, ds(i, 1), :]
                    pool.wait_ge(rotated_ready, i * 2 + b + 1)
                    pool.wait_ge(raw_ready, i * 2 + b + 1)
                    pool.sem_inc(m.turnstile, 1)
                    h = HD // 2
                    for lo, hi in ((0, h), (h, 0)):
                        last = pool.tensor_tensor(out=heads(spun[b])[:, :, lo:lo + h], in0=heads(raw[b])[:, :, hi:hi + h],
                                                  in1=sin[:, :, lo:lo + h].to_broadcast([P, QK // HD, h]), op=ALU.mult)
                    last.then_inc(spun_ready, 1)

        @block.vector
        def _(dve):
            dve.wait_ge(rows_in, 16)
            for k in range(2):
                dve.tensor_copy(m.key_aug[k][ROWS:KROWS, :], key_rows[ROWS:KROWS, :])
            with dve.Fori(0, SEQ_TILES) as i:
                dve_seq.enter(i, 12)
                cos = m.cos.rearrange("p (t d) -> p t d", d=HD)[:, ds(i, 1), :]
                for b in range(2):
                    k = i * 2 + b
                    dve.wait_ge(raw_ready, k + 1)
                    dve_seq.mark(dve.tensor_tensor(out=heads(rotated[b]), in0=heads(raw[b]),
                                                   in1=cos.to_broadcast([P, QK // HD, HD]), op=ALU.mult))
                    dve_seq.wait(dve)
                    dve.wait_ge(spun_ready, k + 1)
                    dve.tensor_tensor(out=rotated[b], in0=rotated[b], in1=spun[b], op=ALU.add).then_inc(rotated_ready, 1)
                for b in range(2):
                    k = i * 2 + b
                    high, mid, low = part[b]
                    dve.wait_ge(high_ready, k + 1)
                    dve_seq.mark(dve.tensor_tensor(out=rotated[b], in0=rotated[b], in1=high, op=ALU.subtract))
                    dve_seq.wait(dve)
                    dve_seq.mark(dve.tensor_copy(mid, rotated[b]))
                    dve_seq.wait(dve)
                    dve_seq.mark(dve.tensor_tensor(out=low, in0=rotated[b], in1=mid, op=ALU.subtract))
                    dve.wait_ge(rows_out[b], i * 32 + 32)
                    q, kk = slots(q_rows[b]), slots(k_rows[b])
                    dve_seq.mark(dve.tensor_copy(kk[:, :, 0:4:3, :], k_of(high, 2)))
                    dve_seq.mark(dve.tensor_copy(kk[:, :, 5:6, :], k_of(high, 1)))
                    dve.tensor_copy(kk[:, :, 1:5:3, :], k_of(mid, 2))
                    dve.tensor_copy(q[:, :, 3:5, :], q_of(mid, 2))
                    dve_seq.wait(dve)
                    dve.tensor_copy(kk[:, :, 2:3, :], k_of(low, 1))
                    dve.tensor_copy(q[:, :, 5:6, :], q_of(low, 1)).then_inc(rows_ready, 1)
            dve_seq.leave(SEQ_TILES)


def attention(nc, m, s, dram):
    take = m.taker(CWORK, WO_AT)
    N = GQ * P
    CLOSES = 3
    ORDER = [7, 0, 6, 1, 5, 2, 4, 3]
    query_aug = [take(2 * N if i >= 4 else N, BF16) for i in ORDER]
    chunk_diag = [take(N, BF16) for _ in ORDER]
    staged = [take(ST_W, BF16) for _ in range(2)]
    v_staged = [take(SEQ_TILES * 32) for _ in range(2)]
    probs = [take(N) for _ in range(4)]
    W = [take(GQ * 2 * (MASK_ROWS + 1), BF16) for _ in range(SEQ_TILES)]
    cmax = [take(GQ * 64) for _ in range(2)]
    left = [take(GQ * 64) for _ in range(2)]
    top = [take(GQ * TOPK) for _ in range(4)]
    own = [take(GQ * CPT) for _ in range(4)]
    own_dropped = [take(GQ) for _ in range(4)]
    minus = [take(GQ) for _ in range(2)]
    minus_rest = [take(GQ) for _ in range(2)]
    ot = [take(P) for _ in ORDER]
    inverse = [take(4 * GQ) for _ in range(CLOSES)]
    o_staged = [take(SEQ_TILES * GQ * HD) for _ in range(2)]
    neg_one, one_row = take(GQ), take(GQ)
    key_aug = m.key_aug

    score_bank, back_bank, turn_bank = m.banks[0:3], m.banks[3:5], m.banks[5]
    sums = [m.banks[6 + i][:, 0:P] for i in range(2)]
    turn_bf = turn_bank[:, :].bitcast(BF16)

    staged_in, v_in, stored = ([s(f"d_{name}{p}") for p in range(2)] for name in ("staged", "v_in", "stored"))
    top_turned, top_kept = s("d_top_turned"), s("d_top_kept")
    scored, reduced = s("d_scored"), s("d_reduced")
    mask_ready, minus_ready = s("d_mask"), s("d_minus")
    mask_turned, mask_kept = s("d_mask_turned"), s("d_mask_kept")
    masked_scored, probs_ready, summed = s("d_masked_scored"), s("d_probs"), s("d_summed")
    ot_ready = s("d_ot")
    w_blank, top_ready, own_ready, diag_ready = s("d_w_blank"), s("d_top"), s("d_own"), s("d_diag")
    dve_seq, pool_seq = Count(s("d_dve_seq")), Count(s("d_pool_seq"))

    halves = [1 if (i + 1) * P <= 512 else 2 for i in range(SEQ_TILES)]
    score_at = [GQ * sum(halves[i] for i in ORDER[:n]) for n in range(SEQ_TILES + 1)]
    back_at = [sum(i + 1 for i in ORDER[:n]) for n in range(SEQ_TILES + 1)]
    drops_at = [sum(i >= 2 for i in ORDER[:n]) for n in range(SEQ_TILES)]
    SC, BK, TT = score_at[-1], back_at[-1], SEQ_TILES + 2
    RING = SC + CLOSES
    assert RING % 3 == 0 and BK % 4 == 0
    PAIR = 2 * SEQ_TILES

    class Step:

        def __init__(self, t, k):
            self.g, self.at, self.k, self.p = t * 2 + k // SEQ_TILES, k % SEQ_TILES, k, k // SEQ_TILES % 2
            self.i = ORDER[self.at]
            self.n, self.q = t * PAIR + k, t + k // PAIR
            self.exists = not isinstance(t, int) or 0 <= t * PAIR + k < GROUPS * SEQ_TILES
            self.slot = k % SEQ_TILES
            self.two = self.i >= 4

    def closing(t, u):
        first = {0: 4, 1: 3, 2: 3}.get(u % 4)
        steps = [Step(t, k) for k in range(2 * (u - first), 2 * (u - 2))] if first else []
        return [st for st in steps if st.exists], Step(t, 2 * u).g, u % 4

    def is_first(g):
        return isinstance(g, int) and g == 0

    def ring_of_score(st, number):
        closes = 0 if is_first(st.g) else min((st.at + 1) // 2, CLOSES) - CLOSES
        return st.g * RING + (score_at[st.at] + number + closes)

    def ring_of_close(g, place):
        last = isinstance(g, int) and g == GROUPS
        return g * RING + ((0 if last else score_at[2 * place + 1]) + place - CLOSES)

    def bank_of_score(st, number):
        return (score_at[st.at] + number + min((st.at + 1) // 2, CLOSES)) % 3 if not is_first(st.g) else (score_at[st.at] + number) % 3

    def closed_bank(g, place):
        return ((0 if isinstance(g, int) and g == GROUPS else score_at[2 * place + 1]) + place) % 3

    def stages(t, u):
        return [[st for st in (Step(t, 2 * (u - n)), Step(t, 2 * (u - n) + 1)) if st.exists] for n in (0, 1, 2, 3, -1)]

    def schedule(t, u):
        front, mid, back, end, after = stages(t, u)
        scores = [("score", st, n) for st in front for n in range(GQ * halves[st.i])]
        tiles = [(st, j) for st in back for j in range(st.i + 1)]
        backs = []
        lag = 2
        for n in range(len(tiles) + lag):
            if n < len(tiles):
                backs.append(("masked", *tiles[n]))
            if n == 1 and end:
                backs.append(("sums", end[1], 0))
            if n >= lag:
                backs.append(("weigh", *tiles[n - lag]))
                if tiles[n - lag] == (back[1], 0):
                    backs.append(("sums", back[0], 0))
        if not back and end:
            backs = [("sums", end[1], 0)]
        if closing(t, u)[0]:
            scores.insert(GQ * halves[front[0].i] if front else 0, ("close", None, 0))
        ahead, choice = 1, 1.6
        at, starts = 0.0, []
        for kind, st, n in scores:
            starts.append(at)
            if kind == "score":
                half = n % halves[st.i]
                at += 0.25 + min((st.i + 1) * P - half * 512, 512) / 1000
                if n == GQ * halves[st.i] - 1:
                    at += choice if st.i >= 2 else 0.2
            else:
                at += 0.5
        places = [(starts[max(n - ahead, 0)] / at if front else 0.99, x) for n, x in enumerate(scores)]
        places += [(n / max(len(backs), 1), x) for n, x in enumerate(backs)]
        places += [(f, ("turn_q", st, 0)) for f, st in zip((0.05, 0.25), after)]
        places += [(f, ("turn_mask", st, 0)) for f, st in zip((0.4, 0.6), mid)]
        if front and front[0].at == 4 and Step(t, 2 * u + 4).exists:
            places += [(f, ("turn_k", Step(t, 2 * u + 4), half)) for f, half in ((0.55, 0), (0.9, 1))]
        return [x for _, x in sorted(places, key=lambda x: x[0])]

    def over_units(eng, body, seq=None, per=0):
        for u in range(4):
            body(0, u)
        if seq:
            seq.settle()
        with eng.Fori(0, GROUPS // 2 - 1) as t:
            if seq:
                seq.enter(t, per)
            for u in range(4, SEQ_TILES + 4):
                body(t, u)
        if seq:
            seq.leave(GROUPS // 2 - 1)
        for u in range(4, SEQ_TILES + 4):
            body(GROUPS // 2 - 1, u)

    with nc.Block() as block:
        @block.sync
        def _(sp):
            def load_rows(g, p):
                sp.dma_start(staged[p], dram["rows"][ds(g, 1)].squeeze(0)).then_inc(staged_in[p], 16)

            def load_v(g, p):
                sp.dma_start(v_staged[p], m.arena[:, ds(g * (SEQ_TILES * 32) + V_AT, SEQ_TILES * 32)]).then_inc(v_in[p], 16)

            def store(g, p):
                sp.wait_ge(reduced, ring_of_close(g + 1, CLOSES - 1) + 4)
                sp.dma_start(m.arena[:, ds(g * (SEQ_TILES * GQ * HD) + O_AT, SEQ_TILES * GQ * HD)], o_staged[p]).then_inc(stored[p], 16)

            for p in range(2):
                load_rows(p, p)
                load_v(p, p)
            load_last_weights(sp, m, dram)
            with sp.Fori(0, GROUPS // 2 - 1) as t:
                for p in range(2):
                    sp.wait_ge(top_turned, t * 2 * TT + (p + 1) * TT)
                    load_rows(t * 2 + (2 + p), p)
                    sp.wait_ge(summed, t * 2 * BK + ((p + 1) * BK + 4))
                    load_v(t * 2 + (2 + p), p)
                    store(t * 2 + p, p)
            for p in range(2):
                store(GROUPS - 2 + p, p)
            for p in range(2):
                sp.wait_ge(stored[p], 16 * (GROUPS // 2 + 1))

        @block.tensor
        def _(pe):
            def turn_q(st):
                pe.wait_ge(top_kept, st.g * TT + (2 + st.at))
                for h in range(GQ):
                    at = st.i * ST_TILE + h * ROWS
                    last = pe.transpose(turn_bf[0:ROWS, h * P:(h + 1) * P], staged[st.p][:, at:at + ROWS], m.ident_bf)
                last.then_inc(top_turned, 1)

            def turn_k(g, p, q, half, first):
                if not first:
                    pe.wait_ge(top_kept, g * TT + half)
                if half == 0:
                    pe.wait_ge(staged_in[p], q * 16 + 16)
                for c in range(4):
                    at = (half * 4 + c) * ST_TILE + GQ * ROWS
                    last = pe.transpose(turn_bf[0:ROWS, c * P:(c + 1) * P], staged[p][:, at:at + ROWS], m.ident_bf)
                last.then_inc(top_turned, 1)

            def turn_mask(st):
                if not (isinstance(st.n, int) and st.n == 0):
                    pe.wait_ge(mask_kept, st.n)
                pe.wait_ge(minus_ready, st.n + 1)
                pe.wait_ge(mask_ready, st.n + 1)
                w = W[st.i].rearrange("p (h f r) -> p h f r", h=GQ, f=2)
                for h in range(GQ):
                    for f in range(1 + st.two):
                        last = pe.transpose(turn_bf[ROWS:KROWS, f * N + h * P:f * N + (h + 1) * P],
                                            w[:, h, f, 0:MASK_ROWS], m.ident_bf)
                last.then_inc(mask_turned, 1)

            def score(st, number):
                ring = ring_of_score(st, number)
                h, half = divmod(number, halves[st.i])
                k0, k1 = half * 512, min((st.i + 1) * P, (half + 1) * 512)
                bank = score_bank[bank_of_score(st, number)]
                diagonal = k1 == (st.i + 1) * P
                if h == 0 and half == 0:
                    pe.wait_ge(top_kept, st.g * TT + (3 + st.at))
                pe.wait_ge(reduced, ring + 1)
                last = pe.matmul(bank[:, 0:k1 - k0], query_aug[st.slot][0:ROWS, h * P:(h + 1) * P], key_aug[st.p][0:ROWS, k0:k1],
                                 start=True, stop=not diagonal)
                if diagonal:
                    last = pe.matmul(bank[:, k1 - k0 - P:k1 - k0], m.ident_bf, m.causal, start=False, stop=True)
                last.then_inc(scored, 1)

            def masked_score(st, j):
                u = back_at[st.at] + j
                bank = back_bank[u % 2]
                if j == 0:
                    pe.wait_ge(mask_kept, st.n + 1)
                pe.wait_ge(probs_ready, st.g * BK + (u + 1))
                f = int(st.two and j >= 4)
                extra = j == st.i or (j == st.i - 1 and st.i >= 2)
                last = pe.matmul(bank[:, :], key_aug[st.p][0:KROWS, j * P:(j + 1) * P], query_aug[st.slot][0:KROWS, f * N:(f + 1) * N],
                                 start=True, stop=not extra)
                if j == st.i:
                    last = pe.matmul(bank[:, :], m.causal, m.ident4, start=False, stop=True)
                elif extra:
                    pe.wait_ge(diag_ready, st.g * (SEQ_TILES - 2) + (drops_at[st.at] + 1))
                    last = pe.matmul(bank[:, :], m.own_chunk, chunk_diag[st.slot], start=False, stop=True)
                last.then_inc(masked_scored, 1)

            def weigh(st, j):
                u = back_at[st.at] + j
                if j == 0:
                    pe.wait_ge(ot_ready, st.n + 1)
                    if st.at == 0:
                        pe.wait_ge(v_in[st.p], st.q * 16 + 16)
                pe.wait_ge(probs_ready, st.g * BK + (u + 3))
                for h in range(GQ):
                    last = pe.matmul(sums[st.k % 2][32 * h:32 * h + 32, :], v_staged[st.p][:, j * 32:(j + 1) * 32],
                                     probs[u % 4][:, h * P:(h + 1) * P], start=j == 0, stop=j == st.i, tile_position=(0, 32 * h))
                last.then_inc(summed, 1)

            def close(t, u):
                steps, g, place = closing(t, u)
                ring = ring_of_close(g, place)
                pe.wait_ge(ot_ready, steps[-1].n + 3)
                pe.wait_ge(reduced, ring + 1)
                bank = score_bank[closed_bank(g, place)]
                for n, st in enumerate(steps):
                    last = pe.transpose(bank[:, n * P:(n + 1) * P], ot[st.slot], m.ident)
                last.then_inc(scored, 1)

            def body(t, u):
                for stage, st, n in schedule(t, u):
                    if stage == "turn_q":
                        turn_q(st)
                    elif stage == "turn_k":
                        turn_k(st.g, st.p, st.q, n, False)
                    elif stage == "turn_mask":
                        turn_mask(st)
                    elif stage == "score":
                        score(st, n)
                    elif stage == "masked":
                        masked_score(st, n)
                    elif stage == "weigh":
                        weigh(st, n)
                    elif stage == "close":
                        close(t, u)

            turn_k(0, 0, 0, 0, True)
            turn_k(0, 0, 0, 1, False)
            for k in range(2):
                turn_q(Step(0, k))
            over_units(pe, body)

        @block.scalar
        def _(act):
            act.sem_inc(probs_ready, 2)
            act.sem_inc(ot_ready, 2)

            def keep_k(g, p, half):
                act.wait_ge(top_turned, g * TT + (half + 1))
                act.activation(key_aug[p][0:ROWS, half * 512:(half + 1) * 512], turn_bf[0:ROWS, 0:N], ACT.Copy).then_inc(top_kept, 1)

            def keep_q(st):
                act.wait_ge(top_turned, st.g * TT + (3 + st.at))
                if st.two:
                    act.activation(query_aug[st.slot][0:ROWS, N:2 * N], turn_bf[0:ROWS, 0:N], ACT.Copy)
                act.activation(query_aug[st.slot][0:ROWS, 0:N], turn_bf[0:ROWS, 0:N], ACT.Copy).then_inc(top_kept, 1)

            def keep_mask(st):
                act.wait_ge(mask_turned, st.n + 1)
                n = (1 + st.two) * N
                act.activation(query_aug[st.slot][ROWS:KROWS, 0:n], turn_bf[ROWS:KROWS, 0:n], ACT.Copy).then_inc(mask_kept, 1)

            def exponent(st, j):
                u = back_at[st.at] + j
                act.wait_ge(masked_scored, st.g * BK + (u + 1))
                act.wait_ge(summed, st.g * BK + (u + 1))
                act.activation(probs[u % 4], back_bank[u % 2][:, :], ACT.Exp, scale=float(HD) ** -0.5).then_inc(probs_ready, 1)

            def keep_sums(st):
                act.wait_ge(summed, st.g * BK + (back_at[st.at + 1] + 4))
                act.activation(ot[st.slot], sums[st.k % 2], ACT.Copy).then_inc(ot_ready, 1)

            def body(t, u):
                for stage, st, n in schedule(t, u):
                    if stage == "turn_q":
                        keep_q(st)
                    elif stage == "turn_k":
                        keep_k(st.g, st.p, n)
                    elif stage == "turn_mask":
                        keep_mask(st)
                    elif stage == "masked":
                        exponent(st, n)
                    elif stage == "sums":
                        keep_sums(st)

            for half in range(2):
                keep_k(0, 0, half)
            for k in range(2):
                keep_q(Step(0, k))
            over_units(act, body)

        @block.vector
        def _(dve):
            dve.sem_inc(reduced, 3)
            dve.wait_ge(w_blank, 1)

            def finish(t, u):
                steps, g, place = closing(t, u)
                n, inv = len(steps), inverse[place]
                dve.wait_ge(scored, ring_of_close(g, place) + 1)
                x = score_bank[closed_bank(g, place)][:, 0:n * P].rearrange("p (h c) -> p h c", h=n * GQ)
                dve_seq.mark(dve.reciprocal(inv[:, 0:n * GQ].unsqueeze(2), x[:, :, HD:HD + 1]))
                if place == 0:
                    dve.wait_ge(stored[steps[0].p], steps[0].q * 16 + 16)
                dve_seq.wait(dve)
                for n, st in enumerate(steps):
                    at = st.i * GQ * HD
                    last = dve.tensor_tensor(out=o_staged[st.p][:, at:at + GQ * HD].rearrange("p (h d) -> p h d", h=GQ),
                                             in0=x[:, n * GQ:(n + 1) * GQ, 0:HD],
                                             in1=inv[:, n * GQ:(n + 1) * GQ].unsqueeze(2).to_broadcast([P, GQ, HD]), op=ALU.mult)
                last.then_inc(reduced, 1)

            def choose(front):
                p, p4 = front.k % 2, front.k % 4
                i = front.i
                n = (i + 1) * CPT
                cm, lf, tp = cmax[p], left[p], top[p4]
                if not (isinstance(front.n, int) and front.n < 4):
                    dve.wait_ge(minus_ready, front.n - 3)
                chunks = lambda x, h: x[:, h * 64:h * 64 + n]

                def reduce(h):
                    for half in range(halves[i]):
                        number = h * halves[i] + half
                        k0, k1 = half * 512, min((i + 1) * P, (half + 1) * 512)
                        dve.wait_ge(scored, ring_of_score(front, number) + 1)
                        dve.tensor_reduce(out=cm[:, h * 64 + k0 // CHUNK:h * 64 + k1 // CHUNK],
                                          in_=score_bank[bank_of_score(front, number)][:, 0:k1 - k0].rearrange("p (c d) -> p c d", d=CHUNK),
                                          axis=AXX, op=ALU.max).then_inc(reduced, 1)

                def best(h):
                    dve.wait_ge(reduced, ring_of_score(front, (h + 1) * halves[i]) + 3)
                    dve.sem_inc(m.turnstile, 1)
                    dve_seq.mark(dve.max(out=tp[:, h * TOPK:(h + 1) * TOPK], in_=chunks(cm, h)))

                def drop(h):
                    dve_seq.mark(dve.match_replace(out=chunks(lf, h), in_to_replace=tp[:, h * TOPK:(h + 1) * TOPK],
                                                   in_values=chunks(cm, h), imm_value=TAKEN))
                for h in range(GQ):
                    reduce(h)
                    if h >= 1:
                        best(h - 1)
                best(GQ - 1)
                dve_seq.wait(dve)
                dve.sem_inc(top_ready, 1)
                if i < 2:
                    dve.sem_inc(mask_ready, 1)
                    return
                for h in range(GQ):
                    drop(h)
                dve_seq.wait(dve)
                w = W[i].rearrange("p (h f r) -> p h f r", h=GQ, f=2)
                lh = lf.rearrange("p (h c) -> p h c", h=GQ)
                near = lh[:, :, (i - 1) * CPT:i * CPT]
                wide = lambda c: c.unsqueeze(1).to_broadcast([P, GQ, CPT])
                own3 = own[p4].rearrange("p (h c) -> p h c", h=GQ)
                dve_seq.mark(dve.scalar_tensor_tensor(out=own3, in0=near, scalar=1e38, in1=wide(m.chunk_own),
                                                      op0=ALU.is_lt, op1=ALU.mult))
                f, c = ((i - 1) - 1) // 3, ((i - 1) - 1) % 3 * CPT
                if i >= 3:
                    a = min(i - 2, 3) * CPT
                    dve.tensor_scalar(out=w[:, :, 0, 0:a], in0=lh[:, :, CPT:CPT + a], scalar1=1e38, scalar2=NEG,
                                      op0=ALU.is_lt, op1=ALU.mult)
                if i >= 6:
                    a = (i - 5) * CPT
                    dve.tensor_scalar(out=w[:, :, 1, 0:a], in0=lh[:, :, 4 * CPT:4 * CPT + a], scalar1=1e38, scalar2=NEG,
                                      op0=ALU.is_lt, op1=ALU.mult)
                dve_seq.wait(dve)
                if not (isinstance(front.n, int) and front.n < 4):
                    dve.wait_ge(minus_ready, front.n - 2)
                dve.tensor_reduce(out=own_dropped[p4].unsqueeze(2), in_=own3, axis=AXX, op=ALU.add).then_inc(own_ready, 1)
                dve.scalar_tensor_tensor(out=w[:, :, f, c:c + CPT], in0=near, scalar=1e38, in1=wide(m.chunk_before),
                                         op0=ALU.is_lt, op1=ALU.mult).then_inc(mask_ready, 1)

            def body(t, u):
                front = stages(t, u)[0]
                for st in front[:1]:
                    choose(st)
                if closing(t, u)[0]:
                    finish(t, u)
                for st in front[1:]:
                    choose(st)

            over_units(dve, body, dve_seq, PAIR * GQ + 2 * CLOSES + 2 * (SEQ_TILES - 2) * (GQ + 1))

        @block.gpsimd
        def _(pool):
            for i in range(SEQ_TILES):
                pool.memset(W[i], 0.0)
            pool.memset(one_row, 1.0)
            pool.memset(neg_one, -1.0).then_inc(w_blank, 1)
            pool.sem_inc(summed, 4)
            for p in range(2):
                pool.sem_inc(stored[p], 16)
            pool.wait_ge(w_blank, 1)

            def mask_parts(st):
                p, p4 = st.k % 2, st.k % 4
                pool.wait_ge(top_ready, st.n + 1)
                w = W[st.i].rearrange("p (h f r) -> p h f r", h=GQ, f=2)
                tp = top[p4].rearrange("p (h c) -> p h c", h=GQ)
                c = 3 * CPT
                both = lambda x: x.unsqueeze(2).unsqueeze(3).to_broadcast([P, GQ, 2, 1])
                slot = lambda n: w[:, :, :, c + n:c + n + 1]
                one = lambda n: w[:, :, 0, c + n:c + n + 1]
                mi, re = minus[p].unsqueeze(2), minus_rest[p].unsqueeze(2)
                minus1 = neg_one.unsqueeze(2)
                pool_seq.mark(pool.tensor_tensor(out=mi, in0=tp[:, :, 0:1], in1=minus1, op=ALU.mult))
                pool_seq.mark(pool.tensor_tensor(out=slot(0), in0=both(tp[:, :, 0]), in1=both(neg_one), op=ALU.mult))
                pool_seq.wait(pool)
                pool_seq.mark(pool.tensor_tensor(out=re, in0=mi, in1=one(0), op=ALU.subtract))
                pool_seq.wait(pool)
                pool_seq.mark(pool.tensor_tensor(out=slot(1), in0=both(minus_rest[p]), in1=both(one_row), op=ALU.mult))
                pool_seq.wait(pool)
                pool.tensor_tensor(out=slot(2), in0=both(minus_rest[p]), in1=w[:, :, :, c + 1:c + 2], op=ALU.subtract).then_inc(minus_ready, 1)
                if st.i >= 2:
                    pool.wait_ge(own_ready, st.g * (SEQ_TILES - 2) + (drops_at[st.at] + 1))
                    pool.sem_inc(m.turnstile, 1)
                    for h in range(GQ):
                        last = pool.tensor_scalar(out=chunk_diag[st.slot][:, h * P:(h + 1) * P], in0=m.ident_bf,
                                                  scalar1=own_dropped[p4][:, h:h + 1], scalar2=NEG, op0=ALU.mult, op1=ALU.mult)
                    last.then_inc(diag_ready, 1)

            def body(t, u):
                for st in stages(t, u)[0]:
                    mask_parts(st)

            over_units(pool, body, pool_seq, PAIR * 4)


def load_last_weights(sp, m, dram):
    kq = "p (c d) -> p c d"
    sp.dma_start(m.f32(WO_AT, DC * D).rearrange(kq, c=DC), dram["wo"].rearrange("(c p) d -> p c d", p=P)).then_inc(m.last_in, 16)
    sp.dma_start(m.f32(LA_AT, D), dram["lora_A"].rearrange("h r d -> (h r) d")).then_inc(m.last_in, 16)
    sp.dma_start(m.f32(WR_AT, D)[0:LORA_H, :], dram["Wr"]).then_inc(m.last_in, 16)
    sp.dma_start(m.f32(BR_AT, LORA_H)[0:1, :], dram["br"].rearrange("(a h) -> a h", a=1)).then_inc(m.last_in, 16)
    for oc in range(DC):
        sp.dma_start(m.f32(LB_AT + oc * P, P).rearrange("p (h r) -> p h r", h=LORA_H),
                     dram["lora_B"][:, oc * P:(oc + 1) * P, :].rearrange("h o r -> o h r")).then_inc(m.last_in, 16)


LAST_LOADS = 4 + DC
WO_AT = 38400
LA_AT, WR_AT, LB_AT, BR_AT = WO_AT + DC * D, WO_AT + (DC + 1) * D, WO_AT + (DC + 2) * D, WO_AT + (DC + 3) * D
WOT_AT = BR_AT + 16
LOW_N = LORA_H * LORA_R + LORA_H
LOWW_AT = WOT_AT + DC * D
LBT_AT = LOWW_AT + DC * LOW_N
LWORK = LBT_AT + D


def output(nc, m, s, dram):
    woT = m.f32(WOT_AT, DC * D)
    low_w = m.f32(LOWW_AT, DC * LOW_N).rearrange("p (c n) -> p c n", c=DC)
    take = m.taker(LWORK, ARENA)
    o_tile, oT = [take(D) for _ in range(2)], [take(D) for _ in range(2)]
    o_all = m.f32(O_AT, GROUPS * SEQ_TILES * GQ * HD).rearrange("p (b k t c) -> p b k t c", b=BATCH, k=KV, t=SEQ_TILES)
    w_turned, w_placed = s("e_w_turned"), s("e_w_placed")
    gathered, turned, oT_ready, y_ready = [s(f"e_gathered{b}") for b in range(2)], s("e_turned"), s("e_oT"), s("e_y")
    stats_ready, branch_rstd_ready, added = s("e_stats"), s("e_branch_rstd"), s("e_added")
    dve_seq, pool_seq = Count(s("e_dve_seq")), Count(s("e_pool_seq"))
    n_weights = DC + 3

    with nc.Block() as block:
        @block.sync
        def _(sp):
            with sp.Fori(0, SEQ_TILES) as i:
                for b in range(2):
                    sp.wait_ge(turned, i * 2 + b + 1)
                    sp.dma_start(o_tile[b].rearrange("p (k c) -> p k c", k=KV),
                                 o_all[:, b, :, ds(i, 1), :].squeeze(2)).then_inc(gathered[b], 16)

        @block.tensor
        def _(pe):
            def turn(i, b):
                pe.wait_ge(gathered[b], i * 16 + 16)
                for dc in range(DC):
                    last = pe.transpose(m.banks[b][:, dc * P:(dc + 1) * P], o_tile[b][:, dc * P:(dc + 1) * P], m.ident)
                last.then_inc(turned, 1)

            def feed(k, b):
                pe.wait_ge(oT_ready, k + 1)
                pe.wait_ge(added, k + 1)
                for dc in range(DC):
                    last = pe.matmul(m.banks[2 + b][:, :], oT[b][:, dc * P:(dc + 1) * P], woT[:, dc * D:(dc + 1) * D],
                                     start=dc == 0, stop=dc == DC - 1)
                last.then_inc(y_ready, 1)

            pe.wait_ge(m.last_in, 16 * LAST_LOADS)
            for c in range(n_weights):
                bank = m.banks[4 + c % 4]
                if c >= 4:
                    pe.wait_ge(w_placed, c - 3)
                for dc in range(DC):
                    if c < DC:
                        last = pe.transpose(bank[:, dc * P:(dc + 1) * P], m.f32(WO_AT + c * D + dc * P, P), m.ident)
                    elif c == DC:
                        last = pe.transpose(bank[:, dc * P:(dc + 1) * P], m.f32(LA_AT + dc * P, P), m.ident)
                    elif c == DC + 1:
                        last = pe.transpose(bank[:, dc * LORA_H:(dc + 1) * LORA_H], m.f32(WR_AT + dc * P, P)[0:LORA_H, :],
                                            m.ident[0:LORA_H, 0:LORA_H])
                    else:
                        last = pe.transpose(bank[:, dc * P:(dc + 1) * P], m.f32(LB_AT + dc * P, P), m.ident)
                last.then_inc(w_turned, 1)
            for b in range(2):
                turn(0, b)
            pe.wait_ge(w_placed, DC)
            with pe.Fori(0, SEQ_TILES - 1) as i:
                for b in range(2):
                    feed(i * 2 + b, b)
                for b in range(2):
                    turn(i + 1, b)
            for b in range(2):
                feed(TILES - 2 + b, b)

        @block.scalar
        def _(act):
            act.sem_inc(turned, 2)
            for c in range(n_weights):
                act.wait_ge(w_turned, c + 1)
                bank = m.banks[4 + c % 4]
                if c < DC:
                    out = woT.rearrange("p (c n) -> p c n", c=DC)[:, :, c * P:(c + 1) * P]
                    last = act.activation(out, bank.rearrange("p (c n) -> p c n", c=DC), ACT.Copy)
                elif c == DC:
                    last = act.activation(low_w[:, :, 0:P], bank.rearrange("p (c n) -> p c n", c=DC), ACT.Copy)
                elif c == DC + 1:
                    last = act.activation(low_w[:, :, P:LOW_N], bank[:, 0:DC * LORA_H].rearrange("p (c n) -> p c n", c=DC), ACT.Copy)
                else:
                    last = act.activation(m.f32(LBT_AT, D), bank[:, :], ACT.Copy)
                last.then_inc(w_placed, 1)
            with act.Fori(0, SEQ_TILES) as i:
                for b in range(2):
                    act.wait_ge(turned, i * 2 + b + 3)
                    act.activation(oT[b], m.banks[b][:, :], ACT.Copy).then_inc(oT_ready, 1)

        @block.vector
        def _(dve):
            dve.sem_inc(added, 2)
            with dve.Fori(0, SEQ_TILES) as i:
                dve_seq.enter(i, 2 * (1 + BRANCH_ADD_STEPS))
                for b in range(2):
                    dve.wait_ge(y_ready, i * 2 + b + 1)
                    branch_stats(dve, m, dve_seq, b, m.banks[2 + b][:, :]).then_inc(stats_ready, 1)
                for b in range(2):
                    dve.wait_ge(branch_rstd_ready, i * 2 + b + 1)
                    branch_add(dve, m, dve_seq, b, m.banks[2 + b][:, :], i + b * SEQ_TILES).then_inc(added, 1)
            dve_seq.leave(SEQ_TILES)

        @block.gpsimd
        def _(pool):
            with pool.Fori(0, SEQ_TILES) as i:
                pool_seq.enter(i, 2)
                for b in range(2):
                    pool.wait_ge(stats_ready, i * 2 + b + 1)
                    branch_rstd(pool, m, pool_seq, b).then_inc(branch_rstd_ready, 1)
            pool_seq.leave(SEQ_TILES)


def routed(nc, m, s, dram):
    low_w = m.f32(LOWW_AT, DC * LOW_N)
    take = m.taker(LWORK, ARENA)
    xn, xT = [take(D) for _ in range(2)], [take(D) for _ in range(2)]
    ls, lsT = [take(P) for _ in range(2)], [take(P) for _ in range(2)]
    peak, total, share = [take(1) for _ in range(2)], [take(1) for _ in range(2)], [take(1) for _ in range(2)]
    e, score = [take(LORA_H) for _ in range(2)], [take(LORA_H) for _ in range(2)]
    ones = take(P)[0:1, :]
    rstd_ready, xn_ready, turned, xT_ready = s("f_rstd"), s("f_xn"), s("f_turned"), s("f_xT")
    low_ready, peak_ready, e_ready, ls_ready = s("f_low"), s("f_peak"), s("f_e"), s("f_ls")
    ls_turned, lsT_ready, y_ready = s("f_ls_turned"), s("f_lsT"), s("f_y")
    stats_ready, branch_rstd_ready, added = s("f_stats"), s("f_branch_rstd"), s("f_added")
    stored = s("f_stored")
    dve_seq, pool_seq = Count(s("f_dve_seq")), Count(s("f_pool_seq"))
    LR = LORA_H * LORA_R
    branch_scale = float(LORA_H * 2)

    def over_pairs(eng, body, seq=None, per=0):
        with eng.Fori(0, TILES // 2 - 1) as u:
            if seq:
                seq.enter(u, per)
            body(u, False)
        if seq:
            seq.leave(TILES // 2 - 1)
        body(TILES // 2 - 1, True)

    with nc.Block() as block:
        @block.sync
        def _(sp):
            with sp.Fori(0, TILES) as k:
                sp.wait_ge(added, k + 3)
                sp.dma_start(dram["out"][ds(k * P, P), :], m.x(k)).then_inc(stored, 16)
            sp.wait_ge(stored, 16 * TILES)

        @block.tensor
        def _(pe):
            def turn(k, p):
                pe.wait_ge(xn_ready, k + 1)
                for dc in range(DC):
                    last = pe.transpose(m.banks[p][:, dc * P:(dc + 1) * P], xn[p][:, dc * P:(dc + 1) * P], m.ident)
                last.then_inc(turned, 1)

            def body(u, last_pair):
                for p in range(2):
                    pe.wait_ge(xT_ready, u * 2 + (p + 1))
                    pe.wait_ge(ls_ready, u * 2 + (p + 1))
                    for dc in range(DC):
                        pe.matmul(m.banks[2 + p][:, 0:LOW_N], xT[p][:, dc * P:(dc + 1) * P], low_w[:, dc * LOW_N:(dc + 1) * LOW_N],
                                  start=dc == 0, stop=False)
                    pe.matmul(m.banks[2 + p][:, LR:LOW_N], ones, m.f32(BR_AT, LORA_H)[0:1, :], start=False, stop=True).then_inc(low_ready, 1)
                if not last_pair:
                    for p in range(2):
                        turn(u * 2 + (2 + p), p)
                for p in range(2):
                    pe.wait_ge(ls_ready, u * 2 + (p + 3))
                    pe.transpose(m.banks[4 + p][:, 0:LR], ls[p], m.ident).then_inc(ls_turned, 1)
                for p in range(2):
                    pe.wait_ge(lsT_ready, u * 2 + (p + 1))
                    pe.wait_ge(added, u * 2 + (p + 1))
                    pe.matmul(m.banks[6 + p][:, :], lsT[p], m.f32(LBT_AT, D), start=True, stop=True).then_inc(y_ready, 1)

            for p in range(2):
                turn(p, p)
            over_pairs(pe, body)

        @block.scalar
        def _(act):
            def normed(k, p):
                act.activation(xn[p], m.x(k), ACT.Identity, bias=m.shift[:, ds(k, 1)],
                               scale=m.rstd[:, ds(k, 1)]).then_inc(xn_ready, 1)

            def keep(k, p):
                act.wait_ge(turned, k + 1)
                act.activation(xT[p], m.banks[p][:, :], ACT.Copy).then_inc(xT_ready, 1)

            def body(u, last_pair):
                if not last_pair:
                    for p in range(2):
                        normed(u * 2 + (2 + p), p)
                for p in range(2):
                    act.wait_ge(peak_ready, u * 2 + (p + 1))
                    act.activation(e[p], m.banks[2 + p][:, LR:LOW_N], ACT.Exp, bias=peak[p], accum_out=total[p]).then_inc(e_ready, 1)
                if not last_pair:
                    for p in range(2):
                        keep(u * 2 + (2 + p), p)
                for p in range(2):
                    act.wait_ge(ls_turned, u * 2 + (p + 1))
                    act.activation(lsT[p], m.banks[4 + p][:, 0:LR], ACT.Copy).then_inc(lsT_ready, 1)

            act.wait_ge(rstd_ready, 1)
            for p in range(2):
                normed(p, p)
            for p in range(2):
                keep(p, p)
            over_pairs(act, body)

        @block.vector
        def _(dve):
            dve.sem_inc(added, 2)
            dve.sem_inc(ls_ready, 2)

            def body(u, _):
                for p in range(2):
                    dve.wait_ge(low_ready, u * 2 + (p + 1))
                    dve.tensor_reduce(out=peak[p], in_=m.banks[2 + p][:, LR:LOW_N], axis=AXX, op=ALU.max, negate=True).then_inc(peak_ready, 1)
                for p in range(2):
                    dve.wait_ge(e_ready, u * 2 + (p + 1))
                    dve_seq.mark(dve.reciprocal(share[p], total[p]))
                    dve_seq.wait(dve)
                    dve_seq.mark(dve.tensor_scalar(out=score[p], in0=e[p], scalar1=share[p], scalar2=branch_scale, op0=ALU.mult, op1=ALU.mult))
                    dve_seq.wait(dve)
                    dve.tensor_tensor(out=ls[p].rearrange("p (h r) -> p h r", h=LORA_H), in0=m.banks[2 + p][:, 0:LR].rearrange("p (h r) -> p h r", h=LORA_H),
                                      in1=score[p].unsqueeze(2).to_broadcast([P, LORA_H, LORA_R]), op=ALU.mult).then_inc(ls_ready, 1)
                for p in range(2):
                    dve.wait_ge(y_ready, u * 2 + (p + 1))
                    branch_stats(dve, m, dve_seq, p, m.banks[6 + p][:, :]).then_inc(stats_ready, 1)
                for p in range(2):
                    dve.wait_ge(branch_rstd_ready, u * 2 + (p + 1))
                    branch_add(dve, m, dve_seq, p, m.banks[6 + p][:, :], u * 2 + p, last=True).then_inc(added, 1)
            over_pairs(dve, body, dve_seq, 2 * 5)

        @block.gpsimd
        def _(pool):
            pool.memset(ones, 1.0)
            rstd_all(pool, m, pool_seq).then_inc(rstd_ready, 1)
            pool_seq.settle()

            def body(u, _):
                for p in range(2):
                    pool.wait_ge(stats_ready, u * 2 + (p + 1))
                    branch_rstd(pool, m, pool_seq, p).then_inc(branch_rstd_ready, 1)
            over_pairs(pool, body, pool_seq, 2)




def program(nc, dram, phases=99):
    with ExitStack() as ctx:
        m = Mem(nc, ctx)
        stages = [setup_and_sparse, weights, gated, project, attention, output, routed]
        for stage in stages[:phases]:
            stage(nc, m, m.sem, dram)


def shape_constants():
    c = np.zeros((P, 6 * P), np.float32)
    row, col = np.arange(P)[:, None], np.arange(P)[None, :]
    c[:, 0:P] = row == col
    c[:, P:2 * P] = np.where(col > row, np.float32(NEG), np.float32(0))
    c[:, 2 * P:3 * P] = (row // CHUNK == col // CHUNK) & (col <= row)
    inv = np.float32(1.0) / np.float32(10000.0) ** (np.arange(0, HD, 2, dtype=np.float32) / np.float32(HD))
    freq = np.arange(SEQ, dtype=np.float32)[:, None] * inv[None, :].astype(np.float32)
    emb = np.concatenate([freq, freq], 1).astype(np.float32)
    sin = np.sin(emb).astype(np.float32)
    sin[:, :HD // 2] *= -1
    lay = lambda t: t.reshape(SEQ_TILES, P, HD).transpose(1, 0, 2).reshape(P, SEQ_TILES * HD)
    c[:, 3 * P:4 * P] = lay(np.cos(emb).astype(np.float32))
    c[:, 4 * P:5 * P] = lay(sin)
    ch = np.arange(CPT)[None, :]
    c[:, 5 * P:5 * P + CPT] = np.where(ch < row // CHUNK, np.float32(NEG), np.float32(0))
    c[:, 5 * P + CPT:5 * P + 2 * CPT] = ch == row // CHUNK
    k = np.zeros((MASK_ROWS, SEQ), np.float32)
    for j in range(1, SEQ_TILES - 1):
        for ch in range(CPT):
            k[(j - 1) % 3 * CPT + ch, j * P + ch * CHUNK:j * P + (ch + 1) * CHUNK] = 1
    k[3 * CPT:, :] = 1
    return c, k


_NAMES = {"x": "L0_attn_x", "w1": "L0_attn_w1", "w2": "L0_attn_w2", "b2": "L0_attn_b2", "mask": "L0_attn_sparse_mask",
          "gate_q": "L0_ffn_gate_q", "gate_scale": "L0_ffn_gate_scale", "gate_A": "L0_ffn_gate_A", "gate_B": "L0_ffn_gate_B",
          "up_q": "L0_ffn_up_q", "up_scale": "L0_ffn_up_scale", "up_A": "L0_ffn_up_A", "up_B": "L0_ffn_up_B",
          "down_q": "L0_ffn_down_q", "down_scale": "L0_ffn_down_scale", "down_A": "L0_ffn_down_A", "down_B": "L0_ffn_down_B",
          "wq": "L1_attn_wq", "wk": "L1_attn_wk", "wv": "L1_attn_wv", "wo": "L1_attn_wo",
          "lora_A": "L1_ffn_A", "lora_B": "L1_ffn_B", "Wr": "L1_ffn_Wr", "br": "L1_ffn_br"}


def kernel(**inputs):
    import concourse.bacc as bacc
    from concourse.bass_utils import run_bass_kernel_spmd

    nc = bacc.Bacc("TRN2", target_bir_lowering=False, num_devices=1)
    consts, key_rows = shape_constants()
    arrays = {"consts": consts, "key_rows": key_rows}
    arrays |= {short: np.ascontiguousarray(inputs[name]) for short, name in _NAMES.items()}
    arrays["x"] = arrays["x"].reshape(BATCH * SEQ, D)
    dram = {n: nc.dram_tensor(f"in_{n}", a.shape, mybir.dt.from_np(a.dtype), kind="ExternalInput").ap()
            for n, a in arrays.items()}
    dram["rows"] = nc.dram_tensor("qk_rows", (GROUPS, P, ST_W), BF16).ap()
    dram["out"] = nc.dram_tensor("out", (BATCH * SEQ, D), F32, kind="ExternalOutput").ap()
    program(nc, dram)
    r = run_bass_kernel_spmd(nc, [{f"in_{n}": a for n, a in arrays.items()}], core_ids=[0])
    return r.results[0]["out"].reshape(BATCH, SEQ, D)
```

```python
from contextlib import ExitStack

import numpy as np

import concourse.bass as bass
from concourse import mybir

F32 = mybir.dt.float32
BF16 = mybir.dt.bfloat16
F16 = mybir.dt.float16
I32 = mybir.dt.int32
ALU = mybir.AluOpType
ACT = mybir.ActivationFunctionType
AXX = mybir.AxisListType.X
ds = bass.ds

P = 128
BATCH, SEQ, D = 2, 1024, 512
TILES = BATCH * SEQ // P
SEQ_TILES = SEQ // P
DC = D // P
INNER = 1376
IT = (INNER + P - 1) // P
I_LAST = INNER - (IT - 1) * P
RANK = 32
Q_ZERO, Q_STEP, LR_SCALE = 7.5, 0.005, 0.02
HEADS, KV, HD = 32, 8, 16
GQ = HEADS // KV
CHUNK = 16
CPT = P // CHUNK
TOPK = 8
PARTS = 3
ROWS = 6 * HD
LORA_H, LORA_R = 8, 16
EPS = 1e-5
NEG = -float(2.0 ** 100)
TAKEN = 3e38
QK = (HEADS + KV) * HD
QKV = QK + KV * HD
GROUPS = BATCH * KV
ST_TILE = (GQ + 1) * ROWS
ST_W = SEQ_TILES * ST_TILE
MASK_ROWS = 3 * CPT + PARTS
KROWS = ROWS + MASK_ROWS

X_AT = 0
CONST_AT = X_AT + TILES * D
REG = CONST_AT + 1152
SLOT = IT * D
UPQ_AT, DOWNQ_AT, GATEQ_AT, WG_AT = REG, REG + SLOT, REG + 2 * SLOT, REG + 3 * SLOT
WD_AT, HT_AT = UPQ_AT, DOWNQ_AT
WU_AT = WG_AT + DC * INNER // 2
ATTN0_AT = WG_AT + DC * INNER
WQKV_AT = ATTN0_AT + DC * D
WORK = WQKV_AT + DC * QKV
V_AT = REG
O_AT = V_AT + GROUPS * SEQ_TILES * 32
CWORK = O_AT + GROUPS * SEQ_TILES * GQ * HD
ARENA = 53100


class Count:

    def __init__(self, sem):
        self.sem, self.total, self.base, self.n = sem, 0, 0, 0

    def enter(self, i, per):
        self.base, self.n, self.per = i * per + self.total, 0, per

    def leave(self, turns):
        assert self.n == self.per, (self.n, self.per)
        self.total += turns * self.per
        self.base, self.n = self.total, 0

    def settle(self):
        self.total, self.base, self.n = self.base + self.n, self.base + self.n, 0

    def mark(self, ins):
        ins.then_inc(self.sem, 1)
        self.n += 1

    def wait(self, eng):
        eng.wait_ge(self.sem, self.base + self.n)

    def wait_apart(self, eng, turnstile):
        self.wait(eng)
        eng.sem_inc(turnstile, 1)


class Mem:

    def __init__(self, nc, ctx):
        self.nc, self.ctx = nc, ctx
        self.arena = ctx.enter_context(nc.sbuf_tensor("arena", [P, ARENA], F32))
        self.banks = [ctx.enter_context(nc.psum_tensor(f"bank{i}", [P, 512], F32)) for i in range(8)]
        self.turnstile, self.last_in = self.sem("turnstile"), self.sem("last_in")
        c = CONST_AT
        self.ident = self.f32(c, P); c += P
        self.causal = self.bf16(c, P); c += P // 2
        self.own_chunk = self.bf16(c, P); c += P // 2
        self.ident_bf = self.bf16(c, P); c += P // 2
        self.ident4 = self.bf16(c, 4 * P); c += 2 * P
        self.chunk_before = self.f32(c, CPT); c += CPT
        self.chunk_own = self.f32(c, CPT); c += CPT
        self.cos = self.f32(c, SEQ_TILES * HD); c += SEQ_TILES * HD
        self.sin = self.f32(c, SEQ_TILES * HD); c += SEQ_TILES * HD
        self.eps = self.f32(c, TILES); c += TILES
        self.half = self.f32(c, TILES); c += TILES
        self.mv_next = self.f32(c, 2 * TILES); c += 2 * TILES
        self.rstd = self.f32(c, TILES); c += TILES
        self.shift = self.f32(c, TILES); c += TILES
        self.scales = self.f32(c, 2 * IT + DC); c += 2 * IT + DC
        self.zero16 = self.f32(c, TILES); c += TILES
        self.ve16 = self.f32(c, TILES); c += TILES
        self.stats = [self.f32(c + 6 * i, 6) for i in range(2)]; c += 12
        self.mv = [self.f32(c + 2 * i, 2) for i in range(2)]; c += 4
        self.ve = [self.f32(c + i, 1) for i in range(2)]; c += 2
        self.rs = [self.f32(c + i, 1) for i in range(2)]; c += 2
        self.ms = [self.f32(c + i, 1) for i in range(2)]; c += 2
        self.stats_x = [self.f32(c + 6 * i, 6) for i in range(2)]; c += 12
        self.mv_x = [self.f32(c + 2 * i, 2) for i in range(2)]; c += 4
        assert c <= REG, c - CONST_AT
        self.key_aug = [self.bf16(ARENA - (2 - i) * SEQ // 2, SEQ) for i in range(2)]

    def f32(self, at, n):
        return self.arena[:, at:at + n]

    def bf16(self, at, n):
        return self.arena[:, at:at + (n + 1) // 2].bitcast(BF16)[:, 0:n]

    def f16(self, at, n):
        return self.arena[:, at:at + (n + 1) // 2].bitcast(F16)[:, 0:n]

    def i32(self, at, n):
        return self.arena[:, at:at + n].bitcast(I32)

    def x(self, tile):
        return self.arena[:, ds(tile * D + X_AT, D)]

    def taker(self, at, limit):
        place = [at]

        def take(n, dtype=F32):
            words = n if dtype == F32 else (n + 1) // 2
            view = {F32: self.f32, BF16: self.bf16, F16: self.f16}[dtype](place[0], n)
            place[0] += words
            assert place[0] <= limit, place[0]
            return view
        return take

    def sem(self, name):
        return self.ctx.enter_context(self.nc.semaphore(name))


def rstd_all(pool, m, seq, a=0, b=TILES):
    mv = m.mv_next.rearrange("p (t s) -> p t s", s=2)[:, a:b]
    rstd, shift, scaled_mean = m.rstd[:, a:b], m.shift[:, a:b], m.ve16[:, a:b]
    seq.mark(pool.tensor_tensor(out=rstd, in0=mv[:, :, 1], in1=m.eps[:, a:b], op=ALU.add))
    seq.wait(pool)
    seq.mark(pool.tensor_tensor(out=shift, in0=rstd, in1=m.half[:, a:b], op=ALU.pow))
    seq.wait(pool)
    seq.mark(pool.tensor_copy(rstd, shift))
    seq.wait(pool)
    seq.mark(pool.tensor_tensor(out=scaled_mean, in0=mv[:, :, 0], in1=rstd, op=ALU.mult))
    seq.wait(pool)
    return pool.tensor_tensor(out=shift, in0=m.zero16[:, a:b], in1=scaled_mean, op=ALU.subtract)


def branch_stats(dve, m, seq, p, y):
    seq.mark(dve.bn_stats(out=m.stats[p], in_=y))
    seq.wait_apart(dve, m.turnstile)
    return dve.bn_aggr(out=m.mv[p], in_=m.stats[p])


def branch_rstd(pool, m, seq, p):
    seq.mark(pool.tensor_tensor(out=m.ve[p], in0=m.mv[p][:, 1:2], in1=m.eps[:, 0:1], op=ALU.add))
    seq.wait(pool)
    return pool.tensor_tensor(out=m.rs[p], in0=m.ve[p], in1=m.half[:, 0:1], op=ALU.pow)


def branch_add(dve, m, seq, p, y, tile, last=False):
    x = m.x(tile)
    seq.mark(dve.scalar_tensor_tensor(out=m.ms[p], in0=m.mv[p][:, 0:1], scalar=-1.0, in1=m.rs[p],
                                      op0=ALU.mult, op1=ALU.mult))
    seq.mark(dve.scalar_tensor_tensor(out=x, in0=y, scalar=m.rs[p], in1=x, op0=ALU.mult, op1=ALU.add))
    seq.wait(dve)
    if last:
        return dve.tensor_scalar(out=x, in0=x, scalar1=m.ms[p], scalar2=None, op0=ALU.add)
    seq.mark(dve.tensor_scalar(out=x, in0=x, scalar1=m.ms[p], scalar2=None, op0=ALU.add))
    seq.wait_apart(dve, m.turnstile)
    seq.mark(dve.bn_stats(out=m.stats_x[p], in_=x))
    seq.wait_apart(dve, m.turnstile)
    seq.mark(dve.bn_aggr(out=m.mv_x[p], in_=m.stats_x[p]))
    seq.wait(dve)
    return dve.tensor_copy(m.mv_next[:, ds(tile * 2, 2)], m.mv_x[p])


BRANCH_ADD_STEPS = 5


def setup_and_sparse(nc, m, s, dram):
    W2, W2T = m.f32(GATEQ_AT, DC * D), m.f32(GATEQ_AT + 2048, DC * D)
    W1, MASK = m.f32(GATEQ_AT + 4096, DC * D), m.f32(GATEQ_AT + 6144, DC * D)
    attn0 = m.f32(ATTN0_AT, DC * D)
    B_ROWS = 65
    b2, b2_rest = m.f32(UP_LOW_AT, D)[0:B_ROWS, :], m.f32(UP_LOW_AT + D, D)[0:B_ROWS, :]
    b2_parts, ones = m.bf16(UP_LOW_AT + 2 * D, D)[0:B_ROWS, :], m.bf16(UP_LOW_AT + 3 * D, P)[0:B_ROWS, :]
    a = WORK
    xn = [m.f32(a + i * D, D) for i in range(2)]
    xT = [m.f32(a + (2 + i) * D, D) for i in range(2)]
    y = [m.f32(a + (4 + i) * D, D) for i in range(2)]
    cst = m.f32(a + 6 * D, 6 * P)
    kq = "p (c d) -> p c d"

    weights_in = [s("w2_in"), s("w1_in"), s("mask_in")]
    b2_blank, b2_in, b2_ready = s("b2_blank"), s("b2_in"), s("b2_ready")
    consts_in, x_in = s("consts_in"), [s(f"x_in{i}") for i in range(4)]
    m.q_in = [s("gate_q_in"), s("up_q_in"), s("down_q_in"), s("lowrank_in"), s("qkv_in")]
    consts_ready, w2_turned, w2T_ready = s("consts_ready"), s("w2_turned"), s("w2T_ready")
    raw_ready, attn0_ready = s("raw_ready"), s("attn0_ready")
    x_stats, rstd_ready = s("x_stats"), s("rstd_ready")
    xn_ready, turned, xT_ready = s("a_xn_ready"), s("a_turned"), s("a_xT_ready")
    y_ready, gelu_ready = s("a_y_ready"), s("a_gelu_ready")
    stats_ready, branch_rstd_ready, added = s("a_stats_ready"), s("a_branch_rstd"), s("a_added")
    dve_seq, pool_seq = Count(s("a_dve_seq")), Count(s("a_pool_seq"))

    with nc.Block() as block:
        @block.sync
        def _(sp):
            sp.dma_start(W2.rearrange(kq, c=DC), dram["w2"].rearrange("(c p) d -> p c d", p=P)).then_inc(weights_in[0], 16)
            sp.dma_start(cst, dram["consts"][:, 0:6 * P]).then_inc(consts_in, 16)
            sp.dma_start(W1.rearrange(kq, c=DC), dram["w1"].rearrange("(c p) d -> p c d", p=P)).then_inc(weights_in[1], 16)
            sp.dma_start(m.f32(X_AT, 4 * D).rearrange(kq, c=4),
                         dram["x"][0:4 * P, :].rearrange("(c p) d -> p c d", p=P)).then_inc(x_in[0], 16)
            sp.dma_start(MASK.rearrange(kq, c=DC), dram["mask"].rearrange("(c p) d -> p c d", p=P)).then_inc(weights_in[2], 16)
            sp.wait_ge(b2_blank, 1)
            for row in (0, 32, 64):
                sp.dma_start(b2[row:row + 1, :], dram["b2"].rearrange("(a d) -> a d", a=1)).then_inc(b2_in, 16)
            for c in range(1, 4):
                sp.dma_start(m.f32(X_AT + c * 4 * D, 4 * D).rearrange(kq, c=4),
                             dram["x"][c * 4 * P:(c + 1) * 4 * P, :].rearrange("(c p) d -> p c d", p=P)).then_inc(x_in[c], 16)
            full = (IT - 1) * P
            sp.dma_start(m.i32(UPQ_AT, (IT - 1) * D).rearrange(kq, c=IT - 1),
                         dram["up_q"][0:full, :].rearrange("(c p) d -> p c d", p=P)).then_inc(m.q_in[1], 16)
            sp.dma_start(m.i32(UPQ_AT + (IT - 1) * D, D)[0:I_LAST, :], dram["up_q"][full:INNER, :]).then_inc(m.q_in[1], 16)
            sp.dma_start(m.i32(DOWNQ_AT, DC * INNER).rearrange(kq, c=DC),
                         dram["down_q"].rearrange("(c p) i -> p c i", p=P)).then_inc(m.q_in[2], 16)
            sp.wait_ge(attn0_ready, DC)
            sp.dma_start(m.i32(GATEQ_AT, (IT - 1) * D).rearrange(kq, c=IT - 1),
                         dram["gate_q"][0:full, :].rearrange("(c p) d -> p c d", p=P)).then_inc(m.q_in[0], 16)
            sp.dma_start(m.i32(GATEQ_AT + (IT - 1) * D, D)[0:I_LAST, :], dram["gate_q"][full:INNER, :]).then_inc(m.q_in[0], 16)
            load_small_weights(sp, m, dram)

        @block.gpsimd
        def _(pool):
            pool.memset(b2, 0.0).then_inc(b2_blank, 1)
            pool.memset(m.eps, EPS)
            pool.memset(m.half, -0.5)
            pool.memset(m.zero16, 0.0)
            pool.memset(ones, 1.0).then_inc(consts_ready, 1)
            pool.wait_ge(consts_in, 16)
            pool.wait_ge(consts_ready, 1)
            pool.tensor_copy(m.ident, cst[:, 0:P]).then_inc(consts_ready, 1)
            pool.tensor_copy(m.ident_bf, cst[:, 0:P])
            for h in range(4):
                pool.tensor_copy(m.ident4[:, h * P:(h + 1) * P], cst[:, 0:P])
            pool.tensor_copy(m.causal, cst[:, P:2 * P])
            pool.tensor_copy(m.own_chunk, cst[:, 2 * P:3 * P])
            pool.tensor_copy(m.cos, cst[:, 3 * P:4 * P])
            pool.tensor_copy(m.sin, cst[:, 4 * P:5 * P])
            pool.tensor_copy(m.chunk_before, cst[:, 5 * P:5 * P + CPT])
            pool.tensor_copy(m.chunk_own, cst[:, 5 * P + CPT:5 * P + 2 * CPT]).then_inc(consts_ready, 1)
            for first, end in ((0, 4), (4, TILES)):
                pool.wait_ge(x_stats, end)
                rstd_all(pool, m, pool_seq, first, end).then_inc(rstd_ready, 1)
            pool_seq.settle()
            with pool.Fori(0, TILES // 2) as u:
                pool_seq.enter(u, 2)
                for p in range(2):
                    pool.wait_ge(stats_ready, u * 2 + p + 1)
                    branch_rstd(pool, m, pool_seq, p).then_inc(branch_rstd_ready, 1)
            pool_seq.leave(TILES // 2)

        @block.tensor
        def _(pe):
            pe.wait_ge(weights_in[0], 16)
            pe.wait_ge(consts_ready, 2)
            for dc in range(DC):
                for tc in range(DC):
                    last = pe.transpose(m.banks[dc][:, tc * P:(tc + 1) * P], W2[:, tc * D + dc * P:tc * D + (dc + 1) * P], m.ident)
                last.then_inc(w2_turned, 1)
            pe.wait_ge(weights_in[1], 16)
            for sc in range(DC):
                for dc in range(DC):
                    if sc == 0:
                        pe.wait_ge(w2T_ready, dc + 1)
                    last = pe.matmul(m.banks[4 + sc][:, :], W1[:, dc * D + sc * P:dc * D + (sc + 1) * P],
                                     W2T[:, dc * D:(dc + 1) * D], start=dc == 0, stop=dc == DC - 1)
                last.then_inc(raw_ready, 1)

            def turn(k, p):
                pe.wait_ge(xn_ready, k * 1 + 1)
                for dc in range(DC):
                    last = pe.transpose(m.banks[p][:, dc * P:(dc + 1) * P], xn[p][:, dc * P:(dc + 1) * P], m.ident)
                last.then_inc(turned, 1)

            def feed(k, p):
                pe.wait_ge(xT_ready, k + 1)
                pe.wait_ge(gelu_ready, k + 1)
                pe.matmul(m.banks[2 + p][:, :], ones, b2_parts, start=True, stop=False)
                for dc in range(DC):
                    last = pe.matmul(m.banks[2 + p][:, :], xT[p][:, dc * P:(dc + 1) * P], attn0[:, dc * D:(dc + 1) * D],
                                     start=False, stop=dc == DC - 1)
                last.then_inc(y_ready, 1)

            for p in range(2):
                turn(p, p)
            pe.wait_ge(attn0_ready, DC)
            pe.wait_ge(b2_ready, 1)
            with pe.Fori(0, TILES // 2 - 1) as u:
                for p in range(2):
                    feed(u * 2 + p, p)
                for p in range(2):
                    turn(u * 2 + (2 + p), p)
            for p in range(2):
                feed(TILES - 2 + p, p)

        @block.scalar
        def _(act):
            act.sem_inc(gelu_ready, 2)
            for dc in range(DC):
                act.wait_ge(w2_turned, dc + 1)
                act.activation(W2T[:, dc * D:(dc + 1) * D], m.banks[dc][:, :], ACT.Copy).then_inc(w2T_ready, 1)

            def normed(k, p):
                act.activation(xn[p], m.x(k), ACT.Identity, bias=m.shift[:, ds(k, 1)],
                               scale=m.rstd[:, ds(k, 1)]).then_inc(xn_ready, 1)

            def keep(k, p):
                act.wait_ge(turned, k + 1)
                act.activation(xT[p], m.banks[p][:, :], ACT.Copy).then_inc(xT_ready, 1)

            def gelu(k, p):
                act.wait_ge(y_ready, k + 1)
                act.wait_ge(added, k + 1)
                act.activation(y[p], m.banks[2 + p][:, :], ACT.Gelu).then_inc(gelu_ready, 1)

            act.wait_ge(rstd_ready, 1)
            for p in range(2):
                normed(p, p)
            for p in range(2):
                keep(p, p)

            def pair(u):
                for p in range(2):
                    normed(u * 2 + (2 + p), p)
                for p in range(2):
                    gelu(u * 2 + p, p)
                for p in range(2):
                    keep(u * 2 + (2 + p), p)

            pair(0)
            act.wait_ge(rstd_ready, 2)
            with act.Fori(1, TILES // 2 - 1) as u:
                pair(u)
            for p in range(2):
                gelu(TILES - 2 + p, p)

        @block.vector
        def _(dve):
            dve.sem_inc(added, 2)
            dve.wait_ge(b2_in, 48)
            two, three = slice(32, 64), slice(64, 65)
            dve_seq.mark(dve.tensor_copy(b2_parts, b2))
            dve_seq.wait(dve)
            dve_seq.mark(dve.tensor_tensor(out=b2_rest, in0=b2, in1=b2_parts, op=ALU.subtract))
            dve_seq.wait(dve)
            dve.tensor_copy(b2_parts[two, :], b2_rest[two, :])
            dve_seq.mark(dve.tensor_copy(b2_parts[three, :], b2_rest[three, :]))
            dve_seq.wait(dve)
            dve.tensor_tensor(out=b2_parts[three, :], in0=b2_rest[three, :], in1=b2_parts[three, :], op=ALU.subtract).then_inc(b2_ready, 1)
            for sc in range(DC):
                if sc == 0:
                    dve.wait_ge(weights_in[2], 16)
                dve.wait_ge(raw_ready, sc + 1)
                dve.tensor_tensor(out=attn0[:, sc * D:(sc + 1) * D], in0=m.banks[4 + sc][:, :],
                                  in1=MASK[:, sc * D:(sc + 1) * D], op=ALU.mult).then_inc(attn0_ready, 1)
            st16 = m.f32(a + 8 * D, 6 * TILES)
            for t in range(TILES):
                if t % 4 == 0:
                    dve.wait_ge(x_in[t // 4], 16)
                dve_seq.mark(dve.bn_stats(out=st16[:, 6 * t:6 * t + 6], in_=m.x(t)))
                if t % 4 == 3:
                    dve_seq.wait(dve)
                    for c in range(t - 3, t + 1):
                        dve.bn_aggr(out=m.mv_next[:, 2 * c:2 * c + 2], in_=st16[:, 6 * c:6 * c + 6]).then_inc(x_stats, 1)
            dve_seq.settle()
            with dve.Fori(0, TILES // 2) as u:
                dve_seq.enter(u, 2 * (1 + BRANCH_ADD_STEPS))
                for p in range(2):
                    dve.wait_ge(gelu_ready, u * 2 + (p + 3))
                    branch_stats(dve, m, dve_seq, p, y[p]).then_inc(stats_ready, 1)
                for p in range(2):
                    dve.wait_ge(branch_rstd_ready, u * 2 + p + 1)
                    branch_add(dve, m, dve_seq, p, y[p], u * 2 + p).then_inc(added, 1)
            dve_seq.leave(TILES // 2)


LOW_AT = WORK + 4864
GB_AT, UB_AT, DB_AT = LOW_AT, LOW_AT + INNER, LOW_AT + 2 * INNER
GA_AT = DB_AT + D
UA_AT, DA_AT = GA_AT + DC * RANK, GA_AT + 2 * DC * RANK
WQ_AT = DA_AT + IT * RANK
DEQ_AT, DOWN_SCALE_AT, CENTRED_AT = WORK, WQ_AT + 6 * D, WQ_AT + 7 * D
TRIPLE = 3 * RANK
LOW_WORDS = INNER
GATE_LOW_AT, BOTH_A_AT, UP_LOW_AT = ATTN0_AT, ATTN0_AT + INNER, WQ_AT + 8 * D
DAT_AT = UP_LOW_AT + LOW_WORDS


def low_factors(m, at):
    return m.bf16(at, INNER)[0:TRIPLE, :], m.bf16(at + INNER // 2, INNER)[0:TRIPLE, :]




def load_small_weights(sp, m, dram):
    kq, full = "p (c d) -> p c d", (IT - 1) * P
    low, qkv = m.q_in[3], m.q_in[4]
    for k in range(PARTS):
        sp.dma_start(m.f32(GB_AT, INNER)[k * RANK:(k + 1) * RANK, :], dram["gate_B"]).then_inc(low, 16)
        sp.dma_start(m.f32(UB_AT, INNER)[k * RANK:(k + 1) * RANK, :], dram["up_B"]).then_inc(low, 16)
    sp.dma_start(m.f32(DB_AT, D)[0:RANK, :], dram["down_B"]).then_inc(low, 16)
    sp.dma_start(m.f32(GA_AT, DC * RANK).rearrange(kq, c=DC), dram["gate_A"].rearrange("(c p) r -> p c r", p=P)).then_inc(low, 16)
    sp.dma_start(m.f32(UA_AT, DC * RANK).rearrange(kq, c=DC), dram["up_A"].rearrange("(c p) r -> p c r", p=P)).then_inc(low, 16)
    sp.dma_start(m.f32(DA_AT, (IT - 1) * RANK).rearrange(kq, c=IT - 1),
                 dram["down_A"][0:full, :].rearrange("(c p) r -> p c r", p=P)).then_inc(low, 16)
    sp.dma_start(m.f32(DA_AT + (IT - 1) * RANK, RANK)[0:I_LAST, :], dram["down_A"][full:INNER, :]).then_inc(low, 16)
    for k, name in enumerate(("gate_scale", "up_scale")):
        sp.dma_start(m.scales[:, k * IT:k * IT + IT - 1], dram[name][0:full].rearrange("(c p) -> p c", p=P), allow_slow_non_contiguous=True).then_inc(low, 16)
        sp.dma_start(m.scales[0:I_LAST, k * IT + IT - 1:(k + 1) * IT],
                     dram[name][full:INNER].rearrange("(p c) -> p c", c=1), allow_slow_non_contiguous=True).then_inc(low, 16)
    sp.dma_start(m.f32(DOWN_SCALE_AT, D), dram["down_scale"].unsqueeze(0).to_broadcast([P, D])).then_inc(low, 16)
    sp.dma_start(m.f32(WQ_AT, DC * D).rearrange(kq, c=DC), dram["wq"].rearrange("(c p) d -> p c d", p=P)).then_inc(qkv, 16)
    sp.dma_start(m.f32(WQ_AT + DC * D, D), dram["wk"]).then_inc(qkv, 16)
    sp.dma_start(m.f32(WQ_AT + (DC + 1) * D, D), dram["wv"]).then_inc(qkv, 16)


LOW_LOADS, QKV_LOADS = 16, 3


def weights(nc, m, s, dram):
    scaled_tile = [m.f32(DEQ_AT + D + i * D, D) for i in range(2)]
    down_scale = m.f32(DOWN_SCALE_AT, D)
    BUFFERS = 4
    wide_bank = [m.banks[i] for i in (0, 1, 6, 7)]
    centred = [m.f16((DEQ_AT, DEQ_AT + D // 2, CENTRED_AT, CENTRED_AT + D // 2)[i], D) for i in range(BUFFERS)]
    gate_rest, up_rest = m.f32(DEQ_AT + 4 * D, INNER), m.f32(DEQ_AT + 4 * D + INNER, INNER)
    ident_h = m.f16(DEQ_AT + 3 * D + 2 * P, P)
    down_AT_tile = [m.f32(DEQ_AT + 3 * D + i * P, P)[0:RANK, :] for i in range(2)]
    dAT = m.f32(DAT_AT, INNER)[0:RANK, :]
    wide = [(GATEQ_AT, WG_AT, 0), (UPQ_AT, WU_AT, IT)]
    cut, pool_cut = Count(s("b_cut")), Count(s("b_pool_cut"))
    down_first = 2 * IT
    scales_ready, factors_turned, factors_ready = s("scales_ready"), s("factors_turned"), s("factors_ready")
    deq_ready, down_A_ready, built, placed = s("deq_ready"), s("down_A_ready"), s("w_built"), s("w_placed")
    qkv_turned, qkv_placed, ident_ready = s("qkv_turned"), s("qkv_placed"), s("ident_h")
    down_placed = s("down_placed")

    def rows(tile):
        return I_LAST if isinstance(tile, int) and tile == IT - 1 else P

    def each_tile(eng, first, body):
        whole = (IT - 1) // BUFFERS * BUFFERS
        with eng.Fori(0, whole // BUFFERS) as u:
            for k in range(BUFFERS):
                body(u * BUFFERS + k, (first + k) % BUFFERS)
        for t in range(whole, IT):
            body(t, (first + t) % BUFFERS)

    def each_down_tile(eng, body):
        with eng.Fori(0, (IT - 1) // 2) as u:
            for k in range(2):
                body(u * 2 + k, k)
        body(IT - 1, (IT - 1) % 2)

    def cut_factors(eng, seq, rest, b_at, a_at, at, k):
        both = m.f32(BOTH_A_AT, DC * 2 * RANK).rearrange("p (c k r) -> p c k r", c=DC, k=2)
        B, (first, second) = m.f32(b_at, INNER)[0:TRIPLE, :], low_factors(m, at)
        one, two, three = (slice(k * RANK, (k + 1) * RANK) for k in range(PARTS))
        eng.tensor_copy(both[:, :, k, :], m.f32(a_at, DC * RANK).rearrange("p (c r) -> p c r", c=DC))
        eng.tensor_copy(first[one, :], B[one, :])
        seq.mark(eng.tensor_copy(second, B))
        seq.wait(eng)
        seq.mark(eng.tensor_tensor(out=rest[0:TRIPLE, :], in0=B, in1=second, op=ALU.subtract))
        seq.wait(eng)
        eng.tensor_copy(first[two, :], rest[two, :])
        eng.tensor_copy(second[two, :], rest[two, :])
        seq.mark(eng.tensor_copy(first[three, :], rest[three, :]))
        seq.wait(eng)
        seq.mark(eng.tensor_tensor(out=first[three, :], in0=rest[three, :], in1=first[three, :], op=ALU.subtract))
        seq.wait(eng)

    with nc.Block() as block:
        @block.tensor
        def _(pe):
            pe.wait_ge(m.q_in[3], 16 * LOW_LOADS)
            for c in range(IT):
                r = rows(c)
                last = pe.transpose(m.banks[2 + c // 4][0:RANK, c % 4 * P:c % 4 * P + r],
                                    m.f32(DA_AT + c * RANK, RANK)[0:r, :], m.ident[0:r, 0:r])
                if c % 4 == 3 or c == IT - 1:
                    last.then_inc(factors_turned, 1)
            pe.wait_ge(ident_ready, 1)
            for _, _, first in wide:
                def tile(t, p):
                    r = rows(t)
                    bank = wide_bank[p]
                    pe.wait_ge(deq_ready, t + first + 1)
                    pe.wait_ge(placed, t + first + 1)
                    for hc in range(DC):
                        last = pe.transpose(bank[:, :].bitcast(F16)[:, hc * P:hc * P + r], centred[p][0:r, hc * P:(hc + 1) * P],
                                            ident_h[0:r, 0:r])
                    last.then_inc(built, 1)
                each_tile(pe, first, tile)
            pe.wait_ge(factors_ready, 3)
            pe.wait_ge(placed, down_first + 4)

            def down_tile(t, p):
                r = rows(t)
                bank = m.banks[6 + p]
                pe.wait_ge(deq_ready, t + down_first + 1)
                pe.wait_ge(down_A_ready, t + 3)
                pe.wait_ge(down_placed, t + 1)
                for oc in range(DC):
                    pe.transpose(bank[:, :].bitcast(F16)[0:r, oc * P:(oc + 1) * P], centred[p][:, oc * P:oc * P + r], ident_h)
                pe.matmul(m.banks[4 + p][0:r, :], down_AT_tile[p][:, 0:r], m.f32(DB_AT, D)[0:RANK, :],
                          start=True, stop=True).then_inc(built, 1)
            each_down_tile(pe, down_tile)

            pe.wait_ge(m.q_in[4], 16 * QKV_LOADS)
            for c in range(DC + 2):
                if c >= 4:
                    pe.wait_ge(qkv_placed, c - 3)
                for hc in range(DC):
                    last = pe.transpose(m.banks[c % 4][:, hc * P:(hc + 1) * P],
                                        m.f32(WQ_AT + c * D + hc * P, P), m.ident)
                last.then_inc(qkv_turned, 1)

        @block.vector
        def _(dve):
            dve.wait_ge(m.q_in[3], 16 * LOW_LOADS)
            dve.tensor_scalar(out=m.scales[:, 0:IT - 1], in0=m.scales[:, 0:IT - 1], scalar1=Q_STEP, scalar2=None, op0=ALU.mult)
            dve.tensor_scalar(out=m.scales[0:I_LAST, IT - 1:IT], in0=m.scales[0:I_LAST, IT - 1:IT], scalar1=Q_STEP, scalar2=None, op0=ALU.mult)
            dve.tensor_scalar(out=m.scales[:, IT:2 * IT - 1], in0=m.scales[:, IT:2 * IT - 1], scalar1=Q_STEP, scalar2=None, op0=ALU.mult)
            dve.tensor_scalar(out=m.scales[0:I_LAST, 2 * IT - 1:2 * IT], in0=m.scales[0:I_LAST, 2 * IT - 1:2 * IT], scalar1=Q_STEP, scalar2=None, op0=ALU.mult)
            dve.tensor_scalar(out=down_scale, in0=down_scale, scalar1=Q_STEP, scalar2=None, op0=ALU.mult).then_inc(scales_ready, 1)
            dve.wait_ge(scales_ready, 1)
            dve.sem_inc(down_placed, 2)
            dve.tensor_copy(ident_h, m.ident).then_inc(ident_ready, 1)
            for k, (q_at, _, first) in enumerate(wide):
                dve.wait_ge(m.q_in[k], 32)

                def tile(t, p):
                    r = rows(t)
                    dve.wait_ge(built, t + first + 1)
                    dve.tensor_scalar(out=centred[p][0:r, :], in0=m.arena[0:r, ds(t * D + q_at, D)].bitcast(I32),
                                      scalar1=-Q_ZERO, scalar2=None, op0=ALU.add).then_inc(deq_ready, 1)
                each_tile(dve, first, tile)
            dve.wait_ge(m.q_in[2], 16)
            q = m.i32(DOWNQ_AT, DC * INNER).rearrange("p (c i) -> p c i", c=DC)

            def centre(t, p):
                r = rows(t)
                dve.wait_ge(built, t + down_first + 3)
                dve.tensor_scalar(out=centred[p].rearrange("p (c i) -> p c i", c=DC)[:, :, 0:r], in0=q[:, :, ds(t * P, r)],
                                  scalar1=-Q_ZERO, scalar2=None, op0=ALU.add).then_inc(deq_ready, 1)

            def combine(t, p):
                r = rows(t)
                dve.wait_ge(built, t + down_first + 5)
                dve.wait_ge(down_placed, t + 1)
                cut.mark(dve.tensor_tensor(out=scaled_tile[p][0:r, :], in0=m.banks[6 + p][:, :].bitcast(F16)[0:r, 0:D],
                                           in1=down_scale[0:r, :], op=ALU.mult))
                cut.wait(dve)
                dve.tensor_tensor(out=m.arena[0:r, ds(t * D + WD_AT, D)], in0=m.banks[4 + p][0:r, :],
                                  in1=scaled_tile[p][0:r, :], op=ALU.add).then_inc(down_placed, 1)

            centre(0, 0)
            with dve.Fori(0, (IT - 3) // 2) as u:
                cut.enter(u, 2)
                for k in range(2):
                    centre(u * 2 + (k + 1), 1 - k)
                    combine(u * 2 + k, k)
            cut.leave((IT - 3) // 2)
            for t in range(IT - 3, IT):
                if t + 1 < IT:
                    centre(t + 1, (t + 1) % 2)
                combine(t, t % 2)
            cut.settle()
            cut_factors(dve, cut, up_rest, UB_AT, UA_AT, UP_LOW_AT, 1)

        @block.gpsimd
        def _(pool):
            pool.sem_inc(down_A_ready, 2)
            pool.sem_inc(built, 4)
            pool.wait_ge(m.q_in[3], 16 * LOW_LOADS)
            cut_factors(pool, pool_cut, gate_rest, GB_AT, GA_AT, GATE_LOW_AT, 0)

        @block.scalar
        def _(act):
            act.sem_inc(placed, 4)
            for k in range(3):
                n = min(D, INNER - k * D)
                act.wait_ge(factors_turned, k + 1)
                act.activation(dAT[:, k * D:k * D + n], m.banks[2 + k][0:RANK, 0:n], ACT.Copy, scale=LR_SCALE).then_inc(factors_ready, 1)
            for _, out_at, first in wide:
                W = m.f16(out_at, DC * INNER).rearrange("p (c i) -> p c i", c=DC)

                def tile(t, p):
                    r = rows(t)
                    act.wait_ge(built, t + first + 5)
                    turned = wide_bank[p][:, :].bitcast(F16)[:, 0:D].rearrange("p (c i) -> p c i", c=DC)
                    act.activation(W[:, :, ds(t * P, r)], turned[:, :, 0:r],
                                   ACT.Copy).then_inc(placed, 1)
                each_tile(act, first, tile)

            def down_factor(t, p):
                r = rows(t)
                act.wait_ge(built, t + down_first + 3)
                act.activation(down_AT_tile[p][:, 0:r], dAT[:, ds(t * P, r)], ACT.Copy).then_inc(down_A_ready, 1)
            act.wait_ge(factors_ready, 3)
            each_down_tile(act, down_factor)

            W = m.f32(WQKV_AT, DC * QKV).rearrange("p (c n) -> p c n", c=DC)
            for c in range(DC + 2):
                act.wait_ge(qkv_turned, c + 1)
                act.activation(W[:, :, c * P:(c + 1) * P], m.banks[c % 4].rearrange("p (c n) -> p c n", c=DC), ACT.Copy).then_inc(qkv_placed, 1)


def gated(nc, m, s, dram):
    G = 4
    W = [m.f16(at, DC * INNER) for at in (WG_AT, WU_AT)]
    low = [low_factors(m, at) for at in (GATE_LOW_AT, UP_LOW_AT)]
    both_A = m.f32(BOTH_A_AT, DC * 2 * RANK)
    take = m.taker(WORK, UP_LOW_AT)
    xT, high, rest = take(DC * G * P), take(DC * G * P, F16), take(DC * G * P, F16)
    xn = [take(D) for _ in range(G)]
    silu, gate, low_sum = [take(D) for _ in range(2)], [take(D) for _ in range(2)], [take(D) for _ in range(2)]
    up = take(D)
    t_all, t_rest = [take(G * P) for _ in range(2)], [take(G * P) for _ in range(2)]
    t_first, t_second = [take(G * P, BF16) for _ in range(2)], [take(G * P, BF16) for _ in range(2)]
    rstd_ready, xn_ready, turned, xT_ready = s("b_rstd"), s("b_xn"), s("b_turned"), s("b_xT")
    parts_ready, t_made, t_kept, t_ready = s("b_parts"), s("b_t_made"), s("b_t_kept"), s("b_t_ready")
    low_made, low_kept, products, combined = s("b_low_made"), s("b_low_kept"), s("b_products"), s("b_combined")
    silu_ready, h_ready = s("b_silu"), s("b_h_ready")
    down_ready, stats_ready, branch_rstd_ready, added = s("b_down"), s("b_stats"), s("b_branch_rstd"), s("b_added")
    dve_seq, pool_seq = Count(s("b_dve_seq")), Count(s("b_pool_seq"))
    n_groups = TILES // G
    HALF = 2 * IT

    def rows(i):
        return I_LAST if i == IT - 1 else P

    def over_groups(eng, body):
        with eng.Fori(0, n_groups - 1) as g:
            body(g, False)
        body(n_groups - 1, True)

    with nc.Block() as block:
        @block.tensor
        def _(pe):
            def turn(g, t):
                k = g * G + t
                pe.wait_ge(xn_ready, k + 1)
                pe.wait_ge(xT_ready, k + 1)
                for dc in range(DC):
                    last = pe.transpose(m.banks[4 + t % 2][:, dc * P:(dc + 1) * P], xn[t][:, dc * P:(dc + 1) * P], m.ident)
                last.then_inc(turned, 1)

            def low_t(g):
                pe.wait_ge(xT_ready, g * G + (G + 2))
                pe.wait_ge(combined, g * HALF + 2)
                for dc in range(DC):
                    last = pe.matmul(m.banks[0][0:2 * RANK, :], both_A[:, dc * 2 * RANK:(dc + 1) * 2 * RANK],
                                     xT[:, dc * G * P:(dc + 1) * G * P], start=dc == 0, stop=dc == DC - 1)
                last.then_inc(t_made, 1)

            def half_step(g, i, k):
                n, r = g * HALF + 2 * i + k, rows(i)
                pe.wait_ge(combined, n + 1)
                if i == 0:
                    pe.wait_ge(t_ready, g * 2 + (k + 1))
                first, second = low[k]
                cols = slice(i * P, i * P + r)
                pe.matmul(m.banks[2 + k][0:r, :], first[:, cols], t_first[k][0:TRIPLE, :], start=True, stop=False)
                pe.matmul(m.banks[2 + k][0:r, :], second[:, cols], t_second[k][0:TRIPLE, :], start=False, stop=True).then_inc(low_made, 1)
                for part in (high, rest):
                    for dc in range(DC):
                        last = pe.matmul(m.banks[k][0:r, :], W[k][:, dc * INNER + i * P:dc * INNER + i * P + r],
                                         part[:, dc * G * P:(dc + 1) * G * P], start=part is high and dc == 0,
                                         stop=part is rest and dc == DC - 1)
                last.then_inc(products, 1)

            def down(g, t):
                pe.wait_ge(added, g * G + (t + 1))
                for i in range(IT):
                    r = rows(i)
                    last = pe.matmul(m.banks[6 + t % 2][:, :], m.f32(HT_AT + i * D + t * P, P)[0:r, :],
                                     m.f32(WD_AT + i * D, D)[0:r, :], start=i == 0, stop=i == IT - 1)
                last.then_inc(down_ready, 1)

            def group(g, last_group):
                pe.wait_ge(t_kept, g * 2 + 2)
                pe.wait_ge(parts_ready, g * G + G)
                for i in range(IT):
                    for k in range(2):
                        half_step(g, i, k)
                if not last_group:
                    for t in range(G):
                        turn(g + 1, t)
                pe.wait_ge(h_ready, g * IT + (IT + 1))
                for t in range(G):
                    down(g, t)
                    if t == 0 and not last_group:
                        low_t(g + 1)

            for t in range(G):
                turn(0, t)
            low_t(0)
            over_groups(pe, group)

        @block.scalar
        def _(act):
            def normed(g, t):
                k = g * G + t
                act.activation(xn[t], m.x(k), ACT.Identity, bias=m.shift[:, ds(k, 1)],
                               scale=m.rstd[:, ds(k, 1)]).then_inc(xn_ready, 1)

            def keep(g, t):
                act.wait_ge(turned, g * G + (t + 1))
                act.activation(xT.rearrange("p (c n) -> p c n", c=DC)[:, :, t * P:(t + 1) * P],
                               m.banks[4 + t % 2].rearrange("p (c n) -> p c n", c=DC), ACT.Copy).then_inc(xT_ready, 1)

            def keep_t(g):
                act.wait_ge(t_made, g + 1)
                for k in range(2):
                    for n in range(PARTS):
                        last = act.activation(t_all[k][n * RANK:(n + 1) * RANK, :], m.banks[0][k * RANK:(k + 1) * RANK, :],
                                              ACT.Copy, scale=LR_SCALE)
                    last.then_inc(t_kept, 1)

            def group(g, last_group):
                for i in range(IT):
                    r = rows(i)
                    for k in range(2):
                        n = g * HALF + 2 * i + k
                        act.wait_ge(low_made, n + 1)
                        act.wait_ge(combined, n + 1)
                        act.activation(low_sum[k][0:r, :], m.banks[2 + k][0:r, :], ACT.Copy).then_inc(low_kept, 1)
                    act.wait_ge(combined, g * HALF + 2 * i + 3)
                    act.activation(silu[i % 2][0:r, :], gate[i % 2][0:r, :], ACT.Silu).then_inc(silu_ready, 1)
                    if i in (1, 3, 5, 7) and not last_group:
                        normed(g + 1, i // 2)
                if not last_group:
                    for t in range(G):
                        keep(g + 1, t)
                    keep_t(g + 1)

            act.sem_inc(xT_ready, 2)
            act.wait_ge(rstd_ready, 1)
            for t in range(G):
                normed(0, t)
            for t in range(G):
                keep(0, t)
            keep_t(0)
            over_groups(act, group)

        @block.vector
        def _(dve):
            dve.sem_inc(combined, 2)
            dve.sem_inc(h_ready, 1)
            dve.sem_inc(added, 2)

            def x_parts(g, seq):
                cut = lambda x, t: x.rearrange("p (c n) -> p c n", c=DC)[:, :, t * P:(t + 1) * P]
                for t in range(G):
                    dve.wait_ge(xT_ready, g * G + (t + 3))
                    seq.mark(dve.tensor_copy(cut(high, t), cut(xT, t)))
                    seq.wait(dve)
                    dve.tensor_tensor(out=cut(rest, t), in0=cut(xT, t), in1=cut(high, t), op=ALU.subtract).then_inc(parts_ready, 1)

            def t_parts(g, seq):
                last = slice(2 * RANK, TRIPLE)
                for k in range(2):
                    dve.wait_ge(t_kept, g * 2 + (k + 1))
                    seq.mark(dve.tensor_copy(t_first[k][0:TRIPLE, :], t_all[k][0:TRIPLE, :]))
                    seq.wait(dve)
                    seq.mark(dve.tensor_tensor(out=t_rest[k][0:TRIPLE, :], in0=t_all[k][0:TRIPLE, :], in1=t_first[k][0:TRIPLE, :], op=ALU.subtract))
                    seq.wait(dve)
                    seq.mark(dve.tensor_copy(t_second[k][0:TRIPLE, :], t_rest[k][0:TRIPLE, :]))
                    seq.wait(dve)
                    dve.tensor_tensor(out=t_second[k][last, :], in0=t_rest[k][last, :], in1=t_second[k][last, :],
                                      op=ALU.subtract).then_inc(t_ready, 1)

            def group(g, last_group):
                for i in range(IT):
                    r = rows(i)
                    for k, out in enumerate((gate[i % 2], up)):
                        n = g * HALF + 2 * i + k
                        dve.wait_ge(products, n + 1)
                        dve.wait_ge(low_kept, n + 1)
                        if k == 1:
                            dve.wait_ge(h_ready, g * IT + (i + 1))
                        dve.scalar_tensor_tensor(out=out[0:r, :], in0=m.banks[k][0:r, :], scalar=m.scales[0:r, k * IT + i:k * IT + i + 1],
                                                 in1=low_sum[k][0:r, :], op0=ALU.mult, op1=ALU.add).then_inc(combined, 1)
                    dve.wait_ge(silu_ready, g * IT + (i + 1))
                    dve.wait_ge(combined, g * HALF + 2 * i + 4)
                    dve.tensor_tensor(out=m.f32(HT_AT + i * D, D)[0:r, :], in0=up[0:r, :],
                                      in1=silu[i % 2][0:r, :], op=ALU.mult).then_inc(h_ready, 1)
                seq = dve_seq
                if last_group:
                    seq.settle()
                else:
                    seq.enter(g, G * (1 + BRANCH_ADD_STEPS) + G + 6)
                    x_parts(g + 1, seq)
                for t in range(G):
                    dve.wait_ge(down_ready, g * G + (t + 1))
                    branch_stats(dve, m, dve_seq, t % 2, m.banks[6 + t % 2][:, :]).then_inc(stats_ready, 1)
                    dve.wait_ge(branch_rstd_ready, g * G + (t + 1))
                    branch_add(dve, m, dve_seq, t % 2, m.banks[6 + t % 2][:, :], g * G + t).then_inc(added, 1)
                    if t == 0 and not last_group:
                        t_parts(g + 1, seq)
                if not last_group:
                    seq.leave(n_groups - 1)

            x_parts(0, dve_seq)
            t_parts(0, dve_seq)
            dve_seq.settle()
            over_groups(dve, group)

        @block.gpsimd
        def _(pool):
            rstd_all(pool, m, pool_seq).then_inc(rstd_ready, 1)
            pool_seq.settle()

            def group(g, _):
                pool_seq.enter(g, G)
                for t in range(G):
                    pool.wait_ge(stats_ready, g * G + (t + 1))
                    branch_rstd(pool, m, pool_seq, t % 2).then_inc(branch_rstd_ready, 1)
            over_groups(pool, group)


def project(nc, m, s, dram):
    W = m.f32(WQKV_AT, DC * QKV)
    take = m.taker(WORK, ARENA - SEQ)
    xn, xT = [take(D) for _ in range(2)], [take(D) for _ in range(2)]
    raw, spun = [take(QK) for _ in range(2)], [take(QK) for _ in range(2)]
    rotated = [take(QK) for _ in range(2)]
    part = [[take(QK, BF16) for _ in range(PARTS)] for _ in range(2)]
    q_rows, k_rows = [take(HEADS * ROWS, BF16) for _ in range(2)], [take(KV * ROWS, BF16) for _ in range(2)]
    key_rows = take(SEQ)
    v_all = m.f32(V_AT, GROUPS * SEQ_TILES * 32)
    rstd_ready, xn_ready, turned, xT_ready = s("c_rstd"), s("c_xn"), s("c_turned"), s("c_xT")
    products, raw_ready, v_ready, spun_ready = s("c_products"), s("c_raw"), s("c_v"), s("c_spun")
    rotated_ready, high_ready, high_rows_ready = s("c_rotated"), s("c_high"), s("c_high_rows")
    rows_ready, rows_out = s("c_rows_ready"), [s(f"c_rows_out{b}") for b in range(2)]
    v_blank, rows_in = s("c_v_blank"), s("c_rows_in")
    dve_seq, pool_seq = Count(s("c_dve_seq")), Count(s("c_pool_seq"))

    def heads(ap):
        return ap.rearrange("p (h d) -> p h d", d=HD)

    def slots(ap):
        return ap.rearrange("p (h r d) -> p h r d", r=6, d=HD)

    def q_of(ap, n):
        return heads(ap[:, 0:HEADS * HD]).unsqueeze(2).to_broadcast([P, HEADS, n, HD])

    def k_of(ap, n):
        return heads(ap[:, HEADS * HD:QK]).unsqueeze(2).to_broadcast([P, KV, n, HD])

    with nc.Block() as block:
        @block.sync
        def _(sp):
            sp.dma_start(key_rows[ROWS:KROWS, :], dram["key_rows"]).then_inc(rows_in, 16)
            with sp.Fori(0, SEQ_TILES) as i:
                for b in range(2):
                    k = i * 2 + b
                    to = dram["rows"][b * KV:(b + 1) * KV].rearrange("k p (t w) -> p k t w", t=SEQ_TILES)[:, :, ds(i, 1), :].squeeze(2)
                    sp.wait_ge(high_rows_ready, k + 1)
                    sp.wait_ge(rows_ready, k + 1)
                    sp.dma_start(to[:, :, 0:GQ * ROWS], q_rows[b].rearrange("p (k w) -> p k w", k=KV)).then_inc(rows_out[b], 16)
                    sp.dma_start(to[:, :, GQ * ROWS:], k_rows[b].rearrange("p (k w) -> p k w", k=KV)).then_inc(rows_out[b], 16)
            for b in range(2):
                sp.wait_ge(rows_out[b], SEQ_TILES * 32 + 32)

        @block.tensor
        def _(pe):
            def turn(k, b):
                pe.wait_ge(xn_ready, k + 1)
                for dc in range(DC):
                    last = pe.transpose(m.banks[b][:, dc * P:(dc + 1) * P], xn[b][:, dc * P:(dc + 1) * P], m.ident)
                last.then_inc(turned, 1)

            def feed(k, b):
                pe.wait_ge(xT_ready, k + 1)
                pe.wait_ge(v_ready, k + 1)
                for dc in range(DC):
                    pe.matmul(m.banks[2 + b][:, :], xT[b][:, dc * P:(dc + 1) * P], W[:, dc * QKV:dc * QKV + D],
                              start=dc == 0, stop=dc == DC - 1)
                for dc in range(DC):
                    last = pe.matmul(m.banks[4 + b][:, 0:QKV - D], xT[b][:, dc * P:(dc + 1) * P], W[:, dc * QKV + D:(dc + 1) * QKV],
                                     start=dc == 0, stop=dc == DC - 1)
                last.then_inc(products, 1)

            for b in range(2):
                turn(b, b)
            with pe.Fori(0, SEQ_TILES - 1) as i:
                for b in range(2):
                    feed(i * 2 + b, b)
                for b in range(2):
                    turn(i * 2 + (2 + b), b)
            for b in range(2):
                feed(TILES - 2 + b, b)

        @block.scalar
        def _(act):
            def normed(i, b):
                act.activation(xn[b], m.x(i + b * SEQ_TILES), ACT.Identity, bias=m.shift[:, ds(i + b * SEQ_TILES, 1)],
                               scale=m.rstd[:, ds(i + b * SEQ_TILES, 1)]).then_inc(xn_ready, 1)

            def keep(k, b):
                act.wait_ge(turned, k + 1)
                act.activation(xT[b], m.banks[b][:, :], ACT.Copy).then_inc(xT_ready, 1)

            def evacuate(i, b):
                k = i * 2 + b
                act.wait_ge(products, k + 1)
                act.wait_ge(rotated_ready, k + 1)
                act.activation(raw[b][:, 0:D], m.banks[2 + b][:, :], ACT.Copy)
                act.activation(raw[b][:, D:QK], m.banks[4 + b][:, 0:QK - D], ACT.Copy).then_inc(raw_ready, 1)
                v = v_all.rearrange("p (b k t c) -> p b k t c", b=BATCH, k=KV, t=SEQ_TILES)[:, b]
                act.activation(v[:, :, ds(i, 1), 0:HD].squeeze(2), heads(m.banks[4 + b][:, QK - D:QKV - D]), ACT.Copy).then_inc(v_ready, 1)

            def cut(i, b):
                k = i * 2 + b
                act.wait_ge(rotated_ready, k + 3)
                act.activation(part[b][0], rotated[b], ACT.Copy).then_inc(high_ready, 1)
                act.wait_ge(rows_out[b], i * 32 + 32)
                act.wait_ge(high_ready, k + 1)
                act.activation(slots(q_rows[b])[:, :, 0:3, :], q_of(part[b][0], 3), ACT.Copy).then_inc(high_rows_ready, 1)

            act.sem_inc(v_ready, 2)
            act.wait_ge(rstd_ready, 1)
            act.wait_ge(v_blank, 1)
            for b in range(2):
                normed(0, b)
            for b in range(2):
                keep(b, b)
            with act.Fori(0, SEQ_TILES - 1) as i:
                for b in range(2):
                    normed(i + 1, b)
                for b in range(2):
                    evacuate(i, b)
                for b in range(2):
                    keep(i * 2 + (2 + b), b)
                for b in range(2):
                    cut(i, b)
            for b in range(2):
                evacuate(SEQ_TILES - 1, b)
            for b in range(2):
                cut(SEQ_TILES - 1, b)

        @block.gpsimd
        def _(pool):
            v = v_all.rearrange("p (n c) -> p n c", c=32)
            pool.memset(v[:, :, HD + 1:], 0.0)
            pool.memset(v[:, :, HD:HD + 1], 1.0).then_inc(v_blank, 1)
            rstd_all(pool, m, pool_seq).then_inc(rstd_ready, 1)
            pool.sem_inc(rotated_ready, 2)
            for b in range(2):
                pool.sem_inc(rows_out[b], 32)
            pool_seq.settle()
            with pool.Fori(0, SEQ_TILES) as i:
                for b in range(2):
                    sin = m.sin.rearrange("p (t d) -> p t d", d=HD)[:, ds(i, 1), :]
                    pool.wait_ge(rotated_ready, i * 2 + b + 1)
                    pool.wait_ge(raw_ready, i * 2 + b + 1)
                    pool.sem_inc(m.turnstile, 1)
                    h = HD // 2
                    for lo, hi in ((0, h), (h, 0)):
                        last = pool.tensor_tensor(out=heads(spun[b])[:, :, lo:lo + h], in0=heads(raw[b])[:, :, hi:hi + h],
                                                  in1=sin[:, :, lo:lo + h].to_broadcast([P, QK // HD, h]), op=ALU.mult)
                    last.then_inc(spun_ready, 1)

        @block.vector
        def _(dve):
            dve.wait_ge(rows_in, 16)
            for k in range(2):
                dve.tensor_copy(m.key_aug[k][ROWS:KROWS, :], key_rows[ROWS:KROWS, :])
            with dve.Fori(0, SEQ_TILES) as i:
                dve_seq.enter(i, 12)
                cos = m.cos.rearrange("p (t d) -> p t d", d=HD)[:, ds(i, 1), :]
                for b in range(2):
                    k = i * 2 + b
                    dve.wait_ge(raw_ready, k + 1)
                    dve_seq.mark(dve.tensor_tensor(out=heads(rotated[b]), in0=heads(raw[b]),
                                                   in1=cos.to_broadcast([P, QK // HD, HD]), op=ALU.mult))
                    dve_seq.wait(dve)
                    dve.wait_ge(spun_ready, k + 1)
                    dve.tensor_tensor(out=rotated[b], in0=rotated[b], in1=spun[b], op=ALU.add).then_inc(rotated_ready, 1)
                for b in range(2):
                    k = i * 2 + b
                    high, mid, low = part[b]
                    dve.wait_ge(high_ready, k + 1)
                    dve_seq.mark(dve.tensor_tensor(out=rotated[b], in0=rotated[b], in1=high, op=ALU.subtract))
                    dve_seq.wait(dve)
                    dve_seq.mark(dve.tensor_copy(mid, rotated[b]))
                    dve_seq.wait(dve)
                    dve_seq.mark(dve.tensor_tensor(out=low, in0=rotated[b], in1=mid, op=ALU.subtract))
                    dve.wait_ge(rows_out[b], i * 32 + 32)
                    q, kk = slots(q_rows[b]), slots(k_rows[b])
                    dve_seq.mark(dve.tensor_copy(kk[:, :, 0:4:3, :], k_of(high, 2)))
                    dve_seq.mark(dve.tensor_copy(kk[:, :, 5:6, :], k_of(high, 1)))
                    dve.tensor_copy(kk[:, :, 1:5:3, :], k_of(mid, 2))
                    dve.tensor_copy(q[:, :, 3:5, :], q_of(mid, 2))
                    dve_seq.wait(dve)
                    dve.tensor_copy(kk[:, :, 2:3, :], k_of(low, 1))
                    dve.tensor_copy(q[:, :, 5:6, :], q_of(low, 1)).then_inc(rows_ready, 1)
            dve_seq.leave(SEQ_TILES)


def attention(nc, m, s, dram):
    take = m.taker(CWORK, WO_AT)
    N = GQ * P
    CLOSES = 3
    ORDER = [7, 0, 4, 3, 6, 1, 5, 2]
    query_aug = [take(2 * N if i >= 4 else N, BF16) for i in ORDER]
    chunk_diag = [take(N, BF16) for _ in ORDER]
    staged = [take(ST_W, BF16) for _ in range(2)]
    v_staged = [take(SEQ_TILES * 32) for _ in range(2)]
    probs = [take(N) for _ in range(4)]
    W = [take(GQ * 2 * (MASK_ROWS + 1), BF16) for _ in range(SEQ_TILES)]
    cmax = [take(GQ * 64) for _ in range(2)]
    left = [take(GQ * 64) for _ in range(2)]
    top = [take(GQ * TOPK) for _ in range(4)]
    own = [take(GQ * CPT) for _ in range(4)]
    own_dropped = [take(GQ) for _ in range(4)]
    minus = [take(GQ) for _ in range(2)]
    minus_rest = [take(GQ) for _ in range(2)]
    ot = [take(P) for _ in ORDER]
    inverse = [take(4 * GQ) for _ in range(CLOSES)]
    o_staged = [take(SEQ_TILES * GQ * HD) for _ in range(2)]
    neg_one, one_row = take(GQ), take(GQ)
    key_aug = m.key_aug

    score_bank, back_bank, turn_bank = m.banks[0:3], m.banks[3:5], m.banks[5]
    sums = [m.banks[6 + i][:, 0:P] for i in range(2)]
    turn_bf = turn_bank[:, :].bitcast(BF16)

    staged_in, v_in, stored = ([s(f"d_{name}{p}") for p in range(2)] for name in ("staged", "v_in", "stored"))
    top_turned, top_kept = s("d_top_turned"), s("d_top_kept")
    scored, reduced = s("d_scored"), s("d_reduced")
    mask_ready, minus_ready = s("d_mask"), s("d_minus")
    mask_turned, mask_kept = s("d_mask_turned"), s("d_mask_kept")
    masked_scored, probs_ready, summed = s("d_masked_scored"), s("d_probs"), s("d_summed")
    ot_ready = s("d_ot")
    w_blank, top_ready, own_ready, diag_ready = s("d_w_blank"), s("d_top"), s("d_own"), s("d_diag")
    dve_seq, pool_seq = Count(s("d_dve_seq")), Count(s("d_pool_seq"))

    halves = [1 if (i + 1) * P <= 512 else 2 for i in range(SEQ_TILES)]
    score_at = [GQ * sum(halves[i] for i in ORDER[:n]) for n in range(SEQ_TILES + 1)]
    back_at = [sum(i + 1 for i in ORDER[:n]) for n in range(SEQ_TILES + 1)]
    drops_at = [sum(i >= 2 for i in ORDER[:n]) for n in range(SEQ_TILES)]
    SC, BK, TT = score_at[-1], back_at[-1], SEQ_TILES + 2
    RING = SC + CLOSES
    assert RING % 3 == 0 and BK % 4 == 0
    PAIR = 2 * SEQ_TILES

    class Step:

        def __init__(self, t, k):
            self.g, self.at, self.k, self.p = t * 2 + k // SEQ_TILES, k % SEQ_TILES, k, k // SEQ_TILES % 2
            self.i = ORDER[self.at]
            self.n, self.q = t * PAIR + k, t + k // PAIR
            self.exists = not isinstance(t, int) or 0 <= t * PAIR + k < GROUPS * SEQ_TILES
            self.slot = k % SEQ_TILES
            self.two = self.i >= 4

    def closing(t, u):
        first = {0: 4, 1: 3, 2: 3}.get(u % 4)
        steps = [Step(t, k) for k in range(2 * (u - first), 2 * (u - 2))] if first else []
        return [st for st in steps if st.exists], Step(t, 2 * u).g, u % 4

    def is_first(g):
        return isinstance(g, int) and g == 0

    def ring_of_score(st, number):
        closes = 0 if is_first(st.g) else min((st.at + 1) // 2, CLOSES) - CLOSES
        return st.g * RING + (score_at[st.at] + number + closes)

    def ring_of_close(g, place):
        last = isinstance(g, int) and g == GROUPS
        return g * RING + ((0 if last else score_at[2 * place + 1]) + place - CLOSES)

    def bank_of_score(st, number):
        closes = 0 if is_first(st.g) else min((st.at + 1) // 2, CLOSES)
        return (score_at[st.at] + number + closes) % 3

    def closed_bank(g, place):
        return ((0 if isinstance(g, int) and g == GROUPS else score_at[2 * place + 1]) + place) % 3

    def stages(t, u):
        return [[st for st in (Step(t, 2 * (u - n)), Step(t, 2 * (u - n) + 1)) if st.exists] for n in (0, 1, 2, 3, -1)]

    def schedule(t, u):
        front, mid, back, end, after = stages(t, u)
        scores = [("score", st, n) for st in front for n in range(GQ * halves[st.i])]
        tiles = [(st, j) for st in back for j in range(st.i + 1)]
        backs = []
        lag = 2
        for n in range(len(tiles) + lag):
            if n < len(tiles):
                backs.append(("masked", *tiles[n]))
            if n == 1 and end:
                backs.append(("sums", end[1], 0))
            if n >= lag:
                backs.append(("weigh", *tiles[n - lag]))
                if tiles[n - lag] == (back[1], 0):
                    backs.append(("sums", back[0], 0))
        if not back and end:
            backs = [("sums", end[1], 0)]
        if closing(t, u)[0]:
            scores.insert(GQ * halves[front[0].i] if front else 0, ("close", None, 0))
        ahead, choice = 1, 1.6
        at, starts = 0.0, []
        for kind, st, n in scores:
            starts.append(at)
            if kind == "score":
                half = n % halves[st.i]
                at += 0.25 + min((st.i + 1) * P - half * 512, 512) / 1000
                if n == GQ * halves[st.i] - 1:
                    at += choice if st.i >= 2 else 0.2
            else:
                at += 0.5
        places = [(starts[max(n - ahead, 0)] / at if front else 0.99, x) for n, x in enumerate(scores)]
        places += [(n / max(len(backs), 1), x) for n, x in enumerate(backs)]
        places += [(f, ("turn_q", st, 0)) for f, st in zip((0.05, 0.25), after)]
        places += [(f, ("turn_mask", st, 0)) for f, st in zip((0.4, 0.8), mid)]
        if front and front[0].at == 4 and Step(t, 2 * u + 4).exists:
            places += [(f, ("turn_k", Step(t, 2 * u + 4), half)) for f, half in ((0.55, 0), (0.9, 1))]
        return [x for _, x in sorted(places, key=lambda x: x[0])]

    def over_units(eng, body, seq=None, per=0):
        for u in range(4):
            body(0, u)
        if seq:
            seq.settle()
        with eng.Fori(0, GROUPS // 2 - 1) as t:
            if seq:
                seq.enter(t, per)
            for u in range(4, SEQ_TILES + 4):
                body(t, u)
        if seq:
            seq.leave(GROUPS // 2 - 1)
        for u in range(4, SEQ_TILES + 4):
            body(GROUPS // 2 - 1, u)

    with nc.Block() as block:
        @block.sync
        def _(sp):
            def load_rows(g, p):
                sp.dma_start(staged[p], dram["rows"][ds(g, 1)].squeeze(0)).then_inc(staged_in[p], 16)

            def load_v(g, p):
                sp.dma_start(v_staged[p], m.arena[:, ds(g * (SEQ_TILES * 32) + V_AT, SEQ_TILES * 32)]).then_inc(v_in[p], 16)

            def store(g, p):
                sp.wait_ge(reduced, ring_of_close(g + 1, CLOSES - 1) + 4)
                sp.dma_start(m.arena[:, ds(g * (SEQ_TILES * GQ * HD) + O_AT, SEQ_TILES * GQ * HD)], o_staged[p]).then_inc(stored[p], 16)

            for p in range(2):
                load_rows(p, p)
                load_v(p, p)
            load_last_weights(sp, m, dram)
            with sp.Fori(0, GROUPS // 2 - 1) as t:
                for p in range(2):
                    sp.wait_ge(top_turned, t * 2 * TT + (p + 1) * TT)
                    load_rows(t * 2 + (2 + p), p)
                    sp.wait_ge(summed, t * 2 * BK + ((p + 1) * BK + 4))
                    load_v(t * 2 + (2 + p), p)
                    store(t * 2 + p, p)
            for p in range(2):
                store(GROUPS - 2 + p, p)
            for p in range(2):
                sp.wait_ge(stored[p], 16 * (GROUPS // 2 + 1))

        @block.tensor
        def _(pe):
            def turn_q(st):
                pe.wait_ge(top_kept, st.g * TT + (2 + st.at))
                for h in range(GQ):
                    at = st.i * ST_TILE + h * ROWS
                    last = pe.transpose(turn_bf[0:ROWS, h * P:(h + 1) * P], staged[st.p][:, at:at + ROWS], m.ident_bf)
                last.then_inc(top_turned, 1)

            def turn_k(g, p, q, half, first):
                if not first:
                    pe.wait_ge(top_kept, g * TT + half)
                if half == 0:
                    pe.wait_ge(staged_in[p], q * 16 + 16)
                for c in range(4):
                    at = (half * 4 + c) * ST_TILE + GQ * ROWS
                    last = pe.transpose(turn_bf[0:ROWS, c * P:(c + 1) * P], staged[p][:, at:at + ROWS], m.ident_bf)
                last.then_inc(top_turned, 1)

            def turn_mask(st):
                if not (isinstance(st.n, int) and st.n == 0):
                    pe.wait_ge(mask_kept, st.n)
                pe.wait_ge(minus_ready, st.n + 1)
                pe.wait_ge(mask_ready, st.n + 1)
                w = W[st.i].rearrange("p (h f r) -> p h f r", h=GQ, f=2)
                for h in range(GQ):
                    for f in range(1 + st.two):
                        last = pe.transpose(turn_bf[ROWS:KROWS, f * N + h * P:f * N + (h + 1) * P],
                                            w[:, h, f, 0:MASK_ROWS], m.ident_bf)
                last.then_inc(mask_turned, 1)

            def score(st, number):
                ring = ring_of_score(st, number)
                h, half = divmod(number, halves[st.i])
                k0, k1 = half * 512, min((st.i + 1) * P, (half + 1) * 512)
                bank = score_bank[bank_of_score(st, number)]
                diagonal = k1 == (st.i + 1) * P
                if h == 0 and half == 0:
                    pe.wait_ge(top_kept, st.g * TT + (3 + st.at))
                pe.wait_ge(reduced, ring + 1)
                last = pe.matmul(bank[:, 0:k1 - k0], query_aug[st.slot][0:ROWS, h * P:(h + 1) * P], key_aug[st.p][0:ROWS, k0:k1],
                                 start=True, stop=not diagonal)
                if diagonal:
                    last = pe.matmul(bank[:, k1 - k0 - P:k1 - k0], m.ident_bf, m.causal, start=False, stop=True)
                last.then_inc(scored, 1)

            def masked_score(st, j):
                u = back_at[st.at] + j
                bank = back_bank[u % 2]
                if j == 0:
                    pe.wait_ge(mask_kept, st.n + 1)
                pe.wait_ge(probs_ready, st.g * BK + (u + 1))
                f = int(st.two and j >= 4)
                extra = j == st.i or (j == st.i - 1 and st.i >= 2)
                last = pe.matmul(bank[:, :], key_aug[st.p][0:KROWS, j * P:(j + 1) * P], query_aug[st.slot][0:KROWS, f * N:(f + 1) * N],
                                 start=True, stop=not extra)
                if j == st.i:
                    last = pe.matmul(bank[:, :], m.causal, m.ident4, start=False, stop=True)
                elif extra:
                    pe.wait_ge(diag_ready, st.g * (SEQ_TILES - 2) + (drops_at[st.at] + 1))
                    last = pe.matmul(bank[:, :], m.own_chunk, chunk_diag[st.slot], start=False, stop=True)
                last.then_inc(masked_scored, 1)

            def weigh(st, j):
                u = back_at[st.at] + j
                if j == 0:
                    pe.wait_ge(ot_ready, st.n + 1)
                    if st.at == 0:
                        pe.wait_ge(v_in[st.p], st.q * 16 + 16)
                pe.wait_ge(probs_ready, st.g * BK + (u + 3))
                for h in range(GQ):
                    last = pe.matmul(sums[st.k % 2][32 * h:32 * h + 32, :], v_staged[st.p][:, j * 32:(j + 1) * 32],
                                     probs[u % 4][:, h * P:(h + 1) * P], start=j == 0, stop=j == st.i, tile_position=(0, 32 * h))
                last.then_inc(summed, 1)

            def close(t, u):
                steps, g, place = closing(t, u)
                ring = ring_of_close(g, place)
                pe.wait_ge(ot_ready, steps[-1].n + 3)
                pe.wait_ge(reduced, ring + 1)
                bank = score_bank[closed_bank(g, place)]
                for n, st in enumerate(steps):
                    last = pe.transpose(bank[:, n * P:(n + 1) * P], ot[st.slot], m.ident)
                last.then_inc(scored, 1)

            def body(t, u):
                for stage, st, n in schedule(t, u):
                    if stage == "turn_q":
                        turn_q(st)
                    elif stage == "turn_k":
                        turn_k(st.g, st.p, st.q, n, False)
                    elif stage == "turn_mask":
                        turn_mask(st)
                    elif stage == "score":
                        score(st, n)
                    elif stage == "masked":
                        masked_score(st, n)
                    elif stage == "weigh":
                        weigh(st, n)
                    elif stage == "close":
                        close(t, u)

            turn_k(0, 0, 0, 0, True)
            turn_k(0, 0, 0, 1, False)
            for k in range(2):
                turn_q(Step(0, k))
            over_units(pe, body)

        @block.scalar
        def _(act):
            act.sem_inc(probs_ready, 2)
            act.sem_inc(ot_ready, 2)

            def keep_k(g, p, half):
                act.wait_ge(top_turned, g * TT + (half + 1))
                act.activation(key_aug[p][0:ROWS, half * 512:(half + 1) * 512], turn_bf[0:ROWS, 0:N], ACT.Copy).then_inc(top_kept, 1)

            def keep_q(st):
                act.wait_ge(top_turned, st.g * TT + (3 + st.at))
                if st.two:
                    act.activation(query_aug[st.slot][0:ROWS, N:2 * N], turn_bf[0:ROWS, 0:N], ACT.Copy)
                act.activation(query_aug[st.slot][0:ROWS, 0:N], turn_bf[0:ROWS, 0:N], ACT.Copy).then_inc(top_kept, 1)

            def keep_mask(st):
                act.wait_ge(mask_turned, st.n + 1)
                n = (1 + st.two) * N
                act.activation(query_aug[st.slot][ROWS:KROWS, 0:n], turn_bf[ROWS:KROWS, 0:n], ACT.Copy).then_inc(mask_kept, 1)

            def exponent(st, j):
                u = back_at[st.at] + j
                act.wait_ge(masked_scored, st.g * BK + (u + 1))
                act.wait_ge(summed, st.g * BK + (u + 1))
                act.activation(probs[u % 4], back_bank[u % 2][:, :], ACT.Exp, scale=float(HD) ** -0.5).then_inc(probs_ready, 1)

            def keep_sums(st):
                act.wait_ge(summed, st.g * BK + (back_at[st.at + 1] + 4))
                act.activation(ot[st.slot], sums[st.k % 2], ACT.Copy).then_inc(ot_ready, 1)

            def body(t, u):
                for stage, st, n in schedule(t, u):
                    if stage == "turn_q":
                        keep_q(st)
                    elif stage == "turn_k":
                        keep_k(st.g, st.p, n)
                    elif stage == "turn_mask":
                        keep_mask(st)
                    elif stage == "masked":
                        exponent(st, n)
                    elif stage == "sums":
                        keep_sums(st)

            for half in range(2):
                keep_k(0, 0, half)
            for k in range(2):
                keep_q(Step(0, k))
            over_units(act, body)

        @block.vector
        def _(dve):
            dve.sem_inc(reduced, 3)
            dve.wait_ge(w_blank, 1)

            def finish(t, u):
                steps, g, place = closing(t, u)
                n, inv = len(steps), inverse[place]
                dve.wait_ge(scored, ring_of_close(g, place) + 1)
                x = score_bank[closed_bank(g, place)][:, 0:n * P].rearrange("p (h c) -> p h c", h=n * GQ)
                dve_seq.mark(dve.reciprocal(inv[:, 0:n * GQ].unsqueeze(2), x[:, :, HD:HD + 1]))
                if place == 0:
                    dve.wait_ge(stored[steps[0].p], steps[0].q * 16 + 16)
                dve_seq.wait(dve)
                for n, st in enumerate(steps):
                    at = st.i * GQ * HD
                    last = dve.tensor_tensor(out=o_staged[st.p][:, at:at + GQ * HD].rearrange("p (h d) -> p h d", h=GQ),
                                             in0=x[:, n * GQ:(n + 1) * GQ, 0:HD],
                                             in1=inv[:, n * GQ:(n + 1) * GQ].unsqueeze(2).to_broadcast([P, GQ, HD]), op=ALU.mult)
                last.then_inc(reduced, 1)

            def choose(front):
                p, p4 = front.k % 2, front.k % 4
                i = front.i
                n = (i + 1) * CPT
                cm, lf, tp = cmax[p], left[p], top[p4]
                if not (isinstance(front.n, int) and front.n < 4):
                    dve.wait_ge(minus_ready, front.n - 3)
                chunks = lambda x, h: x[:, h * 64:h * 64 + n]

                def reduce(h):
                    for half in range(halves[i]):
                        number = h * halves[i] + half
                        k0, k1 = half * 512, min((i + 1) * P, (half + 1) * 512)
                        dve.wait_ge(scored, ring_of_score(front, number) + 1)
                        dve.tensor_reduce(out=cm[:, h * 64 + k0 // CHUNK:h * 64 + k1 // CHUNK],
                                          in_=score_bank[bank_of_score(front, number)][:, 0:k1 - k0].rearrange("p (c d) -> p c d", d=CHUNK),
                                          axis=AXX, op=ALU.max).then_inc(reduced, 1)

                def best(h):
                    dve.wait_ge(reduced, ring_of_score(front, (h + 1) * halves[i]) + 3)
                    dve.sem_inc(m.turnstile, 1)
                    dve_seq.mark(dve.max(out=tp[:, h * TOPK:(h + 1) * TOPK], in_=chunks(cm, h)))

                def drop(h):
                    dve_seq.mark(dve.match_replace(out=chunks(lf, h), in_to_replace=tp[:, h * TOPK:(h + 1) * TOPK],
                                                   in_values=chunks(cm, h), imm_value=TAKEN))
                for h in range(GQ):
                    reduce(h)
                    if h >= 1:
                        best(h - 1)
                best(GQ - 1)
                dve_seq.wait(dve)
                dve.sem_inc(top_ready, 1)
                if i < 2:
                    dve.sem_inc(mask_ready, 1)
                    return
                for h in range(GQ):
                    drop(h)
                dve_seq.wait(dve)
                w = W[i].rearrange("p (h f r) -> p h f r", h=GQ, f=2)
                lh = lf.rearrange("p (h c) -> p h c", h=GQ)
                near = lh[:, :, (i - 1) * CPT:i * CPT]
                wide = lambda c: c.unsqueeze(1).to_broadcast([P, GQ, CPT])
                own3 = own[p4].rearrange("p (h c) -> p h c", h=GQ)
                dve_seq.mark(dve.scalar_tensor_tensor(out=own3, in0=near, scalar=1e38, in1=wide(m.chunk_own),
                                                      op0=ALU.is_lt, op1=ALU.mult))
                f, c = ((i - 1) - 1) // 3, ((i - 1) - 1) % 3 * CPT
                if i >= 3:
                    a = min(i - 2, 3) * CPT
                    dve.tensor_scalar(out=w[:, :, 0, 0:a], in0=lh[:, :, CPT:CPT + a], scalar1=1e38, scalar2=NEG,
                                      op0=ALU.is_lt, op1=ALU.mult)
                if i >= 6:
                    a = (i - 5) * CPT
                    dve.tensor_scalar(out=w[:, :, 1, 0:a], in0=lh[:, :, 4 * CPT:4 * CPT + a], scalar1=1e38, scalar2=NEG,
                                      op0=ALU.is_lt, op1=ALU.mult)
                dve_seq.wait(dve)
                if not (isinstance(front.n, int) and front.n < 4):
                    dve.wait_ge(minus_ready, front.n - 2)
                dve.tensor_reduce(out=own_dropped[p4].unsqueeze(2), in_=own3, axis=AXX, op=ALU.add).then_inc(own_ready, 1)
                dve.scalar_tensor_tensor(out=w[:, :, f, c:c + CPT], in0=near, scalar=1e38, in1=wide(m.chunk_before),
                                         op0=ALU.is_lt, op1=ALU.mult).then_inc(mask_ready, 1)

            def body(t, u):
                front = stages(t, u)[0]
                for st in front[:1]:
                    choose(st)
                if closing(t, u)[0]:
                    finish(t, u)
                for st in front[1:]:
                    choose(st)

            over_units(dve, body, dve_seq, PAIR * GQ + 2 * CLOSES + 2 * (SEQ_TILES - 2) * (GQ + 1))

        @block.gpsimd
        def _(pool):
            for i in range(SEQ_TILES):
                pool.memset(W[i], 0.0)
            pool.memset(one_row, 1.0)
            pool.memset(neg_one, -1.0).then_inc(w_blank, 1)
            pool.sem_inc(summed, 4)
            for p in range(2):
                pool.sem_inc(stored[p], 16)
            pool.wait_ge(w_blank, 1)

            def mask_parts(st):
                p, p4 = st.k % 2, st.k % 4
                pool.wait_ge(top_ready, st.n + 1)
                w = W[st.i].rearrange("p (h f r) -> p h f r", h=GQ, f=2)
                tp = top[p4].rearrange("p (h c) -> p h c", h=GQ)
                c = 3 * CPT
                both = lambda x: x.unsqueeze(2).unsqueeze(3).to_broadcast([P, GQ, 2, 1])
                slot = lambda n: w[:, :, :, c + n:c + n + 1]
                one = lambda n: w[:, :, 0, c + n:c + n + 1]
                mi, re = minus[p].unsqueeze(2), minus_rest[p].unsqueeze(2)
                minus1 = neg_one.unsqueeze(2)
                pool_seq.mark(pool.tensor_tensor(out=mi, in0=tp[:, :, 0:1], in1=minus1, op=ALU.mult))
                pool_seq.mark(pool.tensor_tensor(out=slot(0), in0=both(tp[:, :, 0]), in1=both(neg_one), op=ALU.mult))
                pool_seq.wait(pool)
                pool_seq.mark(pool.tensor_tensor(out=re, in0=mi, in1=one(0), op=ALU.subtract))
                pool_seq.wait(pool)
                pool_seq.mark(pool.tensor_tensor(out=slot(1), in0=both(minus_rest[p]), in1=both(one_row), op=ALU.mult))
                pool_seq.wait(pool)
                pool.tensor_tensor(out=slot(2), in0=both(minus_rest[p]), in1=w[:, :, :, c + 1:c + 2], op=ALU.subtract).then_inc(minus_ready, 1)
                if st.i >= 2:
                    pool.wait_ge(own_ready, st.g * (SEQ_TILES - 2) + (drops_at[st.at] + 1))
                    pool.sem_inc(m.turnstile, 1)
                    for h in range(GQ):
                        last = pool.tensor_scalar(out=chunk_diag[st.slot][:, h * P:(h + 1) * P], in0=m.ident_bf,
                                                  scalar1=own_dropped[p4][:, h:h + 1], scalar2=NEG, op0=ALU.mult, op1=ALU.mult)
                    last.then_inc(diag_ready, 1)

            def body(t, u):
                for st in stages(t, u)[0]:
                    mask_parts(st)

            over_units(pool, body, pool_seq, PAIR * 4)


def load_last_weights(sp, m, dram):
    kq = "p (c d) -> p c d"
    sp.dma_start(m.f32(WO_AT, DC * D).rearrange(kq, c=DC), dram["wo"].rearrange("(c p) d -> p c d", p=P)).then_inc(m.last_in, 16)
    sp.dma_start(m.f32(LA_AT, D), dram["lora_A"].rearrange("h r d -> (h r) d")).then_inc(m.last_in, 16)
    sp.dma_start(m.f32(WR_AT, D)[0:LORA_H, :], dram["Wr"]).then_inc(m.last_in, 16)
    sp.dma_start(m.f32(BR_AT, LORA_H)[0:1, :], dram["br"].rearrange("(a h) -> a h", a=1)).then_inc(m.last_in, 16)
    for oc in range(DC):
        sp.dma_start(m.f32(LB_AT + oc * P, P).rearrange("p (h r) -> p h r", h=LORA_H),
                     dram["lora_B"][:, oc * P:(oc + 1) * P, :].rearrange("h o r -> o h r")).then_inc(m.last_in, 16)


LAST_LOADS = 4 + DC
WO_AT = 38400
LA_AT, WR_AT, LB_AT, BR_AT = WO_AT + DC * D, WO_AT + (DC + 1) * D, WO_AT + (DC + 2) * D, WO_AT + (DC + 3) * D
WOT_AT = BR_AT + 16
LOW_N = LORA_H * LORA_R + LORA_H
LOWW_AT = WOT_AT + DC * D
LBT_AT = LOWW_AT + DC * LOW_N
LWORK = LBT_AT + D


def output(nc, m, s, dram):
    woT = m.f32(WOT_AT, DC * D)
    low_w = m.f32(LOWW_AT, DC * LOW_N).rearrange("p (c n) -> p c n", c=DC)
    take = m.taker(LWORK, ARENA)
    o_tile, oT = [take(D) for _ in range(2)], [take(D) for _ in range(2)]
    o_all = m.f32(O_AT, GROUPS * SEQ_TILES * GQ * HD).rearrange("p (b k t c) -> p b k t c", b=BATCH, k=KV, t=SEQ_TILES)
    w_turned, w_placed = s("e_w_turned"), s("e_w_placed")
    gathered, turned, oT_ready, y_ready = [s(f"e_gathered{b}") for b in range(2)], s("e_turned"), s("e_oT"), s("e_y")
    stats_ready, branch_rstd_ready, added = s("e_stats"), s("e_branch_rstd"), s("e_added")
    dve_seq, pool_seq = Count(s("e_dve_seq")), Count(s("e_pool_seq"))
    n_weights = DC + 3

    with nc.Block() as block:
        @block.sync
        def _(sp):
            with sp.Fori(0, SEQ_TILES) as i:
                for b in range(2):
                    sp.wait_ge(turned, i * 2 + b + 1)
                    sp.dma_start(o_tile[b].rearrange("p (k c) -> p k c", k=KV),
                                 o_all[:, b, :, ds(i, 1), :].squeeze(2)).then_inc(gathered[b], 16)

        @block.tensor
        def _(pe):
            def turn(i, b):
                pe.wait_ge(gathered[b], i * 16 + 16)
                for dc in range(DC):
                    last = pe.transpose(m.banks[b][:, dc * P:(dc + 1) * P], o_tile[b][:, dc * P:(dc + 1) * P], m.ident)
                last.then_inc(turned, 1)

            def feed(k, b):
                pe.wait_ge(oT_ready, k + 1)
                pe.wait_ge(added, k + 1)
                for dc in range(DC):
                    last = pe.matmul(m.banks[2 + b][:, :], oT[b][:, dc * P:(dc + 1) * P], woT[:, dc * D:(dc + 1) * D],
                                     start=dc == 0, stop=dc == DC - 1)
                last.then_inc(y_ready, 1)

            pe.wait_ge(m.last_in, 16 * LAST_LOADS)
            for c in range(n_weights):
                bank = m.banks[4 + c % 4]
                if c >= 4:
                    pe.wait_ge(w_placed, c - 3)
                for dc in range(DC):
                    if c < DC:
                        last = pe.transpose(bank[:, dc * P:(dc + 1) * P], m.f32(WO_AT + c * D + dc * P, P), m.ident)
                    elif c == DC:
                        last = pe.transpose(bank[:, dc * P:(dc + 1) * P], m.f32(LA_AT + dc * P, P), m.ident)
                    elif c == DC + 1:
                        last = pe.transpose(bank[:, dc * LORA_H:(dc + 1) * LORA_H], m.f32(WR_AT + dc * P, P)[0:LORA_H, :],
                                            m.ident[0:LORA_H, 0:LORA_H])
                    else:
                        last = pe.transpose(bank[:, dc * P:(dc + 1) * P], m.f32(LB_AT + dc * P, P), m.ident)
                last.then_inc(w_turned, 1)
            for b in range(2):
                turn(0, b)
            pe.wait_ge(w_placed, DC)
            with pe.Fori(0, SEQ_TILES - 1) as i:
                for b in range(2):
                    feed(i * 2 + b, b)
                for b in range(2):
                    turn(i + 1, b)
            for b in range(2):
                feed(TILES - 2 + b, b)

        @block.scalar
        def _(act):
            act.sem_inc(turned, 2)
            for c in range(n_weights):
                act.wait_ge(w_turned, c + 1)
                bank = m.banks[4 + c % 4]
                if c < DC:
                    out = woT.rearrange("p (c n) -> p c n", c=DC)[:, :, c * P:(c + 1) * P]
                    last = act.activation(out, bank.rearrange("p (c n) -> p c n", c=DC), ACT.Copy)
                elif c == DC:
                    last = act.activation(low_w[:, :, 0:P], bank.rearrange("p (c n) -> p c n", c=DC), ACT.Copy)
                elif c == DC + 1:
                    last = act.activation(low_w[:, :, P:LOW_N], bank[:, 0:DC * LORA_H].rearrange("p (c n) -> p c n", c=DC), ACT.Copy)
                else:
                    last = act.activation(m.f32(LBT_AT, D), bank[:, :], ACT.Copy)
                last.then_inc(w_placed, 1)
            with act.Fori(0, SEQ_TILES) as i:
                for b in range(2):
                    act.wait_ge(turned, i * 2 + b + 3)
                    act.activation(oT[b], m.banks[b][:, :], ACT.Copy).then_inc(oT_ready, 1)

        @block.vector
        def _(dve):
            dve.sem_inc(added, 2)
            with dve.Fori(0, SEQ_TILES) as i:
                dve_seq.enter(i, 2 * (1 + BRANCH_ADD_STEPS))
                for b in range(2):
                    dve.wait_ge(y_ready, i * 2 + b + 1)
                    branch_stats(dve, m, dve_seq, b, m.banks[2 + b][:, :]).then_inc(stats_ready, 1)
                for b in range(2):
                    dve.wait_ge(branch_rstd_ready, i * 2 + b + 1)
                    branch_add(dve, m, dve_seq, b, m.banks[2 + b][:, :], i + b * SEQ_TILES).then_inc(added, 1)
            dve_seq.leave(SEQ_TILES)

        @block.gpsimd
        def _(pool):
            with pool.Fori(0, SEQ_TILES) as i:
                pool_seq.enter(i, 2)
                for b in range(2):
                    pool.wait_ge(stats_ready, i * 2 + b + 1)
                    branch_rstd(pool, m, pool_seq, b).then_inc(branch_rstd_ready, 1)
            pool_seq.leave(SEQ_TILES)


def routed(nc, m, s, dram):
    low_w = m.f32(LOWW_AT, DC * LOW_N)
    take = m.taker(LWORK, ARENA)
    xn, xT = [take(D) for _ in range(2)], [take(D) for _ in range(2)]
    ls, lsT = [take(P) for _ in range(2)], [take(P) for _ in range(2)]
    peak, total, share = [take(1) for _ in range(2)], [take(1) for _ in range(2)], [take(1) for _ in range(2)]
    e, score = [take(LORA_H) for _ in range(2)], [take(LORA_H) for _ in range(2)]
    ones = take(P)[0:1, :]
    rstd_ready, xn_ready, turned, xT_ready = s("f_rstd"), s("f_xn"), s("f_turned"), s("f_xT")
    low_ready, peak_ready, e_ready, ls_ready = s("f_low"), s("f_peak"), s("f_e"), s("f_ls")
    ls_turned, lsT_ready, y_ready = s("f_ls_turned"), s("f_lsT"), s("f_y")
    stats_ready, branch_rstd_ready, added = s("f_stats"), s("f_branch_rstd"), s("f_added")
    stored = s("f_stored")
    dve_seq, pool_seq = Count(s("f_dve_seq")), Count(s("f_pool_seq"))
    LR = LORA_H * LORA_R
    branch_scale = float(LORA_H * 2)

    def over_pairs(eng, body, seq=None, per=0):
        with eng.Fori(0, TILES // 2 - 1) as u:
            if seq:
                seq.enter(u, per)
            body(u, False)
        if seq:
            seq.leave(TILES // 2 - 1)
        body(TILES // 2 - 1, True)

    with nc.Block() as block:
        @block.sync
        def _(sp):
            with sp.Fori(0, TILES) as k:
                sp.wait_ge(added, k + 3)
                sp.dma_start(dram["out"][ds(k * P, P), :], m.x(k)).then_inc(stored, 16)
            sp.wait_ge(stored, 16 * TILES)

        @block.tensor
        def _(pe):
            def turn(k, p):
                pe.wait_ge(xn_ready, k + 1)
                for dc in range(DC):
                    last = pe.transpose(m.banks[p][:, dc * P:(dc + 1) * P], xn[p][:, dc * P:(dc + 1) * P], m.ident)
                last.then_inc(turned, 1)

            def body(u, last_pair):
                for p in range(2):
                    pe.wait_ge(xT_ready, u * 2 + (p + 1))
                    pe.wait_ge(ls_ready, u * 2 + (p + 1))
                    for dc in range(DC):
                        pe.matmul(m.banks[2 + p][:, 0:LOW_N], xT[p][:, dc * P:(dc + 1) * P], low_w[:, dc * LOW_N:(dc + 1) * LOW_N],
                                  start=dc == 0, stop=False)
                    pe.matmul(m.banks[2 + p][:, LR:LOW_N], ones, m.f32(BR_AT, LORA_H)[0:1, :], start=False, stop=True).then_inc(low_ready, 1)
                if not last_pair:
                    for p in range(2):
                        turn(u * 2 + (2 + p), p)
                for p in range(2):
                    pe.wait_ge(ls_ready, u * 2 + (p + 3))
                    pe.transpose(m.banks[4 + p][:, 0:LR], ls[p], m.ident).then_inc(ls_turned, 1)
                for p in range(2):
                    pe.wait_ge(lsT_ready, u * 2 + (p + 1))
                    pe.wait_ge(added, u * 2 + (p + 1))
                    pe.matmul(m.banks[6 + p][:, :], lsT[p], m.f32(LBT_AT, D), start=True, stop=True).then_inc(y_ready, 1)

            for p in range(2):
                turn(p, p)
            over_pairs(pe, body)

        @block.scalar
        def _(act):
            def normed(k, p):
                act.activation(xn[p], m.x(k), ACT.Identity, bias=m.shift[:, ds(k, 1)],
                               scale=m.rstd[:, ds(k, 1)]).then_inc(xn_ready, 1)

            def keep(k, p):
                act.wait_ge(turned, k + 1)
                act.activation(xT[p], m.banks[p][:, :], ACT.Copy).then_inc(xT_ready, 1)

            def body(u, last_pair):
                if not last_pair:
                    for p in range(2):
                        normed(u * 2 + (2 + p), p)
                for p in range(2):
                    act.wait_ge(peak_ready, u * 2 + (p + 1))
                    act.activation(e[p], m.banks[2 + p][:, LR:LOW_N], ACT.Exp, bias=peak[p], accum_out=total[p]).then_inc(e_ready, 1)
                if not last_pair:
                    for p in range(2):
                        keep(u * 2 + (2 + p), p)
                for p in range(2):
                    act.wait_ge(ls_turned, u * 2 + (p + 1))
                    act.activation(lsT[p], m.banks[4 + p][:, 0:LR], ACT.Copy).then_inc(lsT_ready, 1)

            act.wait_ge(rstd_ready, 1)
            for p in range(2):
                normed(p, p)
            for p in range(2):
                keep(p, p)
            over_pairs(act, body)

        @block.vector
        def _(dve):
            dve.sem_inc(added, 2)
            dve.sem_inc(ls_ready, 2)

            def body(u, _):
                for p in range(2):
                    dve.wait_ge(low_ready, u * 2 + (p + 1))
                    dve.tensor_reduce(out=peak[p], in_=m.banks[2 + p][:, LR:LOW_N], axis=AXX, op=ALU.max, negate=True).then_inc(peak_ready, 1)
                for p in range(2):
                    dve.wait_ge(e_ready, u * 2 + (p + 1))
                    dve_seq.mark(dve.reciprocal(share[p], total[p]))
                    dve_seq.wait(dve)
                    dve_seq.mark(dve.tensor_scalar(out=score[p], in0=e[p], scalar1=share[p], scalar2=branch_scale, op0=ALU.mult, op1=ALU.mult))
                    dve_seq.wait(dve)
                    dve.tensor_tensor(out=ls[p].rearrange("p (h r) -> p h r", h=LORA_H), in0=m.banks[2 + p][:, 0:LR].rearrange("p (h r) -> p h r", h=LORA_H),
                                      in1=score[p].unsqueeze(2).to_broadcast([P, LORA_H, LORA_R]), op=ALU.mult).then_inc(ls_ready, 1)
                for p in range(2):
                    dve.wait_ge(y_ready, u * 2 + (p + 1))
                    branch_stats(dve, m, dve_seq, p, m.banks[6 + p][:, :]).then_inc(stats_ready, 1)
                for p in range(2):
                    dve.wait_ge(branch_rstd_ready, u * 2 + (p + 1))
                    branch_add(dve, m, dve_seq, p, m.banks[6 + p][:, :], u * 2 + p, last=True).then_inc(added, 1)
            over_pairs(dve, body, dve_seq, 2 * 5)

        @block.gpsimd
        def _(pool):
            pool.memset(ones, 1.0)
            rstd_all(pool, m, pool_seq).then_inc(rstd_ready, 1)
            pool_seq.settle()

            def body(u, _):
                for p in range(2):
                    pool.wait_ge(stats_ready, u * 2 + (p + 1))
                    branch_rstd(pool, m, pool_seq, p).then_inc(branch_rstd_ready, 1)
            over_pairs(pool, body, pool_seq, 2)




def program(nc, dram):
    with ExitStack() as ctx:
        m = Mem(nc, ctx)
        for stage in (setup_and_sparse, weights, gated, project, attention, output, routed):
            stage(nc, m, m.sem, dram)


def shape_constants():
    c = np.zeros((P, 6 * P), np.float32)
    row, col = np.arange(P)[:, None], np.arange(P)[None, :]
    c[:, 0:P] = row == col
    c[:, P:2 * P] = np.where(col > row, np.float32(NEG), np.float32(0))
    c[:, 2 * P:3 * P] = (row // CHUNK == col // CHUNK) & (col <= row)
    inv = np.float32(1.0) / np.float32(10000.0) ** (np.arange(0, HD, 2, dtype=np.float32) / np.float32(HD))
    freq = np.arange(SEQ, dtype=np.float32)[:, None] * inv[None, :].astype(np.float32)
    emb = np.concatenate([freq, freq], 1).astype(np.float32)
    sin = np.sin(emb).astype(np.float32)
    sin[:, :HD // 2] *= -1
    lay = lambda t: t.reshape(SEQ_TILES, P, HD).transpose(1, 0, 2).reshape(P, SEQ_TILES * HD)
    c[:, 3 * P:4 * P] = lay(np.cos(emb).astype(np.float32))
    c[:, 4 * P:5 * P] = lay(sin)
    ch = np.arange(CPT)[None, :]
    c[:, 5 * P:5 * P + CPT] = np.where(ch < row // CHUNK, np.float32(NEG), np.float32(0))
    c[:, 5 * P + CPT:5 * P + 2 * CPT] = ch == row // CHUNK
    k = np.zeros((MASK_ROWS, SEQ), np.float32)
    for j in range(1, SEQ_TILES - 1):
        for ch in range(CPT):
            k[(j - 1) % 3 * CPT + ch, j * P + ch * CHUNK:j * P + (ch + 1) * CHUNK] = 1
    k[3 * CPT:, :] = 1
    return c, k


_NAMES = {"x": "L0_attn_x", "w1": "L0_attn_w1", "w2": "L0_attn_w2", "b2": "L0_attn_b2", "mask": "L0_attn_sparse_mask",
          "gate_q": "L0_ffn_gate_q", "gate_scale": "L0_ffn_gate_scale", "gate_A": "L0_ffn_gate_A", "gate_B": "L0_ffn_gate_B",
          "up_q": "L0_ffn_up_q", "up_scale": "L0_ffn_up_scale", "up_A": "L0_ffn_up_A", "up_B": "L0_ffn_up_B",
          "down_q": "L0_ffn_down_q", "down_scale": "L0_ffn_down_scale", "down_A": "L0_ffn_down_A", "down_B": "L0_ffn_down_B",
          "wq": "L1_attn_wq", "wk": "L1_attn_wk", "wv": "L1_attn_wv", "wo": "L1_attn_wo",
          "lora_A": "L1_ffn_A", "lora_B": "L1_ffn_B", "Wr": "L1_ffn_Wr", "br": "L1_ffn_br"}


def kernel(**inputs):
    import concourse.bacc as bacc
    from concourse.bass_utils import run_bass_kernel_spmd

    nc = bacc.Bacc("TRN2", target_bir_lowering=False, num_devices=1)
    consts, key_rows = shape_constants()
    arrays = {"consts": consts, "key_rows": key_rows}
    arrays |= {short: np.ascontiguousarray(inputs[name]) for short, name in _NAMES.items()}
    arrays["x"] = arrays["x"].reshape(BATCH * SEQ, D)
    dram = {n: nc.dram_tensor(f"in_{n}", a.shape, mybir.dt.from_np(a.dtype), kind="ExternalInput").ap()
            for n, a in arrays.items()}
    dram["rows"] = nc.dram_tensor("qk_rows", (GROUPS, P, ST_W), BF16).ap()
    dram["out"] = nc.dram_tensor("out", (BATCH * SEQ, D), F32, kind="ExternalOutput").ap()
    program(nc, dram)
    r = run_bass_kernel_spmd(nc, [{f"in_{n}": a for n, a in arrays.items()}], core_ids=[0])
    return r.results[0]["out"].reshape(BATCH, SEQ, D)
```
